# Optimizing a Trainium2 kernel written in Bass

```python
import numpy as np
import jax
import jax.numpy as jnp

def _softmax(x, axis=-1):
    return jax.nn.softmax(x, axis=axis)

def _gelu(x):
    return jax.nn.gelu(x, approximate=True)

def _silu(x):
    return jax.nn.silu(x)

def _sigmoid(x):
    return jax.nn.sigmoid(x)

def _layernorm(x, axis=-1, eps=1e-05):
    m = jnp.mean(x, axis=axis, keepdims=True)
    v = jnp.var(x, axis=axis, keepdims=True)
    return (x - m) / jnp.sqrt(v + eps)

def _scatter_add(tgt, idx, src, axis=0):
    return tgt.at[idx].add(src)

def _segment_sum(src, seg, n):
    return jax.ops.segment_sum(src, seg, n)
kernel_name = 'mk_adaln_d2_jaxref_r8_00ffd0'

def setup_inputs(seed: int=0):
    np.random.seed(seed)
    _w = jnp.asarray

    def _L0_attn_setup():
        import jax, jax.numpy as jnp
        import numpy as np
        BASE_THETA = 0.5
        K_DOP = 0.2
        K_NOR = 0.15
        K_SERO = 0.1
        DIM = 128
        key = jax.random.key(seed)
        ks = jax.random.split(key, 9)
        scale = 1.0 / np.sqrt(DIM)
        x = jax.random.normal(ks[0], (2, 256, DIM), dtype=jnp.float32)
        Wq = jax.random.normal(ks[1], (DIM, DIM), dtype=jnp.float32) * scale
        bq = jnp.zeros((DIM,), dtype=jnp.float32)
        Wk = jax.random.normal(ks[2], (DIM, DIM), dtype=jnp.float32) * scale
        bk = jnp.zeros((DIM,), dtype=jnp.float32)
        Wv = jax.random.normal(ks[3], (DIM, DIM), dtype=jnp.float32) * scale
        bv = jnp.zeros((DIM,), dtype=jnp.float32)
        Wo = jax.random.normal(ks[4], (DIM, DIM), dtype=jnp.float32) * scale
        bo = jnp.zeros((DIM,), dtype=jnp.float32)
        return {'x': x, 'Wq': Wq, 'bq': bq, 'Wk': Wk, 'bk': bk, 'Wv': Wv, 'bv': bv, 'Wo': Wo, 'bo': bo}
    _L0_attn_in = _L0_attn_setup()

    def _L0_ffn_setup():
        import jax, jax.numpy as jnp
        import numpy as np
        DIM = 128
        DEPTH = 6
        HEADS = 16
        DIM_HEAD = 64
        WINDOW = 32
        INNER = HEADS * DIM_HEAD
        DIM_INNER = int(DIM * 4 * 2 / 3)
        QK_SCALE = 8.0

        def shift_tokens(t):
            a, s = jnp.split(t, 2, -1)
            s = jnp.pad(s, ((0, 0), (1, 0), (0, 0)))[:, :-1]
            return jnp.concatenate([a, s], -1)

        def l2norm(t):
            return t / jnp.maximum(jnp.linalg.norm(t, axis=-1, keepdims=True), 1e-12)

        def rotate_half(x):
            x1, x2 = jnp.split(x, 2, -1)
            return jnp.concatenate([-x2, x1], -1)

        def rotary_tables(n):
            half = jnp.arange(0, DIM_HEAD, 2, dtype=jnp.float32)
            inv_freq = 1.0 / 10000.0 ** (half / DIM_HEAD)
            t = jnp.arange(n, dtype=jnp.float32)
            freqs = t[:, None] * inv_freq[None, :]
            freqs = jnp.concatenate([freqs, freqs], -1)
            base_scale = (half + 0.4 * DIM_HEAD) / (1.4 * DIM_HEAD)
            power = (t - n // 2) / (WINDOW // 2)
            scale = base_scale[None, :] ** power[:, None]
            scale = jnp.concatenate([scale, scale], -1)
            return (freqs, scale)

        def local_attention(q, k, v):
            b, h, n, d = q.shape
            w = WINDOW
            nw = n // w
            bq = q.reshape(b, h, nw, w, d)
            bk = k.reshape(b, h, nw, w, d)
            bv = v.reshape(b, h, nw, w, d)

            def look(t):
                p = jnp.pad(t, ((0, 0), (0, 0), (1, 0), (0, 0), (0, 0)))
                return jnp.concatenate([p[:, :, :nw], p[:, :, 1:]], axis=3)
            bk2, bv2 = (look(bk), look(bv))
            seq = jnp.arange(n).reshape(nw, w)
            seq_p = jnp.pad(seq, ((1, 0), (0, 0)), constant_values=-1)
            jt = jnp.concatenate([seq_p[:nw], seq_p[1:]], axis=1)
            it = seq[:, :, None]
            jb = jt[:, None, :]
            mask = (it < jb) | (it > jb + w) | (jb == -1)
            sim = jnp.einsum('bhwie,bhwje->bhwij', bq, bk2) * QK_SCALE
            sim = jnp.where(mask, -jnp.finfo(sim.dtype).max, sim)
            attn = jax.nn.softmax(sim, -1)
            out = jnp.einsum('bhwij,bhwje->bhwie', attn, bv2)
            return out.reshape(b, h, n, d)

        def attn_layer(x, Wqkv, qs, ksc, Wo):
            b, n, _ = x.shape
            qkv = x @ Wqkv
            q, k, v = jnp.split(qkv, 3, -1)
            sh = lambda t: t.reshape(b, n, HEADS, DIM_HEAD).transpose(0, 2, 1, 3)
            q, k, v = (sh(q), sh(k), sh(v))
            q = l2norm(q) * qs
            k = l2norm(k) * ksc
            freqs, scale = rotary_tables(n)
            cos, sin = (jnp.cos(freqs), jnp.sin(freqs))
            q = q * cos * scale + rotate_half(q) * sin * scale
            inv = 1.0 / scale
            k = k * cos * inv + rotate_half(k) * sin * inv
            out = local_attention(q, k, v)
            out = out.transpose(0, 2, 1, 3).reshape(b, n, INNER)
            return out @ Wo

        def ffn_layer(x, g, bln, W1, b1, W2, b2):
            mu = x.mean(-1, keepdims=True)
            var = ((x - mu) ** 2).mean(-1, keepdims=True)
            xn = (x - mu) / jnp.sqrt(var + 1e-05) * g + bln
            hg = xn @ W1 + b1
            a, gate = jnp.split(hg, 2, -1)
            return a * jax.nn.gelu(gate, approximate=False) @ W2 + b2
        key = jax.random.key(seed)
        ks = jax.random.split(key, 8)
        B, N = (2, 256)
        init = lambda k, shape: jax.random.normal(k, shape, jnp.float32) * 0.02
        return {'x': jax.random.normal(ks[0], (B, N, DIM), jnp.float32), 'Wqkv': init(ks[1], (DEPTH, DIM, 3 * INNER)), 'q_scale': jnp.ones((DEPTH, DIM_HEAD), jnp.float32), 'k_scale': jnp.ones((DEPTH, DIM_HEAD), jnp.float32), 'Wo': init(ks[2], (DEPTH, INNER, DIM)), 'ln_g': jnp.ones((DEPTH, DIM), jnp.float32), 'ln_b': jnp.zeros((DEPTH, DIM), jnp.float32), 'W1': init(ks[3], (DEPTH, DIM, 2 * DIM_INNER)), 'b1': jnp.zeros((DEPTH, 2 * DIM_INNER), jnp.float32), 'W2': init(ks[4], (DEPTH, DIM_INNER, DIM)), 'b2': jnp.zeros((DEPTH, DIM), jnp.float32)}
    _L0_ffn_in = _L0_ffn_setup()
    _L0_c = _w((lambda *s: np.random.randn(*s).astype(np.float32) * 0.05)(4, 128))
    _L0_wmod = _w((lambda *s: np.random.randn(*s).astype(np.float32) * 0.05)(128, 6 * 128) * 128 ** (-0.5))

    def _L1_attn_setup():
        import jax, jax.numpy as jnp
        import numpy as np
        NEG_BIG = -1e+38

        def _wkv_scan(w, u, k, v, aa0, bb0, pp0):
            kT = jnp.moveaxis(k, 1, 0)
            vT = jnp.moveaxis(v, 1, 0)

            def step(carry, kv):
                aa, bb, pp = carry
                kt, vt = kv
                ww = u + kt
                p = jnp.maximum(pp, ww)
                e1 = jnp.exp(pp - p)
                e2 = jnp.exp(ww - p)
                y = (e1 * aa + e2 * vt) / (e1 * bb + e2)
                ww2 = pp + w
                p2 = jnp.maximum(ww2, kt)
                e1 = jnp.exp(ww2 - p2)
                e2 = jnp.exp(kt - p2)
                return ((e1 * aa + e2 * vt, e1 * bb + e2, p2), y)
            (aa, bb, pp), yT = jax.lax.scan(step, (aa0, bb0, pp0), (kT, vT))
            return (jnp.moveaxis(yT, 0, 1), aa, bb, pp)

        def _reference_tuple_inner(x, W_rvk, W_out, time_decay, time_first):
            B, T, C = x.shape
            rvk = jnp.einsum('btc,dc->btd', x, W_rvk)
            r, v, k = jnp.split(rvk, 3, axis=-1)
            w = -jnp.exp(time_decay)
            u = time_first
            aa0 = jnp.zeros((B, C), dtype=x.dtype)
            bb0 = jnp.zeros((B, C), dtype=x.dtype)
            pp0 = jnp.full((B, C), NEG_BIG, dtype=x.dtype)
            wkv, aa, bb, pp = _wkv_scan(w, u, k, v, aa0, bb0, pp0)
            rwkv = jax.nn.sigmoid(r) * wkv
            out = jnp.einsum('btc,dc->btd', rwkv, W_out)
            h = aa
            c = jnp.stack([bb, pp], axis=-1).reshape(B, 2 * C)
            return (out, h, c)
        key = jax.random.key(seed)
        k1, k2, k3 = jax.random.split(key, 3)
        B, T, C = (32, 128, 128)
        x = jax.random.normal(k1, (B, T, C), dtype=jnp.float32)
        W_rvk = jax.random.normal(k2, (3 * C, C), dtype=jnp.float32) * (1.0 / np.sqrt(C))
        W_out = jax.random.normal(k3, (C, C), dtype=jnp.float32) * (1.0 / np.sqrt(C))
        time_decay = jnp.ones((C,), dtype=jnp.float32)
        time_first = jnp.ones((C,), dtype=jnp.float32)
        return {'x': x, 'W_rvk': W_rvk, 'W_out': W_out, 'time_decay': time_decay, 'time_first': time_first}
    _L1_attn_in = _L1_attn_setup()

    def _L1_ffn_setup():
        import jax, jax.numpy as jnp
        import numpy as np
        HIDDEN = 128
        NUM_EXPERTS = 8
        BATCH, SEQ = (4, 512)
        key = jax.random.key(seed)
        ks = jax.random.split(key, 6)
        s = 1.0 / np.sqrt(HIDDEN)
        tokens = jax.random.normal(ks[0], (BATCH, SEQ, HIDDEN), dtype=jnp.float32)
        gate_w = jax.random.uniform(ks[1], (NUM_EXPERTS, HIDDEN), jnp.float32, -s, s)
        expert_w = jax.random.uniform(ks[2], (NUM_EXPERTS, HIDDEN, HIDDEN), jnp.float32, -s, s)
        expert_b = jax.random.uniform(ks[3], (NUM_EXPERTS, HIDDEN), jnp.float32, -s, s)
        combine_w = jax.random.uniform(ks[4], (HIDDEN, HIDDEN), jnp.float32, -s, s)
        return {'tokens': tokens, 'gate_w': gate_w, 'expert_w': expert_w, 'expert_b': expert_b, 'combine_w': combine_w}
    _L1_ffn_in = _L1_ffn_setup()
    _L1_c = _w((lambda *s: np.random.randn(*s).astype(np.float32) * 0.05)(4, 128))
    _L1_wmod = _w((lambda *s: np.random.randn(*s).astype(np.float32) * 0.05)(128, 6 * 128) * 128 ** (-0.5))
    _d = {'L0_attn_x': _L0_attn_in['x'], 'L0_attn_Wq': _L0_attn_in['Wq'], 'L0_attn_bq': _L0_attn_in['bq'], 'L0_attn_Wk': _L0_attn_in['Wk'], 'L0_attn_bk': _L0_attn_in['bk'], 'L0_attn_Wv': _L0_attn_in['Wv'], 'L0_attn_bv': _L0_attn_in['bv'], 'L0_attn_Wo': _L0_attn_in['Wo'], 'L0_attn_bo': _L0_attn_in['bo'], 'L0_ffn_Wqkv': _L0_ffn_in['Wqkv'], 'L0_ffn_q_scale': _L0_ffn_in['q_scale'], 'L0_ffn_k_scale': _L0_ffn_in['k_scale'], 'L0_ffn_Wo': _L0_ffn_in['Wo'], 'L0_ffn_ln_g': _L0_ffn_in['ln_g'], 'L0_ffn_ln_b': _L0_ffn_in['ln_b'], 'L0_ffn_W1': _L0_ffn_in['W1'], 'L0_ffn_b1': _L0_ffn_in['b1'], 'L0_ffn_W2': _L0_ffn_in['W2'], 'L0_ffn_b2': _L0_ffn_in['b2'], 'L0_c': _L0_c, 'L0_wmod': _L0_wmod, 'L1_attn_W_rvk': _L1_attn_in['W_rvk'], 'L1_attn_W_out': _L1_attn_in['W_out'], 'L1_attn_time_decay': _L1_attn_in['time_decay'], 'L1_attn_time_first': _L1_attn_in['time_first'], 'L1_ffn_gate_w': _L1_ffn_in['gate_w'], 'L1_ffn_expert_w': _L1_ffn_in['expert_w'], 'L1_ffn_expert_b': _L1_ffn_in['expert_b'], 'L1_ffn_combine_w': _L1_ffn_in['combine_w'], 'L1_c': _L1_c, 'L1_wmod': _L1_wmod}
    _x0 = _d['L0_attn_x']
    _d['L0_attn_x'] = jax.random.normal(jax.random.fold_in(jax.random.key(seed), 1), (4, 1024, 128), dtype=_x0.dtype)
    del _x0
    return _d

def reference(L0_attn_x, L0_attn_Wq, L0_attn_bq, L0_attn_Wk, L0_attn_bk, L0_attn_Wv, L0_attn_bv, L0_attn_Wo, L0_attn_bo, L0_ffn_Wqkv, L0_ffn_q_scale, L0_ffn_k_scale, L0_ffn_Wo, L0_ffn_ln_g, L0_ffn_ln_b, L0_ffn_W1, L0_ffn_b1, L0_ffn_W2, L0_ffn_b2, L0_c, L0_wmod, L1_attn_W_rvk, L1_attn_W_out, L1_attn_time_decay, L1_attn_time_first, L1_ffn_gate_w, L1_ffn_expert_w, L1_ffn_expert_b, L1_ffn_combine_w, L1_c, L1_wmod):

    def _L0_attn_ref(x, Wq, bq, Wk, bk, Wv, bv, Wo, bo):
        import jax, jax.numpy as jnp
        import numpy as np
        BASE_THETA = 0.5
        K_DOP = 0.2
        K_NOR = 0.15
        K_SERO = 0.1
        DIM = 128
        q = jnp.einsum('bsd,ed->bse', x, Wq) + bq
        k = jnp.einsum('bsd,ed->bse', x, Wk) + bk
        v = jnp.einsum('bsd,ed->bse', x, Wv) + bv
        qk = jnp.einsum('bsd,btd->bst', q, k)
        theta = BASE_THETA + K_DOP * jax.nn.sigmoid(qk) + K_NOR * jnp.tanh(qk) + K_SERO * jax.nn.relu(qk)
        attn = jax.nn.softmax(theta, axis=-1)
        out = jnp.einsum('bst,btd->bsd', attn, v)
        return jnp.einsum('bsd,ed->bse', out, Wo) + bo

    def _L0_ffn_ref(x, Wqkv, q_scale, k_scale, Wo, ln_g, ln_b, W1, b1, W2, b2):
        import jax, jax.numpy as jnp
        import numpy as np
        DIM = 128
        DEPTH = 6
        HEADS = 16
        DIM_HEAD = 64
        WINDOW = 32
        INNER = HEADS * DIM_HEAD
        DIM_INNER = int(DIM * 4 * 2 / 3)
        QK_SCALE = 8.0

        def shift_tokens(t):
            a, s = jnp.split(t, 2, -1)
            s = jnp.pad(s, ((0, 0), (1, 0), (0, 0)))[:, :-1]
            return jnp.concatenate([a, s], -1)

        def l2norm(t):
            return t / jnp.maximum(jnp.linalg.norm(t, axis=-1, keepdims=True), 1e-12)

        def rotate_half(x):
            x1, x2 = jnp.split(x, 2, -1)
            return jnp.concatenate([-x2, x1], -1)

        def rotary_tables(n):
            half = jnp.arange(0, DIM_HEAD, 2, dtype=jnp.float32)
            inv_freq = 1.0 / 10000.0 ** (half / DIM_HEAD)
            t = jnp.arange(n, dtype=jnp.float32)
            freqs = t[:, None] * inv_freq[None, :]
            freqs = jnp.concatenate([freqs, freqs], -1)
            base_scale = (half + 0.4 * DIM_HEAD) / (1.4 * DIM_HEAD)
            power = (t - n // 2) / (WINDOW // 2)
            scale = base_scale[None, :] ** power[:, None]
            scale = jnp.concatenate([scale, scale], -1)
            return (freqs, scale)

        def local_attention(q, k, v):
            b, h, n, d = q.shape
            w = WINDOW
            nw = n // w
            bq = q.reshape(b, h, nw, w, d)
            bk = k.reshape(b, h, nw, w, d)
            bv = v.reshape(b, h, nw, w, d)

            def look(t):
                p = jnp.pad(t, ((0, 0), (0, 0), (1, 0), (0, 0), (0, 0)))
                return jnp.concatenate([p[:, :, :nw], p[:, :, 1:]], axis=3)
            bk2, bv2 = (look(bk), look(bv))
            seq = jnp.arange(n).reshape(nw, w)
            seq_p = jnp.pad(seq, ((1, 0), (0, 0)), constant_values=-1)
            jt = jnp.concatenate([seq_p[:nw], seq_p[1:]], axis=1)
            it = seq[:, :, None]
            jb = jt[:, None, :]
            mask = (it < jb) | (it > jb + w) | (jb == -1)
            sim = jnp.einsum('bhwie,bhwje->bhwij', bq, bk2) * QK_SCALE
            sim = jnp.where(mask, -jnp.finfo(sim.dtype).max, sim)
            attn = jax.nn.softmax(sim, -1)
            out = jnp.einsum('bhwij,bhwje->bhwie', attn, bv2)
            return out.reshape(b, h, n, d)

        def attn_layer(x, Wqkv, qs, ksc, Wo):
            b, n, _ = x.shape
            qkv = x @ Wqkv
            q, k, v = jnp.split(qkv, 3, -1)
            sh = lambda t: t.reshape(b, n, HEADS, DIM_HEAD).transpose(0, 2, 1, 3)
            q, k, v = (sh(q), sh(k), sh(v))
            q = l2norm(q) * qs
            k = l2norm(k) * ksc
            freqs, scale = rotary_tables(n)
            cos, sin = (jnp.cos(freqs), jnp.sin(freqs))
            q = q * cos * scale + rotate_half(q) * sin * scale
            inv = 1.0 / scale
            k = k * cos * inv + rotate_half(k) * sin * inv
            out = local_attention(q, k, v)
            out = out.transpose(0, 2, 1, 3).reshape(b, n, INNER)
            return out @ Wo

        def ffn_layer(x, g, bln, W1, b1, W2, b2):
            mu = x.mean(-1, keepdims=True)
            var = ((x - mu) ** 2).mean(-1, keepdims=True)
            xn = (x - mu) / jnp.sqrt(var + 1e-05) * g + bln
            hg = xn @ W1 + b1
            a, gate = jnp.split(hg, 2, -1)
            return a * jax.nn.gelu(gate, approximate=False) @ W2 + b2
        for i in range(DEPTH):
            x = attn_layer(shift_tokens(x), Wqkv[i], q_scale[i], k_scale[i], Wo[i]) + x
            x = ffn_layer(shift_tokens(x), ln_g[i], ln_b[i], W1[i], b1[i], W2[i], b2[i]) + x
        return x

    def _L1_attn_ref(x, W_rvk, W_out, time_decay, time_first):
        import jax, jax.numpy as jnp
        import numpy as np
        NEG_BIG = -1e+38

        def _wkv_scan(w, u, k, v, aa0, bb0, pp0):
            kT = jnp.moveaxis(k, 1, 0)
            vT = jnp.moveaxis(v, 1, 0)

            def step(carry, kv):
                aa, bb, pp = carry
                kt, vt = kv
                ww = u + kt
                p = jnp.maximum(pp, ww)
                e1 = jnp.exp(pp - p)
                e2 = jnp.exp(ww - p)
                y = (e1 * aa + e2 * vt) / (e1 * bb + e2)
                ww2 = pp + w
                p2 = jnp.maximum(ww2, kt)
                e1 = jnp.exp(ww2 - p2)
                e2 = jnp.exp(kt - p2)
                return ((e1 * aa + e2 * vt, e1 * bb + e2, p2), y)
            (aa, bb, pp), yT = jax.lax.scan(step, (aa0, bb0, pp0), (kT, vT))
            return (jnp.moveaxis(yT, 0, 1), aa, bb, pp)

        def _reference_tuple_inner(x, W_rvk, W_out, time_decay, time_first):
            B, T, C = x.shape
            rvk = jnp.einsum('btc,dc->btd', x, W_rvk)
            r, v, k = jnp.split(rvk, 3, axis=-1)
            w = -jnp.exp(time_decay)
            u = time_first
            aa0 = jnp.zeros((B, C), dtype=x.dtype)
            bb0 = jnp.zeros((B, C), dtype=x.dtype)
            pp0 = jnp.full((B, C), NEG_BIG, dtype=x.dtype)
            wkv, aa, bb, pp = _wkv_scan(w, u, k, v, aa0, bb0, pp0)
            rwkv = jax.nn.sigmoid(r) * wkv
            out = jnp.einsum('btc,dc->btd', rwkv, W_out)
            h = aa
            c = jnp.stack([bb, pp], axis=-1).reshape(B, 2 * C)
            return (out, h, c)
        return _reference_tuple_inner(x, W_rvk, W_out, time_decay, time_first)[0]

    def _L1_ffn_ref(tokens, gate_w, expert_w, expert_b, combine_w):
        import jax, jax.numpy as jnp
        import numpy as np
        HIDDEN = 128
        NUM_EXPERTS = 8
        BATCH, SEQ = (4, 512)
        B, S, H = tokens.shape
        logits = jnp.einsum('bsh,eh->bse', tokens, gate_w)
        probs = jax.nn.softmax(logits, axis=-1)
        top2_w, top2_idx = jax.lax.top_k(probs, 2)
        flat = tokens.reshape(B * S, H)
        flat_idx = top2_idx.reshape(B * S, 2)
        flat_w = top2_w.reshape(B * S, 2)
        expert_out = jax.nn.silu(jnp.einsum('nh,edh->ned', flat, expert_w) + expert_b[None, :, :])
        gathered = jnp.take_along_axis(expert_out, flat_idx[:, :, None], axis=1)
        mixed = jnp.sum(gathered * flat_w[:, :, None], axis=1)
        out = jnp.einsum('bsh,dh->bsd', mixed.reshape(B, S, H), combine_w)
        return out
    x = L0_attn_x
    mod = (_silu(L0_c) @ L0_wmod).reshape(L0_c.shape[0], 6, 1, -1)
    sa, ca, ga, sb, cb, gb = (mod[:, 0], mod[:, 1], mod[:, 2], mod[:, 3], mod[:, 4], mod[:, 5])
    ga = (2 * (ga >= 0) - 1) * jnp.maximum(jnp.abs(ga), 0.25)
    gb = (2 * (gb >= 0) - 1) * jnp.maximum(jnp.abs(gb), 0.25)
    h = _layernorm(x, axis=-1) * (1 + ca) + sa
    x = x + ga * _L0_attn_ref(h, L0_attn_Wq, L0_attn_bq, L0_attn_Wk, L0_attn_bk, L0_attn_Wv, L0_attn_bv, L0_attn_Wo, L0_attn_bo)
    h = _layernorm(x, axis=-1) * (1 + cb) + sb
    x = x + gb * _L0_ffn_ref(h, L0_ffn_Wqkv, L0_ffn_q_scale, L0_ffn_k_scale, L0_ffn_Wo, L0_ffn_ln_g, L0_ffn_ln_b, L0_ffn_W1, L0_ffn_b1, L0_ffn_W2, L0_ffn_b2)
    mod = (_silu(L1_c) @ L1_wmod).reshape(L1_c.shape[0], 6, 1, -1)
    sa, ca, ga, sb, cb, gb = (mod[:, 0], mod[:, 1], mod[:, 2], mod[:, 3], mod[:, 4], mod[:, 5])
    ga = (2 * (ga >= 0) - 1) * jnp.maximum(jnp.abs(ga), 0.25)
    gb = (2 * (gb >= 0) - 1) * jnp.maximum(jnp.abs(gb), 0.25)
    h = _layernorm(x, axis=-1) * (1 + ca) + sa
    x = x + ga * _L1_attn_ref(h, L1_attn_W_rvk, L1_attn_W_out, L1_attn_time_decay, L1_attn_time_first)
    h = _layernorm(x, axis=-1) * (1 + cb) + sb
    x = x + gb * _L1_ffn_ref(h, L1_ffn_gate_w, L1_ffn_expert_w, L1_ffn_expert_b, L1_ffn_combine_w)
    return x

_drawn_inputs = setup_inputs


def setup_inputs(seed=0):
    import zlib

    import numpy as np

    out = dict(_drawn_inputs(seed))
    spreads = {'L0_attn_bq': (0.0, 0.8),
     'L0_attn_bk': (0.0, 2.0),
     'L0_attn_bv': (0.0, 0.347),
     'L0_attn_bo': (0.0, 0.322),
     'L0_ffn_q_scale': (1.0, 0.6),
     'L0_ffn_k_scale': (1.0, 0.6),
     'L0_ffn_ln_g': (1.0, 0.6),
     'L0_ffn_ln_b': (0.0, 0.8),
     'L0_ffn_b1': (0.0, 0.8),
     'L0_ffn_b2': (0.0, 0.618),
     'L1_attn_time_decay': (1.0, 0.6),
     'L1_attn_time_first': (1.0, 0.6)}
    factors = {'L0_ffn_W1': 7.333,
     'L0_ffn_W2': 7.194,
     'L1_ffn_gate_w': 4.606,
     'L1_ffn_expert_w': 4.035,
     'L1_ffn_expert_b': 40.66,
     'L1_ffn_combine_w': 3.817,
     'L1_attn_W_rvk': 4.534,
     'L1_attn_W_out': 4.527}
    for name, (base, spread) in spreads.items():
        noise = np.random.default_rng([zlib.crc32(name.encode()), seed]).standard_normal(out[name].shape)
        drawn = base * np.exp(spread * noise) if base else spread * noise
        out[name] = jnp.asarray(drawn.astype(out[name].dtype))
    for name, factor in factors.items():
        out[name] = (out[name] * factor).astype(out[name].dtype)
    return out
```

```python
from contextlib import ExitStack

import numpy as np

import concourse.bass as bass
from concourse import mybir

ALU = mybir.AluOpType
ACT = mybir.ActivationFunctionType
AX = mybir.AxisListType
F32 = mybir.dt.float32
BF16 = mybir.dt.bfloat16
I32 = mybir.dt.int32
U32 = mybir.dt.uint32

P = 128
BATCH = 4
SEQ = 1024
TOK = BATCH * SEQ
CH = 512
NCH = TOK // CH
DEPTH = 6
HEADS = 16
DH = 64
HALF = DH // 2
WIN = 32
G = 4
BLK = 128
NBLK = TOK // BLK
BPS = SEQ // BLK
SROW = SEQ + 2
INNER = 341
NFB = -(-INNER // P)
FB = [min(P, INNER - P * j) for j in range(NFB)]
EXPERTS = 8
MASKED = -1.0e30
RSQRT_MAGIC = float(0x5F3759DF)
EPS = 1e-5
START = 1


def semaphores(nc, ctx, prefix):
    made = []

    def sem(name):
        made.append(ctx.enter_context(nc.semaphore(prefix + name)))
        return made[-1]

    return made, sem


class Links:

    def __init__(self, eng, sem):
        self.eng, self.sem, self.base, self.n = eng, sem, 0, 0

    def start(self, base):
        self.base, self.n = base, 0

    def __call__(self, ins):
        ins.then_inc(self.sem, 1)
        self.n += 1
        self.eng.wait_ge(self.sem, START + self.base + self.n)


def bcast_mid(ap, n):
    return ap.unsqueeze(1).broadcast_to([ap.shape[0], n, ap.shape[1]])


def bcast_last(ap, n):
    return ap.unsqueeze(len(ap.shape)).broadcast_to(list(ap.shape) + [n])


def newton_rsqrt(nc, link, y, v, a, last=None):
    link(nc.vector.tensor_scalar(y.bitcast(I32), v.bitcast(I32), -0.5, RSQRT_MAGIC, ALU.mult, ALU.add))
    for i in range(3):
        link(nc.vector.scalar_tensor_tensor(a, y, -0.5, v, ALU.mult, ALU.mult))
        link(nc.vector.tensor_tensor(a, a, y, ALU.mult))
        ins = nc.vector.scalar_tensor_tensor(y, a, 1.5, y, ALU.add, ALU.mult)
        if i < 2 or last is None:
            link(ins)
        else:
            ins.then_inc(last, 1)


def own_wait(eng, passed):
    eng.sem_inc(passed, 1)


LN_LINKS = 1 + 10


class LayerNorm:

    def __init__(self, nc, ctx, name, const, phase_sem):
        self.nc, self.const = nc, const
        sb = lambda s, sh: ctx.enter_context(nc.sbuf_tensor(f"{name}_{s}", sh, F32))
        sem = lambda s: phase_sem("ln_" + s)
        self.xc = sb("centred", [P, CH])
        self.sq = sb("squares", [P, CH])
        self.xn = sb("normed", [P, CH])
        self.var = sb("var", [P, 4])
        self.rstd = sb("rstd", [P, 4])
        self.tmp = sb("tmp", [P, 4])
        self.mean_ready, self.centred_ready, self.squares_ready = sem("mean_ready"), sem("centred_ready"), sem("squares_ready")
        self.var_ready, self.rstd_ready, self.spread_ready = sem("var_ready"), sem("rstd_ready"), sem("spread_ready")
        self.normed_ready, self.out_ready, self.links = sem("normed_ready"), sem("out_ready"), sem("links")

    def tensor(self, pe, n, src, wide, small):
        nc, c = self.nc, self.const
        pe.wait_ge(self.normed_ready, START + n)
        nc.tensor.matmul(wide, c["mean_w"][:, :], src, start=True, stop=True).then_inc(self.mean_ready, 1)
        pe.wait_ge(self.squares_ready, START + n + 1)
        for k in range(4):
            ins = nc.tensor.matmul(small[:, k:k + 1], self.sq[:, k * P:(k + 1) * P], c["mean_w"][:, 0:1], start=True, stop=True)
        ins.then_inc(self.var_ready, 1)
        pe.wait_ge(self.rstd_ready, START + n + 1)
        for k in range(4):
            ins = nc.tensor.matmul(wide[:, k * P:(k + 1) * P], self.rstd[:, k:k + 1].broadcast_to([P, P]),
                                   c["ident"][:, :], start=True, stop=True)
        ins.then_inc(self.spread_ready, 1)

    def vector(self, dve, n, src, wide, small, gain):
        nc = self.nc
        link = Links(dve, self.links)
        link.start(n * LN_LINKS)
        dve.wait_ge(self.mean_ready, START + n + 1)
        nc.vector.tensor_tensor(self.xc[:, :], src, wide, ALU.subtract).then_inc(self.centred_ready, 1)
        dve.wait_ge(self.var_ready, START + n + 1)
        link(nc.vector.tensor_scalar(self.var[:, :], small, EPS, None, ALU.add))
        newton_rsqrt(nc, link, self.rstd[:, :], self.var[:, :], self.tmp[:, :])
        dve.sem_inc(self.rstd_ready, 1)
        dve.wait_ge(self.spread_ready, START + n + 1)
        dve.wait_ge(self.out_ready, START + n)
        nc.vector.scalar_tensor_tensor(self.xn[:, :], self.xc[:, :], gain, wide, ALU.mult, ALU.mult).then_inc(self.normed_ready, 1)

    def scalar_squares(self, act, n):
        act.wait_ge(self.centred_ready, START + n + 1)
        self.nc.scalar.activation(self.sq[:, :], self.xc[:, :], ACT.Square).then_inc(self.squares_ready, 1)

    def scalar_out(self, act, n, dsts, bias):
        act.wait_ge(self.normed_ready, START + n + 1)
        for ps, dst in dsts:
            ins = self.nc.scalar.activation(dst, self.xn[ps, :], ACT.Identity, bias=bias[ps, :])
        ins.then_inc(self.out_ready, 1)


def prepare(nc, const, t):
    ctx = ExitStack()
    with ctx:
        sb = lambda s, sh, dt=F32: ctx.enter_context(nc.sbuf_tensor("prep_" + s, sh, dt))
        sems, sem = semaphores(nc, ctx, "prep_")
        cT = sb("cT", [P, 2, BATCH])
        silu = sb("silu", [P, 2, BATCH])
        wmod = sb("wmod", [P, 2, 6 * P])
        neg = sb("neg", [P, 2, 2, BATCH])
        sign = sb("sign", [P, 2, 2, BATCH])
        ps = ctx.enter_context(nc.psum_tensor("prep_ps", [P, 512], F32))
        loaded, silu_ready, mod_ready, links, ones = sem("loaded"), sem("silu_ready"), sem("mod_ready"), sem("links"), sem("ones")
        block = ctx.enter_context(nc.Block())
        mod = const["mod"]

        @block.sync
        def _(sp):
            for s in sems:
                sp.sem_inc(s, START)
            sp.dma_start(const["x"][:, :], t["xT"]).then_inc(loaded, 16)
            sp.dma_start(cT[:, :, :], t["cT"]).then_inc(loaded, 16)
            sp.dma_start(wmod[:, :, :], t["wmod"]).then_inc(loaded, 16)
            sp.dma_start(const["ident"][:, :], t["ident"]).then_inc(loaded, 16)
            sp.wait_ge(loaded, START + 64)

        @block.gpsimd
        def _(pool):
            nc.gpsimd.memset(const["mean_w"][:, :], 1.0 / P).then_inc(ones, 1)

        @block.scalar
        def _(act):
            act.wait_ge(loaded, START + 64)
            nc.scalar.activation(silu[:, :, :], cT[:, :, :], ACT.Silu).then_inc(silu_ready, 1)

        @block.tensor
        def _(pe):
            pe.wait_ge(silu_ready, START + 1)
            for b in range(2):
                for j in range(6):
                    ins = nc.tensor.matmul(ps[:, (b * 6 + j) * BATCH:(b * 6 + j + 1) * BATCH], wmod[:, b, j * P:(j + 1) * P],
                                           silu[:, b, :], start=True, stop=True)
            ins.then_inc(mod_ready, 1)

        @block.vector
        def _(dve):
            link = Links(dve, links)
            dve.wait_ge(mod_ready, START + 1)
            psm = ps[:, 0:48].rearrange("p (b j n) -> p b j n", b=2, j=6)
            link(nc.vector.tensor_copy(mod[:, :], ps[:, 0:48]))
            m = mod[:, :].rearrange("p (b k j n) -> p b k j n", b=2, k=2, j=3)
            for b in range(2):
                link(nc.vector.tensor_scalar(m[:, b, :, 1, :], m[:, b, :, 1, :], 1.0, None, ALU.add))
                gate = m[:, b, :, 2, :]
                link(nc.vector.tensor_scalar(neg[:, b, :, :], gate, -1.0, None, ALU.mult))
                link(nc.vector.tensor_scalar(sign[:, b, :, :], gate, 0.0, 2.0, ALU.is_ge, ALU.mult))
                link(nc.vector.tensor_tensor(gate, gate, neg[:, b, :, :], ALU.max))
                link(nc.vector.tensor_scalar(gate, gate, 0.25, None, ALU.max))
                link(nc.vector.scalar_tensor_tensor(gate, sign[:, b, :, :], -1.0, gate, ALU.add, ALU.mult))


def modcol(const, block, which, b):
    at = (block * 6 + which) * BATCH + b
    return const["mod"][:, at:at + 1]


def theta_attention(nc, const, t):
    ctx = ExitStack()
    with ctx:
        sb = lambda s, sh, dt=F32: ctx.enter_context(nc.sbuf_tensor("att_" + s, sh, dt))
        pb = lambda s, sh: ctx.enter_context(nc.psum_tensor("att_ps_" + s, sh, F32))
        sems, sem = semaphores(nc, ctx, "att_")
        ln = LayerNorm(nc, ctx, "att_ln", const, sem)
        x = const["x"]
        w = sb("w", [P, 4, P])
        bias = sb("bias", [P, 4])
        out_bias = sb("out_bias", [P, 1])
        mods = sb("mods", [P, 3])
        gated_bias = sb("gated_bias", [P, 1])
        h = sb("h", [P, SEQ])
        q, k, v = sb("q", [P, SEQ]), sb("k", [P, SEQ]), sb("v", [P, SEQ])
        t1, t2, theta = sb("t1", [P, SEQ]), sb("t2", [P, SEQ]), sb("theta", [P, SEQ])
        probs, probsT = sb("probs", [P, SEQ]), sb("probsT", [P, SEQ])
        mx, shift, total, recip = sb("mx", [P, 1]), sb("shift", [P, 1]), sb("total", [P, 1]), sb("recip", [P, 1])
        spread, oT, upd = sb("spread", [P, P]), sb("oT", [P, P]), sb("upd", [P, P])
        ps_s = pb("scores", [P, SEQ])
        ps_t = pb("probsT", [P, SEQ])
        ps_ln, ps_small, ps_o, ps_y = pb("ln", [P, CH]), pb("small", [P, CH]), pb("o", [P, CH]), pb("y", [P, CH])
        loaded, bias_ps, bias_ready, mods_ready = sem("loaded"), sem("bias_ps"), sem("bias_ready"), sem("mods_ready")
        proj_ps, proj_ready, scores_ps, tanh_ready = sem("proj_ps"), sem("proj_ready"), sem("scores_ps"), sem("tanh_ready")
        theta_ready, probs_ready, probsT_ps = sem("theta_ready"), sem("probs_ready"), sem("probsT_ps")
        probsT_a, probsT_d = sem("probsT_act"), sem("probsT_dve")
        recip_ready, pv_ps, o_ready, y_ps, x_done = sem("recip_ready"), sem("pv_ps"), sem("o_ready"), sem("y_ps"), sem("x_done")
        links, setup_links = sem("links"), sem("setup_links")
        block = ctx.enter_context(nc.Block())
        NS = SEQ // P
        VL = 1 + 5 * NS

        @block.sync
        def _(sp):
            for s in sems:
                sp.sem_inc(s, START)
            sp.dma_start(w[:, :, :], t["att_w"]).then_inc(loaded, 16)
            sp.dma_start(bias[:, :], t["att_b"]).then_inc(loaded, 16)
            sp.wait_ge(loaded, START + 32)

        @block.tensor
        def _(pe):
            pe.wait_ge(loaded, START + 32)
            nc.tensor.matmul(ps_y[:, 0:1], w[:, 3, :], bias[:, 2:3], start=True, stop=True).then_inc(bias_ps, 1)
            pe.wait_ge(bias_ready, START + 1)
            with pe.Fori(0, BATCH) as b:
                for c in range(2):
                    ln.tensor(pe, b * 2 + c, x[:, bass.ds(b * SEQ + c * CH, CH)], ps_ln[:, :], ps_small[:, 0:4])
                pe.wait_ge(ln.out_ready, START + 2 * b + 2)
                for i, dst in ((0, ps_s), (1, ps_t)):
                    for c in range(2):
                        ins = nc.tensor.matmul(dst[:, c * CH:(c + 1) * CH], w[:, i, :], h[:, c * CH:(c + 1) * CH], start=True, stop=True)
                    ins.then_inc(proj_ps, 1)
                pe.wait_ge(proj_ready, START + 3 * b + 1)
                for j in range(NS):
                    ins = nc.tensor.matmul(ps_s[:, j * P:(j + 1) * P], h[:, j * P:(j + 1) * P], w[:, 2, :], start=True, stop=True)
                ins.then_inc(proj_ps, 1)
                pe.wait_ge(proj_ready, START + 3 * b + 3)
                for j in range(NS):
                    n = b * NS + j
                    for c in range(2):
                        ins = nc.tensor.matmul(ps_s[:, c * CH:(c + 1) * CH], q[:, j * P:(j + 1) * P], k[:, c * CH:(c + 1) * CH], start=True, stop=True)
                    ins.then_inc(scores_ps, 1)
                    pe.wait_ge(probs_ready, START + n + 1)
                    for c in range(8):
                        ins = nc.tensor.transpose(ps_t[:, c * P:(c + 1) * P], probs[:, c * P:(c + 1) * P], const["ident"][:, :])
                    ins.then_inc(probsT_ps, 1)
                    pe.wait_ge(recip_ready, START + n + 1)
                    nc.tensor.matmul(ps_o[:, P:2 * P], recip[:, 0:1].broadcast_to([P, P]), const["ident"][:, :], start=True, stop=True)
                    pe.wait_ge(probsT_a, START + n + 1)
                    pe.wait_ge(probsT_d, START + n + 1)
                    for c in range(8):
                        ins = nc.tensor.matmul(ps_o[:, 0:P], v[:, c * P:(c + 1) * P], probsT[:, c * P:(c + 1) * P], start=c == 0, stop=c == 7)
                    ins.then_inc(pv_ps, 1)
                    pe.wait_ge(o_ready, START + n + 1)
                    nc.tensor.matmul(ps_y[:, 0:P], w[:, 3, :], oT[:, :], start=True, stop=True).then_inc(y_ps, 1)
                pe.wait_ge(x_done, START + NS * b + NS)

        @block.scalar
        def _(act):
            act.wait_ge(loaded, START + 32)
            with act.Fori(0, BATCH) as b:
                act.wait_ge(mods_ready, START + b + 1)
                for c in range(2):
                    n = b * 2 + c
                    ln.scalar_squares(act, n)
                    ln.scalar_out(act, n, [(slice(0, P), h[:, c * CH:(c + 1) * CH])], mods[:, 0:1])
                act.wait_ge(proj_ps, START + 3 * b + 1)
                nc.scalar.activation(q[:, :], ps_s[:, :], ACT.Identity, bias=bias[:, 0:1]).then_inc(proj_ready, 1)
                act.wait_ge(proj_ps, START + 3 * b + 2)
                nc.scalar.activation(k[:, :], ps_t[:, :], ACT.Identity, bias=bias[:, 1:2]).then_inc(proj_ready, 1)
                act.wait_ge(proj_ps, START + 3 * b + 3)
                nc.scalar.activation(v[:, :], ps_s[:, :], ACT.Copy).then_inc(proj_ready, 1)
                for j in range(NS):
                    n = b * NS + j
                    act.wait_ge(scores_ps, START + n + 1)
                    for c in range(2):
                        cols = slice(c * CH, (c + 1) * CH)
                        nc.scalar.activation(t1[:, cols], ps_s[:, cols], ACT.Tanh, scale=0.5)
                        nc.scalar.activation(t2[:, cols], ps_s[:, cols], ACT.Tanh).then_inc(tanh_ready, 1)
                    act.wait_ge(theta_ready, START + n + 1)
                    nc.scalar.activation(probs[:, :], theta[:, :], ACT.Exp, bias=shift[:, :], scale=0.15, accum_out=total[:, :]).then_inc(probs_ready, 1)
                    act.wait_ge(probsT_ps, START + n + 1)
                    nc.scalar.activation(probsT[:, 0:CH], ps_t[:, 0:CH], ACT.Copy).then_inc(probsT_a, 1)

        @block.vector
        def _(dve):
            link = Links(dve, setup_links)
            dve.wait_ge(loaded, START + 32)
            dve.wait_ge(bias_ps, START + 1)
            link(nc.vector.tensor_tensor(out_bias[:, :], ps_y[:, 0:1], bias[:, 3:4], ALU.add))
            dve.sem_inc(bias_ready, 1)
            link = Links(dve, links)
            with dve.Fori(0, BATCH) as b:
                link.start(b * VL)
                for i in range(3):
                    ins = nc.vector.tensor_copy(mods[:, i:i + 1], const["mod"][:, bass.ds(b + i * BATCH, 1)])
                link(ins)
                dve.sem_inc(mods_ready, 1)
                nc.vector.tensor_tensor(gated_bias[:, :], mods[:, 2:3], out_bias[:, :], ALU.mult)
                for c in range(2):
                    ln.vector(dve, b * 2 + c, x[:, bass.ds(b * SEQ + c * CH, CH)], ps_ln[:, :], ps_small[:, 0:4], mods[:, 1:2])
                for j in range(NS):
                    n = b * NS + j
                    for c in range(2):
                        cols = slice(c * CH, (c + 1) * CH)
                        dve.wait_ge(tanh_ready, START + 2 * n + c + 1)
                        ins = nc.vector.scalar_tensor_tensor(theta[:, cols], ps_s[:, cols], 0.0, t1[:, cols], ALU.max, ALU.add)
                    link(ins)
                    link(nc.vector.scalar_tensor_tensor(theta[:, :], theta[:, :], 2.0 / 3.0, t2[:, :], ALU.mult, ALU.add))
                    link(nc.vector.tensor_reduce(mx[:, :], theta[:, :], AX.X, ALU.max))
                    nc.vector.tensor_scalar(shift[:, :], mx[:, :], -0.15, None, ALU.mult).then_inc(theta_ready, 1)
                    dve.wait_ge(probs_ready, START + n + 1)
                    nc.vector.reciprocal(recip[:, :], total[:, :]).then_inc(recip_ready, 1)
                    dve.wait_ge(probsT_ps, START + n + 1)
                    nc.vector.tensor_copy(probsT[:, CH:], ps_t[:, CH:]).then_inc(probsT_d, 1)
                    dve.wait_ge(pv_ps, START + n + 1)
                    link(nc.vector.tensor_copy(spread[:, :], ps_o[:, P:2 * P]))
                    nc.vector.tensor_tensor(oT[:, :], ps_o[:, 0:P], spread[:, :], ALU.mult).then_inc(o_ready, 1)
                    dve.wait_ge(y_ps, START + n + 1)
                    link(nc.vector.tensor_scalar(upd[:, :], ps_y[:, 0:P], mods[:, 2:3], gated_bias[:, 0:1], ALU.mult, ALU.add))
                    cols = bass.ds(b * SEQ + j * P, P)
                    nc.vector.tensor_tensor(x[:, cols], x[:, cols], upd[:, :], ALU.add).then_inc(x_done, 1)
                assert link.n == VL, link.n


def local_layers(nc, const, t):
    ctx = ExitStack()
    with ctx:
        sb = lambda s, sh, dt=F32: ctx.enter_context(nc.sbuf_tensor("loc_" + s, sh, dt))
        sems, sem = semaphores(nc, ctx, "loc_")
        ln = LayerNorm(nc, ctx, "loc_ln", const, sem)
        x, ident = const["x"], const["ident"]
        xa, xb = sb("xa", [P, BATCH, SROW]), sb("xb", [P, BATCH, SROW])
        xaf, xbf = xa[:, :, :].rearrange("p b s -> p (b s)"), xb[:, :, :].rearrange("p b s -> p (b s)")
        base_tab, tab = sb("base_tab", [P, 4, SEQ]), sb("tab", [P, 8, SEQ])
        ident16, mask = sb("ident16", [P, P], BF16), sb("mask", [P, BPS, 2 * WIN], BF16)
        head_sum = sb("head_sum", [P, G])
        wqk, wv, wo = sb("wqk", [P, 2, 2, G, P]), sb("wv", [P, HEADS * DH]), sb("wo", [P, 2, 4, P])
        scales = sb("scales", [P, 4])
        kept = sb("kept", [P, BPS])
        w1, w2, fpar = sb("w1", [P, 2 * INNER]), sb("w2", [P, NFB, P]), sb("fpar", [P, 3 + 2 * NFB])
        mods = sb("mods", [P, 3])
        hs = sb("hs", [P, BLK])
        sq = sb("sq", [P, 4, G, BLK])
        m = sb("m", [P, 8, G, BLK])
        mask32 = m[:, 0, :, :].rearrange("p g t -> p (g t)")
        act_out = m[:, 0:NFB, :, :].rearrange("p a g t -> p a (g t)")
        qr, ks = sb("qr", [P, 2, G, BLK]), sb("ks", [P, 2, G, BLK])
        kr = sb("kr", [P, 2, G, WIN + BLK])
        norm, rnorm, ntmp = sb("norm", [P, 2 * HEADS]), sb("rnorm", [P, 2 * HEADS]), sb("ntmp", [P, 2 * HEADS])
        rk_wide = sb("rk_wide", [P, HEADS * HALF])
        mx, ebias, total, recip = sb("mx", [P, HEADS]), sb("ebias", [P, HEADS]), sb("total", [P, HEADS]), sb("recip", [P, HEADS])
        probs, probsT = sb("probs", [P, HEADS, 2 * WIN]), sb("probsT", [P, HEADS, 2 * WIN])
        v, vprev = sb("v", [P, HEADS * DH]), sb("vprev", [P, HEADS * DH])
        o, oT = sb("o", [P, 4, G * DH]), sb("oT", [P, 2, 4, P])
        h, gelu = sb("h", [P, CH]), sb("gelu", [P, 2, CH])
        pa = ctx.enter_context(nc.psum_tensor("loc_pa", [P, 4, 512], F32))
        pw = ctx.enter_context(nc.psum_tensor("loc_pw", [P, 4, 512], F32))

        mask_ready = sem("mask_ready")
        consts, mem, tabs_ready = sem("consts"), sem("mem"), sem("tabs_ready")
        mods_ready, ln_in_done = sem("mods_ready"), sem("ln_in_done")
        aw, fw = sem("attn_weights"), sem("ffn_weights")
        hs_ready, qk_ps, sq_ready, rot, rope_add = sem("hs_ready"), sem("qk_ps"), sem("sq_ready"), sem("rot"), sem("rope_add")
        v_ps, v_ready, norm_ps, rnorm_ready, spread_ps = sem("v_ps"), sem("v_ready"), sem("norm_ps"), sem("rnorm_ready"), sem("spread_ps")
        kr_ready, sim_ps, ebias_ready, exp_ready = sem("kr_ready"), sem("sim_ps"), sem("ebias_ready"), sem("exp_ready")
        probsT_ready, pv_ps, o_ready, oT_ps, oT_ready = sem("probsT_ready"), sem("pv_ps"), sem("o_ready"), sem("oT_ps"), sem("oT_ready")
        wo_ps, xb_done, ktail, vprev_dma, vtail_dma = sem("wo_ps"), sem("xb_done"), sem("ktail"), sem("vprev_dma"), sem("vtail_dma")
        ff_ps, gelu_ready, hidden_ready, y_ps, xa_done = sem("ff_ps"), sem("gelu_ready"), sem("hidden_ready"), sem("y_ps"), sem("xa_done")
        links, flinks, passed = sem("links"), sem("flinks"), sem("passed")
        block = ctx.enter_context(nc.Block())

        BL = NBLK
        FL = NCH
        PRE = NCH
        VL = 1 + 10 + 1 + 2
        AW, FW = 16 * 4, 16 * 3

        def pipelined(eng, layer, step):
            first = layer * BL
            step(first, None, 0, None)
            with eng.Fori(1, BL) as i:
                step(first + i, first + i - 1, i, i - 1)
            step(None, first + BL - 1, None, BL - 1)

        def col(i):
            return i * BLK + (i // BPS) * (SROW - SEQ)

        @block.sync
        def _(sp):
            for s in sems:
                sp.sem_inc(s, START)
            for name, dst in (("tables", base_tab), ("mask", mask32), ("head_sum", head_sum)):
                sp.dma_start(dst if name == "mask" else dst[:], t[name]).then_inc(consts, 16)

            def attn_weights(layer):
                sp.dma_start(wqk[:, :, :, :, :], t["wqk"][bass.ds(layer, 1)].rearrange("l p a b g n -> (l p) a b g n")).then_inc(aw, 16)
                sp.dma_start(wv[:, :], t["wv"][bass.ds(layer, 1)].rearrange("l p n -> (l p) n")).then_inc(aw, 16)
                sp.dma_start(wo[:, :, :, :], t["wo"][bass.ds(layer, 1)].rearrange("l p a r n -> (l p) a r n")).then_inc(aw, 16)
                sp.dma_start(scales[:, :], t["scales"][bass.ds(layer, 1)].rearrange("l p n -> (l p) n")).then_inc(aw, 16)

            attn_weights(0)
            sp.wait_ge(mem, START + 6)
            with sp.Fori(0, DEPTH) as layer:
                sp.wait_ge(xa_done, START + FL * layer)
                sp.dma_start(w1[:, :], t["w1"][bass.ds(layer, 1)].rearrange("l p n -> (l p) n")).then_inc(fw, 16)
                sp.dma_start(w2[:, :, :], t["w2"][bass.ds(layer, 1)].rearrange("l p j n -> (l p) j n")).then_inc(fw, 16)
                sp.dma_start(fpar[:, :], t["fpar"][bass.ds(layer, 1)].rearrange("l p n -> (l p) n")).then_inc(fw, 16)

                def step(n, late, i, li):
                    if late is not None:
                        sp.wait_ge(pv_ps, START + late + 1)
                        sp.dma_start(vprev[0:WIN, :], v[P - WIN:P, :]).then_inc(vtail_dma, 16)
                    if n is not None:
                        sp.wait_ge(v_ready, START + 2 * n + 2)
                        sp.dma_start(vprev[WIN:P, :], v[0:P - WIN, :]).then_inc(vprev_dma, 16)

                pipelined(sp, layer, step)
                sp.wait_ge(wo_ps, START + BL * layer + BL)
                attn_weights(layer + 1)
            sp.wait_ge(aw, START + AW * (DEPTH + 1))
            sp.wait_ge(fw, START + FW * DEPTH)

        @block.gpsimd
        def _(pool):
            for k, (view, value) in enumerate(((kept[:, :], 1.0), (kept[:, BPS - 1:BPS], 0.0), (kr[:, :, :, 0:WIN], 0.0),
                                               (vprev[0:WIN, :], 0.0), (xa[DH:P, :, 0:1], 0.0), (xb[DH:P, :, 0:1], 0.0))):
                nc.gpsimd.memset(view, value).then_inc(mem, 1)
                pool.wait_ge(mem, START + k + 1)
            pool.wait_ge(ln.out_ready, START + PRE)
            with pool.Fori(0, DEPTH) as layer:
                pool.wait_ge(xa_done, START + FL * layer)

                def step(n, late, i, li):
                    if n is None:
                        return
                    pool.wait_ge(v_ps, START + 2 * n)
                    own_wait(pool, passed)
                    nc.gpsimd.tensor_copy(hs[:, :], xaf[:, bass.ds(col(i), BLK)]).then_inc(hs_ready, 1)
                    for s in range(2):
                        out, used = (qr, sim_ps) if s == 0 else (ks, kr_ready)
                        pool.wait_ge(used, START + (n if s == 0 else 2 * n))
                        pool.wait_ge(rot, START + 8 * n + 4 * s + 4)
                        a = m[:, 4 * s:4 * s + 4, :, :]
                        nc.gpsimd.tensor_tensor(out[:, 0, :, :], a[:, 0], a[:, 2], ALU.subtract).then_inc(rope_add, 1)
                        nc.gpsimd.tensor_tensor(out[:, 1, :, :], a[:, 1], a[:, 3], ALU.add).then_inc(rope_add, 1)
                    pool.wait_ge(sim_ps, START + n + 1)
                    keep = kept[:, bass.ds(i % BPS, 1)].broadcast_to([P, G * WIN]).rearrange("p (g j) -> p g j", g=G)
                    for s in range(2):
                        ins = nc.gpsimd.tensor_tensor(kr[:, s, :, 0:WIN], kr[:, s, :, BLK:BLK + WIN], keep, ALU.mult)
                    ins.then_inc(ktail, 1)

                pipelined(pool, layer, step)

        @block.tensor
        def _(pe):
            pe.wait_ge(consts, START + 48)
            pe.wait_ge(mask_ready, START + 2)
            pe.wait_ge(mem, START + 6)
            with pe.Fori(0, BATCH) as b:
                for c in range(2):
                    ln.tensor(pe, b * 2 + c, x[:, bass.ds(b * SEQ + c * CH, CH)], pa[:, 0, :], pa[:, 1, 0:4])
            pe.wait_ge(ln.out_ready, START + PRE)
            with pe.Fori(0, DEPTH) as layer:
                pe.wait_ge(aw, START + AW * layer + AW)
                pe.wait_ge(xa_done, START + FL * layer)

                def step(n, late, i, li):
                    if n is not None:
                        pe.wait_ge(ebias_ready, START + n)
                        pe.wait_ge(v_ready, START + 2 * n)
                        src = xaf[:, bass.ds(col(i), BLK)]
                        for s in range(4):
                            for g in range(G):
                                ins = nc.tensor.matmul(pa[:, s, g * BLK:(g + 1) * BLK], wqk[:, s // 2, s % 2, g, :], src, start=True, stop=True)
                            ins.then_inc(qk_ps, 1)
                    if late is not None:
                        pe.wait_ge(probsT_ready, START + late + 1)
                        pe.wait_ge(vprev_dma, START + 16 * late + 16)
                        pe.wait_ge(v_ready, START + 2 * late + 2)
                        own_wait(pe, passed)
                        for g in range(G):
                            for r in range(4):
                                for half, val in ((0, vprev), (1, v)):
                                    for w in range(4):
                                        hd = 4 * g + r
                                        ws = slice(WIN * w, WIN * w + WIN)
                                        ins = nc.tensor.matmul(pw[WIN * r:WIN * r + WIN, w, 256 + g * DH:256 + (g + 1) * DH],
                                                               probsT[ws, r * G + g, half * WIN:(half + 1) * WIN], val[ws, hd * DH:(hd + 1) * DH],
                                                               start=half == 0, stop=half == 1, tile_position=(WIN * w, WIN * r))
                        ins.then_inc(pv_ps, 1)
                    if n is not None:
                        pe.wait_ge(sq_ready, START + 4 * n + 4)
                        pe.wait_ge(rot, START + 8 * n + 2)
                        for s in range(2):
                            for g in range(G):
                                for half in range(2):
                                    ins = nc.tensor.matmul(pa[:, 0, s * HEADS + g * 4:s * HEADS + g * 4 + 4], sq[:, 2 * s + half, g, :],
                                                           head_sum[:, :], start=half == 0, stop=half == 1)
                        ins.then_inc(norm_ps, 1)
                    if late is not None:
                        pe.wait_ge(o_ready, START + late + 1)
                        if n is not None:
                            pe.wait_ge(rot, START + 8 * n + 8)
                        for gp in range(2):
                            for w in range(4):
                                ins = nc.tensor.transpose(pa[:, 2 + gp, w * P:(w + 1) * P], o[:, w, gp * P:(gp + 1) * P], ident[:, :])
                        ins.then_inc(oT_ps, 1)
                    if n is not None:
                        pe.wait_ge(rnorm_ready, START + n + 1)
                        pe.wait_ge(rot, START + 8 * n + 8)
                        for g in range(G):
                            ins = nc.tensor.matmul(pa[:, 1, g * BLK:(g + 1) * BLK],
                                                   rk_wide[:, g * BLK:(g + 1) * BLK], ident[:, :], start=True, stop=True)
                        ins.then_inc(spread_ps, 1)
                        pe.wait_ge(oT_ready, START + n)
                        pe.wait_ge(hs_ready, START + n + 1)
                        for c in range(2):
                            nc.tensor.matmul(pa[:, 2 + c, :], hs[:, :], wv[:, c * 512:(c + 1) * 512], start=True, stop=True).then_inc(v_ps, 1)
                    if late is not None:
                        pe.wait_ge(oT_ready, START + late + 1)
                        for gp in range(2):
                            for r in range(4):
                                ins = nc.tensor.matmul(pa[:, 0, P:2 * P], wo[:, gp, r, :], oT[:, gp, :, r * WIN:(r + 1) * WIN],
                                                       start=gp + r == 0, stop=gp + r == 4)
                        ins.then_inc(wo_ps, 1)
                    if n is not None:
                        pe.wait_ge(rope_add, START + 4 * n + 2)
                        pe.wait_ge(kr_ready, START + 2 * n + 2)
                        for r in range(4):
                            nc.tensor.matmul(pw[:, r, 0:256], ident16[:, :], bcast_mid(mask[:, :, :].rearrange("p c j -> p (c j)")
                                             [:, bass.ds((i % BPS) * 2 * WIN, 2 * WIN)], G), start=True, stop=False, skip_group_check=True)
                        for w in range(4):
                            for g in range(G):
                                for half in range(2):
                                    for r in range(4):
                                        rs = slice(WIN * r, WIN * r + WIN)
                                        ins = nc.tensor.matmul(pw[WIN * w:WIN * w + WIN, r, g * 2 * WIN:(g + 1) * 2 * WIN],
                                                               qr[rs, half, g, WIN * w:WIN * w + WIN], kr[rs, half, g, WIN * w:WIN * w + 2 * WIN],
                                                               start=False, stop=half == 1, skip_group_check=True, tile_position=(WIN * r, WIN * w))
                        ins.then_inc(sim_ps, 1)

                pipelined(pe, layer, step)
                pe.wait_ge(xb_done, START + BL * layer + BL)
                pe.wait_ge(fw, START + FW * layer + FW)
                own_wait(pe, passed)
                with pe.Fori(0, BATCH) as b:
                    for c in range(2):
                        n = layer * FL + b * 2 + c
                        ln.tensor(pe, PRE + n, xbf[:, bass.ds(b * SROW + c * CH, CH)], pa[:, 0, :], pa[:, 1, 0:4])
                        pe.wait_ge(ln.out_ready, START + PRE + n + 1)
                        for j in range(NFB + 1):
                            if j < NFB:
                                if j >= 2:
                                    pe.wait_ge(hidden_ready, START + NFB * n + j - 1)
                                nc.tensor.matmul(pa[0:FB[j], 2 + j % 2, :], w1[:, j * P:j * P + FB[j]], h[:, :], start=True, stop=True)
                                nc.tensor.matmul(pw[0:FB[j], j % 2, :], w1[:, INNER + j * P:INNER + j * P + FB[j]], h[:, :],
                                                 start=True, stop=True).then_inc(ff_ps, 1)
                            if j > 0:
                                pe.wait_ge(hidden_ready, START + NFB * n + j)
                                ins = nc.tensor.matmul(pw[:, 2, :], w2[0:FB[j - 1], j - 1, :], act_out[0:FB[j - 1], j - 1, :],
                                                       start=j == 1, stop=j == NFB)
                        ins.then_inc(y_ps, 1)
                pe.wait_ge(xa_done, START + FL * layer + FL)

        @block.scalar
        def _(act):
            with act.Fori(0, BATCH) as b:
                act.wait_ge(mods_ready, START + b + 1)
                for c in range(2):
                    n = b * 2 + c
                    ln.scalar_squares(act, n)
                    at = b * SROW + c * CH
                    ln.scalar_out(act, n, [(slice(0, DH), xaf[0:DH, bass.ds(at, CH)]), (slice(DH, P), xaf[DH:P, bass.ds(at + 1, CH)])], mods[:, 0:1])
            with act.Fori(0, DEPTH) as layer:
                def step(n, late, i, li):
                    if n is not None:
                        act.wait_ge(norm_ps, START + n)
                        for s in range(4):
                            act.wait_ge(qk_ps, START + 4 * n + s + 1)
                            nc.scalar.activation(sq[:, s, :, :], pa[:, s, :].rearrange("p (g t) -> p g t", g=G), ACT.Square).then_inc(sq_ready, 1)
                    if late is not None:
                        act.wait_ge(pv_ps, START + late + 1)
                        nc.scalar.activation(o[:, :, :], pw[:, :, 256:512], ACT.Copy).then_inc(o_ready, 1)
                        act.wait_ge(oT_ps, START + late + 1)
                        nc.scalar.activation(oT[:, :, :, :].rearrange("p a w n -> p a (w n)"), pa[:, 2:4, :], ACT.Copy).then_inc(oT_ready, 1)
                    if n is not None:
                        act.wait_ge(vtail_dma, START + 16 * n)
                        act.wait_ge(pv_ps, START + n)
                        for c in range(2):
                            act.wait_ge(v_ps, START + 2 * n + c + 1)
                            nc.scalar.activation(v[:, c * 512:(c + 1) * 512], pa[:, 2 + c, :], ACT.Copy).then_inc(v_ready, 1)
                        act.wait_ge(ebias_ready, START + n + 1)
                        act.wait_ge(probsT_ready, START + n)
                        for r in range(4):
                            for g in range(G):
                                k = r * G + g
                                ins = nc.scalar.activation(probs[:, k, :], pw[:, r, g * 2 * WIN:(g + 1) * 2 * WIN], ACT.Exp, bias=ebias[:, k:k + 1],
                                                           scale=rnorm[:, 4 * g + r:4 * g + r + 1], accum_out=total[:, k:k + 1])
                        ins.then_inc(exp_ready, 1)

                pipelined(act, layer, step)
                act.wait_ge(fw, START + FW * layer + FW)
                with act.Fori(0, BATCH) as b:
                    for c in range(2):
                        n = layer * FL + b * 2 + c
                        ln.scalar_squares(act, PRE + n)
                        ln.scalar_out(act, PRE + n, [(slice(0, P), h[:, :])], fpar[:, 1:2])
                        for j in range(NFB):
                            act.wait_ge(ff_ps, START + NFB * n + j + 1)
                            if j >= 2:
                                act.wait_ge(hidden_ready, START + NFB * n + j - 1)
                            nc.scalar.activation(gelu[0:FB[j], j % 2, :], pw[0:FB[j], j % 2, :], ACT.Gelu,
                                                 bias=fpar[0:FB[j], 3 + NFB + j:4 + NFB + j]).then_inc(gelu_ready, 1)

        @block.vector
        def _(dve):
            dve.wait_ge(consts, START + 48)
            nc.vector.tensor_copy(mask[:, :, :].rearrange("p c j -> p (c j)"), mask32).then_inc(mask_ready, 1)
            nc.vector.tensor_copy(ident16[:, :], ident[:, :]).then_inc(mask_ready, 1)
            dve.wait_ge(mask_ready, START + 2)
            link = Links(dve, flinks)
            with dve.Fori(0, BATCH) as b:
                link.start(b)
                dve.wait_ge(ln.normed_ready, START + 2 * b)
                dve.wait_ge(ln.out_ready, START + 2 * b)
                for k in range(3):
                    ins = nc.vector.tensor_copy(mods[:, k:k + 1], const["mod"][:, bass.ds(b + (3 + k) * BATCH, 1)])
                link(ins)
                dve.sem_inc(mods_ready, 1)
                for c in range(2):
                    ln.vector(dve, b * 2 + c, x[:, bass.ds(b * SEQ + c * CH, CH)], pa[:, 0, :], pa[:, 1, 0:4], mods[:, 1:2])
            dve.wait_ge(ln.out_ready, START + PRE)
            with dve.Fori(0, DEPTH) as layer:
                dve.wait_ge(consts, START + 48)
                dve.wait_ge(aw, START + AW * layer + AW)
                for s in range(2):
                    for half in range(2):
                        for cs in range(2):
                            ins = nc.vector.tensor_scalar(tab[:, 4 * s + 2 * half + cs, :], base_tab[:, 2 * s + cs, :],
                                                          scales[:, 2 * s + half:2 * s + half + 1], None, ALU.mult)
                ins.then_inc(tabs_ready, 1)
                dve.wait_ge(tabs_ready, START + layer + 1)
                link = Links(dve, links)

                def step(n, late, i, li):
                    if n is not None:
                        link.start(VL * n)
                        tc = bass.ds((i % BPS) * BLK, BLK)
                        dve.wait_ge(rope_add, START + 4 * n)
                        for s in range(4):
                            dve.wait_ge(sq_ready, START + 4 * n + s + 1)
                            for cs in range(2):
                                slot = 4 * (s // 2) + (cs if s % 2 == 0 else 3 - cs)
                                nc.vector.tensor_tensor(m[:, slot, :, :], pa[:, s, :].rearrange("p (g t) -> p g t", g=G),
                                                        bcast_mid(tab[:, 2 * s + cs, tc], G), ALU.mult).then_inc(rot, 1)
                        dve.wait_ge(norm_ps, START + n + 1)
                        link(nc.vector.tensor_scalar(norm[:, :], pa[:, 0, 0:2 * HEADS], 1e-24, None, ALU.max))
                        newton_rsqrt(nc, link, rnorm[:, :], norm[:, :], ntmp[:, :])
                        nc.vector.tensor_copy(rk_wide[:, :].rearrange("p (a f) -> p a f", f=HALF), bcast_last(rnorm[:, HEADS:], HALF))\
                            .then_inc(rnorm_ready, 1)
                        dve.wait_ge(ktail, START + n)
                        dve.wait_ge(rope_add, START + 4 * n + 4)
                        dve.wait_ge(spread_ps, START + n + 1)
                        for half in range(2):
                            nc.vector.tensor_tensor(kr[:, half, :, WIN:WIN + BLK], ks[:, half, :, :],
                                                    pa[:, 1, :].rearrange("p (g t) -> p g t", g=G), ALU.mult).then_inc(kr_ready, 1)
                    if late is not None:
                        dve.wait_ge(wo_ps, START + late + 1)
                        c = col(li)
                        nc.vector.tensor_tensor(xbf[0:DH, bass.ds(c, BLK)], pa[0:DH, 0, P:2 * P], xaf[0:DH, bass.ds(c, BLK)], ALU.add)
                        nc.vector.tensor_tensor(xbf[DH:P, bass.ds(c + 1, BLK)], pa[DH:P, 0, P:2 * P], xaf[DH:P, bass.ds(c + 1, BLK)], ALU.add)\
                            .then_inc(xb_done, 1)
                    if n is not None:
                        dve.wait_ge(sim_ps, START + n + 1)
                        link(nc.vector.tensor_reduce(mx[:, :].rearrange("p (r g) -> p r g", r=4),
                                                     pw[:, :, 0:256].rearrange("p r (g j) -> p r g j", g=G), AX.X, ALU.max))
                        nc.vector.scalar_tensor_tensor(ebias[:, :].rearrange("p (r g) -> p r g", r=4), mx[:, :].rearrange("p (r g) -> p r g", r=4), -1.0,
                                                       rnorm[:, 0:HEADS].rearrange("p (g r) -> p r g", r=4), ALU.mult, ALU.mult).then_inc(ebias_ready, 1)
                        dve.wait_ge(exp_ready, START + n + 1)
                        link(nc.vector.reciprocal(recip[:, :], total[:, :]))
                        link(nc.vector.tensor_tensor(probs[:, :, :], probs[:, :, :], bcast_last(recip[:, :], 2 * WIN), ALU.mult))
                        dve.wait_ge(pv_ps, START + n)
                        nc.vector.transpose(probsT[:, :, :].rearrange("p h j -> p (h j)"), probs[:, :, :].rearrange("p h j -> p (h j)"))\
                            .then_inc(probsT_ready, 1)
                        assert link.n == VL, link.n

                pipelined(dve, layer, step)
                dve.wait_ge(xb_done, START + BL * layer + BL)
                dve.wait_ge(fw, START + FW * layer + FW)
                own_wait(dve, passed)
                with dve.Fori(0, BATCH) as b:
                    for c in range(2):
                        n = layer * FL + b * 2 + c
                        at = b * SROW + c * CH
                        ln.vector(dve, PRE + n, xbf[:, bass.ds(at, CH)], pa[:, 0, :], pa[:, 1, 0:4], fpar[:, 0:1])
                        dve.wait_ge(y_ps, START + n)
                        for j in range(NFB):
                            dve.wait_ge(gelu_ready, START + NFB * n + j + 1)
                            nc.vector.scalar_tensor_tensor(act_out[0:FB[j], j, :], pa[0:FB[j], 2 + j % 2, :], fpar[0:FB[j], 3 + j:4 + j],
                                                           gelu[0:FB[j], j % 2, :], ALU.add, ALU.mult).then_inc(hidden_ready, 1)
                        dve.wait_ge(y_ps, START + n + 1)
                        nc.vector.scalar_tensor_tensor(xaf[0:DH, bass.ds(at, CH)], pw[0:DH, 2, :], fpar[0:DH, 2:3], xbf[0:DH, bass.ds(at, CH)], ALU.add, ALU.add)
                        nc.vector.scalar_tensor_tensor(xaf[DH:P, bass.ds(at + 1, CH)], pw[DH:P, 2, :], fpar[DH:P, 2:3], xbf[DH:P, bass.ds(at + 1, CH)],
                                                       ALU.add, ALU.add).then_inc(xa_done, 1)
            dve.wait_ge(xa_done, START + FL * DEPTH)
            for b in range(BATCH):
                at = (3 + 2) * BATCH + b
                for lo, hi, shift in ((0, DH, 0), (DH, P, 1)):
                    nc.vector.scalar_tensor_tensor(x[lo:hi, b * SEQ:(b + 1) * SEQ], xa[lo:hi, b, shift:shift + SEQ], const["mod"][lo:hi, at:at + 1],
                                                   x[lo:hi, b * SEQ:(b + 1) * SEQ], ALU.mult, ALU.add)


def rwkv(nc, const, t):
    ctx = ExitStack()
    with ctx:
        sb = lambda s, sh, dt=F32: ctx.enter_context(nc.sbuf_tensor("wkv_" + s, sh, dt))
        sems, sem = semaphores(nc, ctx, "wkv_")
        ln = LayerNorm(nc, ctx, "wkv_ln", const, sem)
        x = const["x"]
        w = sb("w", [P, 4, P])
        decay = sb("decay", [P, 2])
        wdec = sb("wdec", [P, 1])
        ew = sb("ew", [P, 1])
        mods = sb("mods", [P, 3])
        h, k, v, sr = sb("h", [P, SEQ]), sb("k", [P, SEQ]), sb("v", [P, SEQ]), sb("sr", [P, SEQ])
        pp, aa, bb = sb("pp", [P, SEQ + 1]), sb("aa", [P, SEQ + 1]), sb("bb", [P, SEQ + 1])
        e1, e2, f1, f2, pm = (sb(n, [P, SEQ]) for n in ("e1", "e2", "f1", "f2", "pm"))
        e2v, num, den, f2v = (sb(n, [P, SEQ]) for n in ("e2v", "num", "den", "f2v"))
        ps = [ctx.enter_context(nc.psum_tensor(f"wkv_ps{i}", [P, 2 * CH], F32)) for i in range(3)]
        ps_ln = ctx.enter_context(nc.psum_tensor("wkv_ps_ln", [P, CH], F32))
        ps_small = ctx.enter_context(nc.psum_tensor("wkv_ps_small", [P, CH], F32))
        loaded, w_ready, mods_ready, init = sem("loaded"), sem("w_ready"), sem("mods_ready"), sem("init")
        proj_ps, proj_ready, arg_ready, exp_ready = sem("proj_ps"), sem("proj_ready"), sem("arg_ready"), sem("exp_ready")
        den_part, y_ready, out_ps, x_done, links, pool_links = sem("den_part"), sem("y_ready"), sem("out_ps"), sem("x_done"), sem("links"), sem("pool_links")
        block = ctx.enter_context(nc.Block())
        VL = 13

        @block.sync
        def _(sp):
            for s in sems:
                sp.sem_inc(s, START)
            sp.dma_start(w[:, :, :], t["wkv_w"]).then_inc(loaded, 16)
            sp.dma_start(decay[:, :], t["wkv_decay"]).then_inc(loaded, 16)
            sp.wait_ge(loaded, START + 32)

        @block.tensor
        def _(pe):
            pe.wait_ge(loaded, START + 32)
            with pe.Fori(0, BATCH) as b:
                for c in range(2):
                    ln.tensor(pe, b * 2 + c, x[:, bass.ds(b * SEQ + c * CH, CH)], ps_ln[:, :], ps_small[:, 0:4])
                pe.wait_ge(ln.out_ready, START + 2 * b + 2)
                pe.wait_ge(x_done, START + b)
                for i in (2, 1, 0):
                    for c in range(2):
                        ins = nc.tensor.matmul(ps[i][:, c * CH:(c + 1) * CH], w[:, i, :], h[:, c * CH:(c + 1) * CH], start=True, stop=True)
                    ins.then_inc(proj_ps, 1)
                pe.wait_ge(y_ready, START + b + 1)
                for c in range(2):
                    ins = nc.tensor.matmul(ps[0][:, c * CH:(c + 1) * CH], w[:, 3, :], num[:, c * CH:(c + 1) * CH], start=True, stop=True)
                ins.then_inc(out_ps, 1)

        @block.gpsimd
        def _(pool):
            nc.gpsimd.memset(pp[:, 0:1], -1e38)
            nc.gpsimd.memset(aa[:, 0:1], 0.0)
            nc.gpsimd.memset(bb[:, 0:1], 0.0).then_inc(init, 1)
            with pool.Fori(0, BATCH) as b:
                pool.wait_ge(proj_ready, START + 3 * b + 2)
                pool.wait_ge(exp_ready, START + 4 * b + 2)
                nc.gpsimd.tensor_tensor(e2v[:, :], e2[:, :], v[:, :], ALU.mult).then_inc(den_part, 1)
                pool.wait_ge(exp_ready, START + 4 * b + 4)
                nc.gpsimd.tensor_tensor(f2v[:, :], f2[:, :], v[:, :], ALU.mult).then_inc(den_part, 1)

        @block.scalar
        def _(act):
            act.wait_ge(loaded, START + 32)
            nc.scalar.activation(ew[:, :], decay[:, 0:1], ACT.Exp).then_inc(w_ready, 1)
            with act.Fori(0, BATCH) as b:
                act.wait_ge(mods_ready, START + b + 1)
                for c in range(2):
                    n = b * 2 + c
                    ln.scalar_squares(act, n)
                    ln.scalar_out(act, n, [(slice(0, P), h[:, c * CH:(c + 1) * CH])], mods[:, 0:1])
                act.wait_ge(proj_ps, START + 3 * b + 1)
                nc.scalar.activation(k[:, :], ps[2][:, :], ACT.Copy).then_inc(proj_ready, 1)
                act.wait_ge(proj_ps, START + 3 * b + 2)
                nc.scalar.activation(v[:, :], ps[1][:, :], ACT.Copy).then_inc(proj_ready, 1)
                act.wait_ge(proj_ps, START + 3 * b + 3)
                nc.scalar.activation(sr[:, :], ps[0][:, :], ACT.Tanh, scale=0.5).then_inc(proj_ready, 1)
                for i, buf in enumerate((e1, e2, f1, f2)):
                    act.wait_ge(arg_ready, START + 4 * b + i + 1)
                    nc.scalar.activation(buf[:, :], buf[:, :], ACT.Exp).then_inc(exp_ready, 1)

        @block.vector
        def _(dve):
            link = Links(dve, links)
            dve.wait_ge(w_ready, START + 1)
            link(nc.vector.tensor_scalar(wdec[:, :], ew[:, :], -1.0, None, ALU.mult))
            dve.wait_ge(init, START + 1)
            with dve.Fori(0, BATCH) as b:
                link.start(1 + b * VL)
                dve.wait_ge(ln.out_ready, START + 2 * b)
                dve.wait_ge(x_done, START + b)
                for i in range(3):
                    ins = nc.vector.tensor_copy(mods[:, i:i + 1], const["mod"][:, bass.ds(b + (6 + i) * BATCH, 1)])
                link(ins)
                dve.sem_inc(mods_ready, 1)
                for c in range(2):
                    ln.vector(dve, b * 2 + c, x[:, bass.ds(b * SEQ + c * CH, CH)], ps_ln[:, :], ps_small[:, 0:4], mods[:, 1:2])
                dve.wait_ge(proj_ready, START + 3 * b + 1)
                first, now, prev = decay[:, 1:2], slice(1, SEQ + 1), slice(0, SEQ)
                link(nc.vector.tensor_tensor_scan(pp[:, now], wdec[:, 0:1].broadcast_to([P, SEQ]), k[:, :], -1e38, ALU.add, ALU.max))
                nc.vector.scalar_tensor_tensor(e1[:, :], pp[:, prev], wdec[:, :], pp[:, now], ALU.add, ALU.subtract).then_inc(arg_ready, 1)
                nc.vector.tensor_tensor(e2[:, :], k[:, :], pp[:, now], ALU.subtract).then_inc(arg_ready, 1)
                link(nc.vector.scalar_tensor_tensor(pm[:, :], k[:, :], first, pp[:, prev], ALU.add, ALU.max))
                nc.vector.tensor_tensor(f1[:, :], pp[:, prev], pm[:, :], ALU.subtract).then_inc(arg_ready, 1)
                nc.vector.scalar_tensor_tensor(f2[:, :], k[:, :], first, pm[:, :], ALU.add, ALU.subtract).then_inc(arg_ready, 1)
                dve.wait_ge(exp_ready, START + 4 * b + 2)
                link(nc.vector.tensor_tensor_scan(bb[:, now], e1[:, :], e2[:, :], 0.0, ALU.mult, ALU.add))
                dve.wait_ge(den_part, START + 2 * b + 1)
                link(nc.vector.tensor_tensor_scan(aa[:, now], e1[:, :], e2v[:, :], 0.0, ALU.mult, ALU.add))
                dve.wait_ge(exp_ready, START + 4 * b + 4)
                link(nc.vector.tensor_tensor(den[:, :], f1[:, :], bb[:, prev], ALU.mult))
                link(nc.vector.tensor_tensor(den[:, :], den[:, :], f2[:, :], ALU.add))
                link(nc.vector.reciprocal(den[:, :], den[:, :]))
                link(nc.vector.tensor_tensor(num[:, :], f1[:, :], aa[:, prev], ALU.mult))
                dve.wait_ge(den_part, START + 2 * b + 2)
                link(nc.vector.tensor_tensor(num[:, :], num[:, :], f2v[:, :], ALU.add))
                link(nc.vector.tensor_tensor(num[:, :], num[:, :], den[:, :], ALU.mult))
                dve.wait_ge(proj_ready, START + 3 * b + 3)
                nc.vector.scalar_tensor_tensor(num[:, :], sr[:, :], 1.0, num[:, :], ALU.add, ALU.mult).then_inc(y_ready, 1)
                link(nc.vector.tensor_scalar(mods[:, 2:3], mods[:, 2:3], 0.5, None, ALU.mult))
                dve.wait_ge(out_ps, START + b + 1)
                cols = bass.ds(b * SEQ, SEQ)
                nc.vector.scalar_tensor_tensor(x[:, cols], ps[0][:, :], mods[:, 2:3], x[:, cols], ALU.mult, ALU.add).then_inc(x_done, 1)
                link(nc.vector.tensor_copy(pm[:, 0:1], mods[:, 2:3]))
                assert link.n == VL, link.n


def mixture(nc, const, t, out):
    ctx = ExitStack()
    with ctx:
        sb = lambda s, sh, dt=F32: ctx.enter_context(nc.sbuf_tensor("moe_" + s, sh, dt))
        sems, sem = semaphores(nc, ctx, "moe_")
        ln = LayerNorm(nc, ctx, "moe_ln", const, sem)
        x, ident = const["x"], const["ident"]
        gate_w, ew, eb, cw = sb("gate_w", [P, EXPERTS]), sb("expert_w", [P, EXPERTS, P]), sb("expert_b", [P, EXPERTS]), sb("combine_w", [P, P])
        mods = sb("mods", [P, 3])
        h = sb("h", [P, CH])
        logits = sb("logits", [P, 4, EXPERTS])
        one = sb("one", [P, 4])
        probs, top, gates = sb("probs", [P, 4, EXPERTS]), sb("top", [P, 4, 8]), sb("gates", [P, 4, EXPERTS])
        idx, idxf, iota = sb("idx", [P, 4, 8], U32), sb("idxf", [P, 4, 8]), sb("iota", [P, 4, EXPERTS])
        wide = sb("wide", [P, 2, 4, P])
        y, yg = sb("y", [P, 2, CH]), sb("yg", [P, 2, CH])
        pb = lambda n: ctx.enter_context(nc.psum_tensor("moe_ps_" + n, [P, CH], F32))
        ps_ln, ps_small, ps_c = pb("ln"), pb("small"), pb("c")
        ps_e, ps_g = [pb(f"e{i}") for i in range(2)], [pb(f"g{i}") for i in range(2)]
        loaded, mods_ready, logits_ps, centred, exp_ready, gates_ready = (sem(n) for n in ("loaded", "mods_ready", "logits_ps", "centred", "exp_ready", "gates_ready"))
        wide_ready, expert_ps, spread_ps, y_ready, yg_ready, c_ps, x_done, stored, links = (
            sem(n) for n in ("wide_ready", "expert_ps", "spread_ps", "y_ready", "yg_ready", "c_ps", "x_done", "stored", "links"))
        passed = sem("passed")
        block = ctx.enter_context(nc.Block())
        VL = 15

        @block.sync
        def _(sp):
            for s in sems:
                sp.sem_inc(s, START)
            for name, dst in (("gate_w", gate_w), ("expert_w", ew), ("expert_b", eb), ("combine_w", cw), ("iota", iota)):
                sp.dma_start(dst[:], t[name]).then_inc(loaded, 16)
            sp.wait_ge(loaded, START + 80)
            with sp.Fori(0, NCH) as n:
                sp.wait_ge(x_done, START + n + 1)
                sp.dma_start(out[:, bass.ds(n * CH, CH)], x[:, bass.ds(n * CH, CH)]).then_inc(stored, 16)
            sp.wait_ge(stored, START + 16 * NCH)

        @block.tensor
        def _(pe):
            pe.wait_ge(loaded, START + 80)
            with pe.Fori(0, NCH) as n:
                ln.tensor(pe, n, x[:, bass.ds(n * CH, CH)], ps_ln[:, :], ps_small[:, 0:4])
                pe.wait_ge(ln.out_ready, START + n + 1)
                for c in range(4):
                    ins = nc.tensor.matmul(ps_small[:, 64 + c * EXPERTS:64 + (c + 1) * EXPERTS], h[:, c * P:(c + 1) * P], gate_w[:, :], start=True, stop=True)
                ins.then_inc(logits_ps, 1)
                for e in range(EXPERTS + 1):
                    if e < EXPERTS:
                        if e >= 2:
                            pe.wait_ge(yg_ready, START + EXPERTS * n + e - 1)
                        nc.tensor.matmul(ps_e[e % 2][:, :], ew[:, e, :], h[:, :], start=True, stop=True).then_inc(expert_ps, 1)
                        pe.wait_ge(wide_ready, START + EXPERTS * n + e + 1)
                        for c in range(4):
                            ins = nc.tensor.matmul(ps_g[e % 2][:, c * P:(c + 1) * P], wide[:, e % 2, c, :], ident[:, :], start=True, stop=True)
                        ins.then_inc(spread_ps, 1)
                    if e > 0:
                        pe.wait_ge(yg_ready, START + EXPERTS * n + e)
                        ins = nc.tensor.matmul(ps_c[:, :], cw[:, :], yg[:, (e - 1) % 2, :], start=e == 1, stop=e == EXPERTS)
                ins.then_inc(c_ps, 1)

        @block.gpsimd
        def _(pool):
            with pool.Fori(0, NCH) as n:
                pool.wait_ge(gates_ready, START + n + 1)
                for e in range(EXPERTS):
                    if e >= 2:
                        pool.wait_ge(spread_ps, START + EXPERTS * n + e - 1)
                    own_wait(pool, passed)
                    nc.gpsimd.tensor_copy(wide[:, e % 2, :, :], bcast_last(gates[:, :, e], P)).then_inc(wide_ready, 1)

        @block.scalar
        def _(act):
            act.wait_ge(loaded, START + 80)
            with act.Fori(0, NCH) as n:
                ln.scalar_squares(act, n)
                act.wait_ge(mods_ready, START + n + 1)
                ln.scalar_out(act, n, [(slice(0, P), h[:, :])], mods[:, 0:1])
                act.wait_ge(centred, START + n + 1)
                nc.scalar.activation(probs[:, :, :], logits[:, :, :], ACT.Exp).then_inc(exp_ready, 1)
                for e in range(EXPERTS):
                    act.wait_ge(expert_ps, START + EXPERTS * n + e + 1)
                    if e >= 2:
                        act.wait_ge(yg_ready, START + EXPERTS * n + e - 1)
                    nc.scalar.activation(y[:, e % 2, :], ps_e[e % 2][:, :], ACT.Silu, bias=eb[:, e:e + 1]).then_inc(y_ready, 1)

        @block.vector
        def _(dve):
            dve.wait_ge(loaded, START + 80)
            link = Links(dve, links)
            with dve.Fori(0, NCH) as n:
                link.start(n * VL)
                dve.wait_ge(ln.out_ready, START + n)
                dve.wait_ge(x_done, START + n)
                for i in range(3):
                    ins = nc.vector.tensor_copy(mods[:, i:i + 1], const["mod"][:, bass.ds(n // 2 + (9 + i) * BATCH, 1)])
                link(ins)
                dve.sem_inc(mods_ready, 1)
                ln.vector(dve, n, x[:, bass.ds(n * CH, CH)], ps_ln[:, :], ps_small[:, 0:4], mods[:, 1:2])
                dve.wait_ge(logits_ps, START + n + 1)
                raw = ps_small[:, 64:64 + 4 * EXPERTS].rearrange("p (c e) -> p c e", c=4)
                link(nc.vector.tensor_reduce(one[:, :], raw, AX.X, ALU.max))
                nc.vector.tensor_tensor(logits[:, :, :], raw, bcast_last(one[:, :], EXPERTS), ALU.subtract).then_inc(centred, 1)
                dve.wait_ge(exp_ready, START + n + 1)
                link(nc.vector.tensor_reduce(one[:, :], probs[:, :, :], AX.X, ALU.add))
                link(nc.vector.reciprocal(one[:, :], one[:, :]))
                link(nc.vector.tensor_tensor(probs[:, :, :], probs[:, :, :], bcast_last(one[:, :], EXPERTS), ALU.mult))
                own_wait(dve, passed)
                for c in range(4):
                    link(nc.vector.max(top[:, c, :], probs[:, c, :]))
                    own_wait(dve, passed)
                for c in range(4):
                    ins = nc.vector.max_index(idx[:, c, :], top[:, c, :], probs[:, c, :])
                link(ins)
                link(nc.vector.tensor_copy(idxf[:, :, :], idx[:, :, :]))
                link(nc.vector.tensor_tensor(gates[:, :, :], iota[:, :, :], idxf[:, :, 0:1].broadcast_to([P, 4, EXPERTS]), ALU.is_equal))
                link(nc.vector.tensor_tensor(logits[:, :, :], iota[:, :, :], idxf[:, :, 1:2].broadcast_to([P, 4, EXPERTS]), ALU.is_equal))
                link(nc.vector.tensor_tensor(gates[:, :, :], gates[:, :, :], logits[:, :, :], ALU.add))
                link(nc.vector.tensor_tensor(gates[:, :, :], gates[:, :, :], probs[:, :, :], ALU.mult))
                dve.sem_inc(gates_ready, 1)
                for e in range(EXPERTS):
                    dve.wait_ge(y_ready, START + EXPERTS * n + e + 1)
                    dve.wait_ge(spread_ps, START + EXPERTS * n + e + 1)
                    nc.vector.tensor_tensor(yg[:, e % 2, :], y[:, e % 2, :], ps_g[e % 2][:, :], ALU.mult).then_inc(yg_ready, 1)
                dve.wait_ge(c_ps, START + n + 1)
                cols = bass.ds(n * CH, CH)
                nc.vector.scalar_tensor_tensor(x[:, cols], ps_c[:, :], mods[:, 2:3], x[:, cols], ALU.mult, ALU.add).then_inc(x_done, 1)
                assert link.n == VL, link.n


def kernel_program(nc, t, out, phases=5):
    ctx = ExitStack()
    with ctx:
        sb = lambda s, sh, dt=F32: ctx.enter_context(nc.sbuf_tensor(s, sh, dt))
        const = {
            "x": sb("x", [P, TOK]), "ident": sb("ident", [P, P]), "mean_w": sb("mean_w", [P, P]),
            "mod": sb("mod", [P, 2 * 6 * BATCH]),
        }
        prepare(nc, const, t)
        if phases >= 1:
            theta_attention(nc, const, t)
        if phases >= 2:
            local_layers(nc, const, t)
        if phases >= 3:
            rwkv(nc, const, t)
        if phases >= 4:
            mixture(nc, const, t, out)
        else:
            store(nc, const, out)


def store(nc, const, out):
    with ExitStack() as ctx:
        sems, sem = semaphores(nc, ctx, "store_")
        stored = sem("stored")
        block = ctx.enter_context(nc.Block())

        @block.sync
        def _(sp):
            for s in sems:
                sp.sem_inc(s, START)
            sp.dma_start(out, const["x"][:, :]).then_inc(stored, 16)
            sp.wait_ge(stored, START + 16)


def rotary_tables():
    half = np.arange(0, DH, 2, dtype=np.float32)
    inv_freq = (1.0 / np.float32(10000.0) ** (half / np.float32(DH))).astype(np.float32)
    pos = np.arange(SEQ, dtype=np.float32)
    freqs = (inv_freq[:, None] * pos[None, :]).astype(np.float32).astype(np.float64)
    base = ((half + np.float32(0.4 * DH)) / np.float32(1.4 * DH)).astype(np.float32).astype(np.float64)
    scale = base[:, None] ** ((pos[None, :] - SEQ // 2) / (WIN // 2)).astype(np.float64)
    tabs = [8 * np.cos(freqs) * scale, 8 * np.sin(freqs) * scale, np.cos(freqs) / scale, np.sin(freqs) / scale]
    return np.ascontiguousarray(np.stack([np.tile(x, (G, 1)) for x in tabs], 1).astype(np.float32))


def band_mask():
    m = np.full((4, WIN, BPS, 2, WIN), MASKED, np.float32)
    i, j = np.arange(WIN)[:, None], np.arange(WIN)[None, :]
    m[:, :, :, 0, :] = np.where(j >= i, 0.0, MASKED)[None, :, None, :]
    m[:, :, :, 1, :] = np.where(j <= i, 0.0, MASKED)[None, :, None, :]
    m[0, :, 0, 0, :] = MASKED
    return m.reshape(P, BPS * 2 * WIN)


def lay_out(i):
    a = {k: np.asarray(v) for k, v in i.items()}
    c = np.ascontiguousarray
    o = {}
    o["xT"] = c(a["L0_attn_x"].reshape(TOK, P).T)
    o["cT"] = c(np.stack([a["L0_c"].T, a["L1_c"].T], 1))
    o["wmod"] = c(np.stack([a["L0_wmod"], a["L1_wmod"]], 1))
    o["ident"] = np.eye(P, dtype=np.float32)
    o["att_w"] = c(np.stack([a["L0_attn_" + n].T for n in ("Wq", "Wk", "Wv", "Wo")], 1))
    o["att_b"] = c(np.stack([a["L0_attn_" + n] for n in ("bq", "bk", "bv", "bo")], 1))
    o["wkv_w"] = c(np.stack([a["L1_attn_W_rvk"][k * P:(k + 1) * P].T for k in range(3)] + [a["L1_attn_W_out"].T], 1))
    o["wkv_decay"] = c(np.stack([a["L1_attn_time_decay"], a["L1_attn_time_first"]], 1))
    o["gate_w"], o["combine_w"] = c(a["L1_ffn_gate_w"].T), c(a["L1_ffn_combine_w"].T)
    o["expert_w"], o["expert_b"] = c(a["L1_ffn_expert_w"].transpose(2, 0, 1)), c(a["L1_ffn_expert_b"].T)
    o["iota"] = np.ascontiguousarray(np.broadcast_to(np.arange(EXPERTS, dtype=np.float32), (P, 4, EXPERTS)))
    o["tables"], o["mask"] = rotary_tables(), band_mask()
    o["head_sum"] = np.repeat(np.eye(4, dtype=np.float32), WIN, 0)
    wqkv = a["L0_ffn_Wqkv"]
    qk = wqkv[:, :, :2 * HEADS * DH].reshape(DEPTH, P, 2, G, 4, 2, HALF).transpose(0, 1, 2, 5, 3, 4, 6)
    pad = lambda w: c(np.concatenate([w, np.zeros_like(w[:1])], 0))
    o["wqk"] = pad(qk.reshape(DEPTH, P, 2, 2, G, P))
    o["wv"] = pad(wqkv[:, :, 2 * HEADS * DH:])
    wo = a["L0_ffn_Wo"].reshape(DEPTH, 2, 2, 4, DH, P).transpose(0, 2, 4, 1, 3, 5)
    o["wo"] = pad(wo.reshape(DEPTH, P, 2, 4, P))
    sc = np.stack([a["L0_ffn_q_scale"], a["L0_ffn_k_scale"]], 1).reshape(DEPTH, 4, HALF)
    o["scales"] = pad(np.tile(sc.transpose(0, 2, 1), (1, G, 1)))
    o["w1"] = c(a["L0_ffn_W1"])
    pad_rows = lambda w: np.concatenate([w, np.zeros((DEPTH, NFB * P - INNER) + w.shape[2:], np.float32)], 1)
    o["w2"] = c(pad_rows(a["L0_ffn_W2"]).reshape(DEPTH, NFB, P, P).transpose(0, 2, 1, 3))
    b1 = [pad_rows(a["L0_ffn_b1"][:, k * INNER:(k + 1) * INNER]).reshape(DEPTH, NFB, P).transpose(0, 2, 1) for k in range(2)]
    o["fpar"] = c(np.concatenate([a["L0_ffn_ln_g"][:, :, None], a["L0_ffn_ln_b"][:, :, None], a["L0_ffn_b2"][:, :, None]] + b1, 2))
    return o


def kernel(**inputs):
    import concourse.bacc as _bacc
    from concourse.bass_utils import run_bass_kernel_spmd as _run

    nc = _bacc.Bacc("TRN2", target_bir_lowering=False, num_devices=1)
    arrays, t = {}, {}
    for name, a in lay_out(inputs).items():
        arrays[name + "_dram"] = a
        t[name] = nc.dram_tensor(name + "_dram", a.shape, mybir.dt.from_np(a.dtype), kind="ExternalInput").ap()
    out = nc.dram_tensor("out_dram", (P, TOK), F32, kind="ExternalOutput").ap()
    kernel_program(nc, t, out)
    r = _run(nc, [arrays], core_ids=[0])
    return np.ascontiguousarray(r.results[0]["out_dram"].T.reshape(BATCH, SEQ, P))
```

```python
from contextlib import ExitStack

import numpy as np

import concourse.bass as bass
from concourse import mybir

ALU = mybir.AluOpType
ACT = mybir.ActivationFunctionType
AX = mybir.AxisListType
F32 = mybir.dt.float32
BF16 = mybir.dt.bfloat16
I32 = mybir.dt.int32
U32 = mybir.dt.uint32

P = 128
BATCH = 4
SEQ = 1024
TOK = BATCH * SEQ
CH = 512
NCH = TOK // CH
DEPTH = 6
HEADS = 16
DH = 64
HALF = DH // 2
WIN = 32
PAIRS = HEADS // 2
BLK = 128
NBLK = TOK // BLK
BPS = SEQ // BLK
SROW = SEQ + 2
INNER = 341
NFB = -(-INNER // P)
FB = [min(P, INNER - P * j) for j in range(NFB)]
EXPERTS = 8
MASKED = -1.0e30
RSQRT_MAGIC = float(0x5F3759DF)
EPS = 1e-5
START = 1


def semaphores(nc, ctx, prefix):
    made = []

    def sem(name):
        made.append(ctx.enter_context(nc.semaphore(prefix + name)))
        return made[-1]

    return made, sem


class Links:

    def __init__(self, eng, sem):
        self.eng, self.sem, self.base, self.n = eng, sem, 0, 0

    def start(self, base):
        self.base, self.n = base, 0

    def __call__(self, ins):
        ins.then_inc(self.sem, 1)
        self.n += 1
        self.eng.wait_ge(self.sem, START + self.base + self.n)


def bcast_mid(ap, n):
    return ap.unsqueeze(1).broadcast_to([ap.shape[0], n, ap.shape[1]])


def bcast_last(ap, n):
    return ap.unsqueeze(len(ap.shape)).broadcast_to(list(ap.shape) + [n])


def newton_rsqrt(nc, link, y, v, a, last=None):
    link(nc.vector.tensor_scalar(y.bitcast(I32), v.bitcast(I32), -0.5, RSQRT_MAGIC, ALU.mult, ALU.add))
    for i in range(3):
        link(nc.vector.scalar_tensor_tensor(a, y, -0.5, v, ALU.mult, ALU.mult))
        link(nc.vector.tensor_tensor(a, a, y, ALU.mult))
        ins = nc.vector.scalar_tensor_tensor(y, a, 1.5, y, ALU.add, ALU.mult)
        if i < 2 or last is None:
            link(ins)
        else:
            ins.then_inc(last, 1)


def own_wait(eng, passed):
    eng.sem_inc(passed, 1)


LN_LINKS = 1 + 10


class LayerNorm:

    def __init__(self, nc, ctx, name, const, phase_sem):
        self.nc, self.const = nc, const
        sb = lambda s, sh: ctx.enter_context(nc.sbuf_tensor(f"{name}_{s}", sh, F32))
        sem = lambda s: phase_sem("ln_" + s)
        self.xc = sb("centred", [P, CH])
        self.sq = sb("squares", [P, CH])
        self.xn = sb("normed", [P, CH])
        self.var = sb("var", [P, 4])
        self.rstd = sb("rstd", [P, 4])
        self.tmp = sb("tmp", [P, 4])
        self.mean_ready, self.centred_ready, self.squares_ready = sem("mean_ready"), sem("centred_ready"), sem("squares_ready")
        self.var_ready, self.rstd_ready, self.spread_ready = sem("var_ready"), sem("rstd_ready"), sem("spread_ready")
        self.normed_ready, self.out_ready, self.links = sem("normed_ready"), sem("out_ready"), sem("links")

    def tensor(self, pe, n, src, wide, small):
        nc, c = self.nc, self.const
        pe.wait_ge(self.normed_ready, START + n)
        nc.tensor.matmul(wide, c["mean_w"][:, :], src, start=True, stop=True).then_inc(self.mean_ready, 1)
        pe.wait_ge(self.squares_ready, START + n + 1)
        for k in range(4):
            ins = nc.tensor.matmul(small[:, k:k + 1], self.sq[:, k * P:(k + 1) * P], c["mean_w"][:, 0:1], start=True, stop=True)
        ins.then_inc(self.var_ready, 1)
        pe.wait_ge(self.rstd_ready, START + n + 1)
        for k in range(4):
            ins = nc.tensor.matmul(wide[:, k * P:(k + 1) * P], self.rstd[:, k:k + 1].broadcast_to([P, P]),
                                   c["ident"][:, :], start=True, stop=True)
        ins.then_inc(self.spread_ready, 1)

    def vector(self, dve, n, src, wide, small, gain):
        nc = self.nc
        link = Links(dve, self.links)
        link.start(n * LN_LINKS)
        dve.wait_ge(self.mean_ready, START + n + 1)
        nc.vector.tensor_tensor(self.xc[:, :], src, wide, ALU.subtract).then_inc(self.centred_ready, 1)
        dve.wait_ge(self.var_ready, START + n + 1)
        link(nc.vector.tensor_scalar(self.var[:, :], small, EPS, None, ALU.add))
        newton_rsqrt(nc, link, self.rstd[:, :], self.var[:, :], self.tmp[:, :])
        dve.sem_inc(self.rstd_ready, 1)
        dve.wait_ge(self.spread_ready, START + n + 1)
        dve.wait_ge(self.out_ready, START + n)
        nc.vector.scalar_tensor_tensor(self.xn[:, :], self.xc[:, :], gain, wide, ALU.mult, ALU.mult).then_inc(self.normed_ready, 1)

    def scalar_squares(self, act, n):
        act.wait_ge(self.centred_ready, START + n + 1)
        self.nc.scalar.activation(self.sq[:, :], self.xc[:, :], ACT.Square).then_inc(self.squares_ready, 1)

    def scalar_out(self, act, n, dsts, bias):
        act.wait_ge(self.normed_ready, START + n + 1)
        for ps, dst in dsts:
            ins = self.nc.scalar.activation(dst, self.xn[ps, :], ACT.Identity, bias=bias[ps, :])
        ins.then_inc(self.out_ready, 1)


def prepare(nc, const, t):
    ctx = ExitStack()
    with ctx:
        sb = lambda s, sh, dt=F32: ctx.enter_context(nc.sbuf_tensor("prep_" + s, sh, dt))
        sems, sem = semaphores(nc, ctx, "prep_")
        cT = sb("cT", [P, 2, BATCH])
        silu = sb("silu", [P, 2, BATCH])
        wmod = sb("wmod", [P, 2, 6 * P])
        neg = sb("neg", [P, 2, 2, BATCH])
        sign = sb("sign", [P, 2, 2, BATCH])
        ps = ctx.enter_context(nc.psum_tensor("prep_ps", [P, 512], F32))
        loaded, silu_ready, mod_ready, links, ones = sem("loaded"), sem("silu_ready"), sem("mod_ready"), sem("links"), sem("ones")
        block = ctx.enter_context(nc.Block())
        mod = const["mod"]

        @block.sync
        def _(sp):
            for s in sems:
                sp.sem_inc(s, START)
            sp.dma_start(const["x"][:, :], t["xT"]).then_inc(loaded, 16)
            sp.dma_start(cT[:, :, :], t["cT"]).then_inc(loaded, 16)
            sp.dma_start(wmod[:, :, :], t["wmod"]).then_inc(loaded, 16)
            sp.dma_start(const["ident"][:, :], t["ident"]).then_inc(loaded, 16)
            sp.wait_ge(loaded, START + 64)

        @block.gpsimd
        def _(pool):
            nc.gpsimd.memset(const["mean_w"][:, :], 1.0 / P).then_inc(ones, 1)

        @block.scalar
        def _(act):
            act.wait_ge(loaded, START + 64)
            nc.scalar.activation(silu[:, :, :], cT[:, :, :], ACT.Silu).then_inc(silu_ready, 1)

        @block.tensor
        def _(pe):
            pe.wait_ge(silu_ready, START + 1)
            for b in range(2):
                for j in range(6):
                    ins = nc.tensor.matmul(ps[:, (b * 6 + j) * BATCH:(b * 6 + j + 1) * BATCH], wmod[:, b, j * P:(j + 1) * P],
                                           silu[:, b, :], start=True, stop=True)
            ins.then_inc(mod_ready, 1)

        @block.vector
        def _(dve):
            link = Links(dve, links)
            dve.wait_ge(mod_ready, START + 1)
            psm = ps[:, 0:48].rearrange("p (b j n) -> p b j n", b=2, j=6)
            link(nc.vector.tensor_copy(mod[:, :], ps[:, 0:48]))
            m = mod[:, :].rearrange("p (b k j n) -> p b k j n", b=2, k=2, j=3)
            for b in range(2):
                link(nc.vector.tensor_scalar(m[:, b, :, 1, :], m[:, b, :, 1, :], 1.0, None, ALU.add))
                gate = m[:, b, :, 2, :]
                link(nc.vector.tensor_scalar(neg[:, b, :, :], gate, -1.0, None, ALU.mult))
                link(nc.vector.tensor_scalar(sign[:, b, :, :], gate, 0.0, 2.0, ALU.is_ge, ALU.mult))
                link(nc.vector.tensor_tensor(gate, gate, neg[:, b, :, :], ALU.max))
                link(nc.vector.tensor_scalar(gate, gate, 0.25, None, ALU.max))
                link(nc.vector.scalar_tensor_tensor(gate, sign[:, b, :, :], -1.0, gate, ALU.add, ALU.mult))


def modcol(const, block, which, b):
    at = (block * 6 + which) * BATCH + b
    return const["mod"][:, at:at + 1]


def theta_attention(nc, const, t):
    ctx = ExitStack()
    with ctx:
        sb = lambda s, sh, dt=F32: ctx.enter_context(nc.sbuf_tensor("att_" + s, sh, dt))
        pb = lambda s, sh: ctx.enter_context(nc.psum_tensor("att_ps_" + s, sh, F32))
        sems, sem = semaphores(nc, ctx, "att_")
        ln = LayerNorm(nc, ctx, "att_ln", const, sem)
        x = const["x"]
        w = sb("w", [P, 4, P])
        bias = sb("bias", [P, 4])
        out_bias = sb("out_bias", [P, 1])
        mods = sb("mods", [P, 3])
        gated_bias = sb("gated_bias", [P, 1])
        h = sb("h", [P, SEQ])
        q, k, v = sb("q", [P, SEQ]), sb("k", [P, SEQ]), sb("v", [P, SEQ])
        t1, t2, theta = sb("t1", [P, SEQ]), sb("t2", [P, SEQ]), sb("theta", [P, SEQ])
        probs, probsT = sb("probs", [P, SEQ]), sb("probsT", [P, SEQ])
        mx, shift, total, recip = sb("mx", [P, 1]), sb("shift", [P, 1]), sb("total", [P, 1]), sb("recip", [P, 1])
        spread, oT, upd = sb("spread", [P, P]), sb("oT", [P, P]), sb("upd", [P, P])
        ps_s = pb("scores", [P, SEQ])
        ps_t = pb("probsT", [P, SEQ])
        ps_ln, ps_small, ps_o, ps_y = pb("ln", [P, CH]), pb("small", [P, CH]), pb("o", [P, CH]), pb("y", [P, CH])
        loaded, bias_ps, bias_ready, mods_ready = sem("loaded"), sem("bias_ps"), sem("bias_ready"), sem("mods_ready")
        proj_ps, proj_ready, scores_ps, tanh_ready = sem("proj_ps"), sem("proj_ready"), sem("scores_ps"), sem("tanh_ready")
        theta_ready, probs_ready, probsT_ps = sem("theta_ready"), sem("probs_ready"), sem("probsT_ps")
        probsT_a, probsT_d = sem("probsT_act"), sem("probsT_dve")
        recip_ready, pv_ps, o_ready, y_ps, x_done = sem("recip_ready"), sem("pv_ps"), sem("o_ready"), sem("y_ps"), sem("x_done")
        links, setup_links, scores_used = sem("links"), sem("setup_links"), sem("scores_used")
        block = ctx.enter_context(nc.Block())
        NS = SEQ // P
        VL = 1 + 5 * NS

        @block.sync
        def _(sp):
            for s in sems:
                sp.sem_inc(s, START)
            sp.dma_start(w[:, :, :], t["att_w"]).then_inc(loaded, 16)
            sp.dma_start(bias[:, :], t["att_b"]).then_inc(loaded, 16)
            sp.wait_ge(loaded, START + 32)

        @block.tensor
        def _(pe):
            pe.wait_ge(loaded, START + 32)
            nc.tensor.matmul(ps_y[:, 0:1], w[:, 3, :], bias[:, 2:3], start=True, stop=True).then_inc(bias_ps, 1)
            pe.wait_ge(bias_ready, START + 1)
            with pe.Fori(0, BATCH) as b:
                for c in range(2):
                    ln.tensor(pe, b * 2 + c, x[:, bass.ds(b * SEQ + c * CH, CH)], ps_ln[:, :], ps_small[:, 0:4])
                pe.wait_ge(ln.out_ready, START + 2 * b + 2)
                for i, dst in ((0, ps_s), (1, ps_t)):
                    for c in range(2):
                        ins = nc.tensor.matmul(dst[:, c * CH:(c + 1) * CH], w[:, i, :], h[:, c * CH:(c + 1) * CH], start=True, stop=True)
                    ins.then_inc(proj_ps, 1)
                pe.wait_ge(proj_ready, START + 3 * b + 1)
                for j in range(NS):
                    ins = nc.tensor.matmul(ps_s[:, j * P:(j + 1) * P], h[:, j * P:(j + 1) * P], w[:, 2, :], start=True, stop=True)
                ins.then_inc(proj_ps, 1)
                pe.wait_ge(proj_ready, START + 3 * b + 3)
                for j in range(NS + 2):
                    n = b * NS + j
                    if j < NS:
                        pe.wait_ge(scores_used, START + n)
                        for c in range(2):
                            ins = nc.tensor.matmul(ps_s[:, c * CH:(c + 1) * CH], q[:, j * P:(j + 1) * P], k[:, c * CH:(c + 1) * CH], start=True, stop=True)
                        ins.then_inc(scores_ps, 1)
                    if j >= 2:
                        pe.wait_ge(o_ready, START + n - 1)
                        nc.tensor.matmul(ps_y[:, 0:P], w[:, 3, :], oT[:, :], start=True, stop=True).then_inc(y_ps, 1)
                    if 1 <= j <= NS:
                        pe.wait_ge(probs_ready, START + n)
                        for c in range(8):
                            ins = nc.tensor.transpose(ps_t[:, c * P:(c + 1) * P], probs[:, c * P:(c + 1) * P], const["ident"][:, :])
                        ins.then_inc(probsT_ps, 1)
                        pe.wait_ge(recip_ready, START + n)
                        nc.tensor.matmul(ps_o[:, P:2 * P], recip[:, 0:1].broadcast_to([P, P]), const["ident"][:, :], start=True, stop=True)
                        pe.wait_ge(probsT_a, START + n)
                        pe.wait_ge(probsT_d, START + n)
                        for c in range(8):
                            ins = nc.tensor.matmul(ps_o[:, 0:P], v[:, c * P:(c + 1) * P], probsT[:, c * P:(c + 1) * P], start=c == 0, stop=c == 7)
                        ins.then_inc(pv_ps, 1)
                pe.wait_ge(x_done, START + NS * b + NS)

        @block.scalar
        def _(act):
            act.wait_ge(loaded, START + 32)
            with act.Fori(0, BATCH) as b:
                act.wait_ge(mods_ready, START + b + 1)
                for c in range(2):
                    n = b * 2 + c
                    ln.scalar_squares(act, n)
                    ln.scalar_out(act, n, [(slice(0, P), h[:, c * CH:(c + 1) * CH])], mods[:, 0:1])
                act.wait_ge(proj_ps, START + 3 * b + 1)
                nc.scalar.activation(q[:, :], ps_s[:, :], ACT.Identity, bias=bias[:, 0:1]).then_inc(proj_ready, 1)
                act.wait_ge(proj_ps, START + 3 * b + 2)
                nc.scalar.activation(k[:, :], ps_t[:, :], ACT.Identity, bias=bias[:, 1:2]).then_inc(proj_ready, 1)
                act.wait_ge(proj_ps, START + 3 * b + 3)
                nc.scalar.activation(v[:, :], ps_s[:, :], ACT.Copy).then_inc(proj_ready, 1)
                for j in range(NS + 1):
                    n = b * NS + j
                    if j < NS:
                        act.wait_ge(scores_ps, START + n + 1)
                        for c in range(2):
                            cols = slice(c * CH, (c + 1) * CH)
                            nc.scalar.activation(t1[:, cols], ps_s[:, cols], ACT.Tanh, scale=0.5)
                            nc.scalar.activation(t2[:, cols], ps_s[:, cols], ACT.Tanh).then_inc(tanh_ready, 1)
                    if j >= 1:
                        act.wait_ge(probsT_ps, START + n)
                        nc.scalar.activation(probsT[:, 0:CH], ps_t[:, 0:CH], ACT.Copy).then_inc(probsT_a, 1)
                    if j < NS:
                        act.wait_ge(theta_ready, START + n + 1)
                        nc.scalar.activation(probs[:, :], theta[:, :], ACT.Exp, bias=shift[:, :], scale=0.15, accum_out=total[:, :]).then_inc(probs_ready, 1)

        @block.vector
        def _(dve):
            link = Links(dve, setup_links)
            dve.wait_ge(loaded, START + 32)
            dve.wait_ge(bias_ps, START + 1)
            link(nc.vector.tensor_tensor(out_bias[:, :], ps_y[:, 0:1], bias[:, 3:4], ALU.add))
            dve.sem_inc(bias_ready, 1)
            link = Links(dve, links)
            with dve.Fori(0, BATCH) as b:
                link.start(b * VL)
                for i in range(3):
                    ins = nc.vector.tensor_copy(mods[:, i:i + 1], const["mod"][:, bass.ds(b + i * BATCH, 1)])
                link(ins)
                dve.sem_inc(mods_ready, 1)
                nc.vector.tensor_tensor(gated_bias[:, :], mods[:, 2:3], out_bias[:, :], ALU.mult)
                for c in range(2):
                    ln.vector(dve, b * 2 + c, x[:, bass.ds(b * SEQ + c * CH, CH)], ps_ln[:, :], ps_small[:, 0:4], mods[:, 1:2])
                for j in range(NS + 2):
                    n = b * NS + j
                    if j < NS:
                        for c in range(2):
                            cols = slice(c * CH, (c + 1) * CH)
                            dve.wait_ge(tanh_ready, START + 2 * n + c + 1)
                            ins = nc.vector.scalar_tensor_tensor(theta[:, cols], ps_s[:, cols], 0.0, t1[:, cols], ALU.max, ALU.add)
                        link(ins)
                        dve.sem_inc(scores_used, 1)
                    if 1 <= j <= NS:
                        dve.wait_ge(probsT_ps, START + n)
                        nc.vector.tensor_copy(probsT[:, CH:], ps_t[:, CH:]).then_inc(probsT_d, 1)
                    if j < NS:
                        link(nc.vector.scalar_tensor_tensor(theta[:, :], theta[:, :], 2.0 / 3.0, t2[:, :], ALU.mult, ALU.add))
                        link(nc.vector.tensor_reduce(mx[:, :], theta[:, :], AX.X, ALU.max))
                        nc.vector.tensor_scalar(shift[:, :], mx[:, :], -0.15, None, ALU.mult).then_inc(theta_ready, 1)
                    if j >= 2:
                        dve.wait_ge(y_ps, START + n - 1)
                        link(nc.vector.tensor_scalar(upd[:, :], ps_y[:, 0:P], mods[:, 2:3], gated_bias[:, 0:1], ALU.mult, ALU.add))
                        cols = bass.ds(b * SEQ + (j - 2) * P, P)
                        nc.vector.tensor_tensor(x[:, cols], x[:, cols], upd[:, :], ALU.add).then_inc(x_done, 1)
                    if 1 <= j <= NS:
                        dve.wait_ge(pv_ps, START + n)
                        link(nc.vector.tensor_copy(spread[:, :], ps_o[:, P:2 * P]))
                        nc.vector.tensor_tensor(oT[:, :], ps_o[:, 0:P], spread[:, :], ALU.mult).then_inc(o_ready, 1)
                    if j < NS:
                        dve.wait_ge(probs_ready, START + n + 1)
                        nc.vector.reciprocal(recip[:, :], total[:, :]).then_inc(recip_ready, 1)
                assert link.n == VL, link.n

def local_layers(nc, const, t):
    ctx = ExitStack()
    with ctx:
        sb = lambda s, sh, dt=F32: ctx.enter_context(nc.sbuf_tensor("loc_" + s, sh, dt))
        sems, sem = semaphores(nc, ctx, "loc_")
        ln = LayerNorm(nc, ctx, "loc_ln", const, sem)
        x, ident = const["x"], const["ident"]
        xa_pad, xb = sb("xa", [P, WIN + BATCH * SROW]), sb("xb", [P, BATCH, SROW])
        xaf, xbf = xa_pad[:, WIN:], xb[:, :, :].rearrange("p b s -> p (b s)")
        xa = xaf.rearrange("p (b s) -> p b s", b=BATCH)
        base_tab, tab = sb("base_tab", [P, 4, SEQ]), sb("tab", [P, 4, SEQ])
        ident16, mask = sb("ident16", [P, P], BF16), sb("mask", [P, BPS, 2 * WIN], BF16)
        head_sum = sb("head_sum", [P, WIN])
        wqk, wv, wo = sb("wqk", [P, 2, PAIRS * P]), sb("wv", [P, 2, PAIRS * DH]), sb("wo", [P, PAIRS, P])
        scales = sb("scales", [P, 2])
        kept = sb("kept", [P, BPS])
        w1, w2, fpar = sb("w1", [P, 2 * INNER]), sb("w2", [P, NFB, P]), sb("fpar", [P, 3 + 2 * NFB])
        mods = sb("mods", [P, 3])
        hs = sb("hs", [P, WIN + BLK])
        sq = sb("sq", [P, 2, PAIRS * BLK])
        m = sb("m", [P, 4, PAIRS * BLK])
        mask32 = m[:, 0, 0:BPS * 2 * WIN]
        act_out = m[:, :, :].rearrange("p a t -> p (a t)").rearrange("p (j t) -> p j t", t=CH)
        qr, ks = sb("qr", [P, PAIRS, BLK]), sb("ks", [P, PAIRS, BLK])
        kr = sb("kr", [P, PAIRS, WIN + BLK])
        nT = sb("nT", [P, 4 * BLK])
        norm, rnorm, ntmp = sb("norm", [P, 2 * HEADS]), sb("rnorm", [P, 2 * HEADS]), sb("ntmp", [P, 2 * HEADS])
        rk_wide = sb("rk_wide", [P, HEADS * DH])
        mx, ebias, total, recip = sb("mx", [P, HEADS]), sb("ebias", [P, HEADS]), sb("total", [P, HEADS]), sb("recip", [P, HEADS])
        probs = sb("probs", [P, PAIRS, 2, 2 * WIN])
        probsT = sb("probsT", [P, PAIRS, BLK])
        v = sb("v", [P, 4, PAIRS * DH])
        o, oT = sb("o", [P, PAIRS, 2, DH]), sb("oT", [P, PAIRS, BLK])
        h, gelu = sb("h", [P, CH]), sb("gelu", [P, 2, CH])
        pa = ctx.enter_context(nc.psum_tensor("loc_pa", [P, 4, 512], F32))
        pw = ctx.enter_context(nc.psum_tensor("loc_pw", [P, 4, 512], F32))

        mask_ready = sem("mask_ready")
        consts, mem, tabs_ready = sem("consts"), sem("mem"), sem("tabs_ready")
        mods_ready, ln_in_done = sem("mods_ready"), sem("ln_in_done")
        aw, fw = sem("attn_weights"), sem("ffn_weights")
        hs_ready, qk_ps, sq_ready, rot, rope_add = sem("hs_ready"), sem("qk_ps"), sem("sq_ready"), sem("rot"), sem("rope_add")
        v_ps, v_ready, norm_ps, nT_ready, nT_ps = sem("v_ps"), sem("v_ready"), sem("norm_ps"), sem("nT_ready"), sem("nT_ps")
        rnorm_ready, spread_ps, kr_ready, ktail = sem("rnorm_ready"), sem("spread_ps"), sem("kr_ready"), sem("ktail")
        sim_ps, ebias_ready, exp_ready, probsT_ps = sem("sim_ps"), sem("ebias_ready"), sem("exp_ready"), sem("probsT_ps")
        probsT_ready, pv_ps, o_ready = sem("probsT_ready"), sem("pv_ps"), sem("o_ready")
        oT_ps, oT_ready, wo_ps, xb_done = sem("oT_ps"), sem("oT_ready"), sem("wo_ps"), sem("xb_done")
        ff_ps, gelu_ready, hidden_ready, y_ps, xa_done = sem("ff_ps"), sem("gelu_ready"), sem("hidden_ready"), sem("y_ps"), sem("xa_done")
        links, late_links, flinks, passed = sem("links"), sem("late_links"), sem("flinks"), sem("passed")
        block = ctx.enter_context(nc.Block())

        BL = NBLK
        FL = NCH
        PRE = NCH
        EARLY_LINKS, LATE_LINKS = 1 + 10 + 2, 1
        AW, FW = 16 * 4, 16 * 3
        MEMSETS = 8

        def pipelined(eng, layer, step):
            first = layer * BL
            step(first, None, None, 0, None, None)
            step(first + 1, first, None, 1, 0, None)
            with eng.Fori(1, BL - 1) as i:
                step(first + i + 1, first + i, first + i - 1, i + 1, i, i - 1)
            step(None, first + BL - 1, first + BL - 2, None, BL - 1, BL - 2)
            step(None, None, first + BL - 1, None, None, BL - 1)

        def col(i):
            return i * BLK + (i // BPS) * (SROW - SEQ)

        @block.sync
        def _(sp):
            for s in sems:
                sp.sem_inc(s, START)
            for name, dst in (("tables", base_tab), ("mask", mask32), ("head_sum", head_sum)):
                sp.dma_start(dst if name == "mask" else dst[:], t[name]).then_inc(consts, 16)

            def attn_weights(layer):
                sp.dma_start(wqk[:, :, :], t["wqk"][bass.ds(layer, 1)].rearrange("l p a n -> (l p) a n")).then_inc(aw, 16)
                sp.dma_start(wv[:, :, :], t["wv"][bass.ds(layer, 1)].rearrange("l p a n -> (l p) a n")).then_inc(aw, 16)
                sp.dma_start(wo[:, :, :], t["wo"][bass.ds(layer, 1)].rearrange("l p a n -> (l p) a n")).then_inc(aw, 16)
                sp.dma_start(scales[:, :], t["scales"][bass.ds(layer, 1)].rearrange("l p n -> (l p) n")).then_inc(aw, 16)

            attn_weights(0)
            sp.wait_ge(mem, START + MEMSETS)
            with sp.Fori(0, DEPTH) as layer:
                sp.wait_ge(xa_done, START + FL * layer)
                sp.dma_start(w1[:, :], t["w1"][bass.ds(layer, 1)].rearrange("l p n -> (l p) n")).then_inc(fw, 16)
                sp.dma_start(w2[:, :, :], t["w2"][bass.ds(layer, 1)].rearrange("l p j n -> (l p) j n")).then_inc(fw, 16)
                sp.dma_start(fpar[:, :], t["fpar"][bass.ds(layer, 1)].rearrange("l p n -> (l p) n")).then_inc(fw, 16)

                sp.wait_ge(wo_ps, START + BL * layer + BL)
                attn_weights(layer + 1)
            sp.wait_ge(aw, START + AW * (DEPTH + 1))
            sp.wait_ge(fw, START + FW * DEPTH)

        @block.gpsimd
        def _(pool):
            memsets = ((kept[:, :], 1.0), (kept[:, BPS - 1:BPS], 0.0), (kr[:, :, 0:WIN], 0.0), (xa_pad[:, 0:WIN], 0.0),
                       (xa[0:DH, :, SEQ:SROW], 0.0), (xa[DH:P, :, SEQ + 1:SROW], 0.0), (xa[DH:P, :, 0:1], 0.0), (xb[DH:P, :, 0:1], 0.0))
            assert len(memsets) == MEMSETS
            for k, (view, value) in enumerate(memsets):
                nc.gpsimd.memset(view, value).then_inc(mem, 1)
                pool.wait_ge(mem, START + k + 1)
            pool.wait_ge(ln.out_ready, START + PRE)
            with pool.Fori(0, DEPTH) as layer:
                pool.wait_ge(xa_done, START + FL * layer)

                def step(q, n, late, iq, i, li):
                    if late is not None:
                        pool.wait_ge(sim_ps, START + late + 1)
                        keep = kept[:, bass.ds(li % BPS, 1)].broadcast_to([P, PAIRS * WIN]).rearrange("p (g j) -> p g j", g=PAIRS)
                        nc.gpsimd.tensor_tensor(kr[:, :, 0:WIN], kr[:, :, BLK:BLK + WIN], keep, ALU.mult).then_inc(ktail, 1)
                    def rotated(s, block):
                        pool.wait_ge(rot, START + 4 * block + 2 * s + 2)
                        nc.gpsimd.tensor_tensor((qr, ks)[s][:, :, :].rearrange("p g t -> p (g t)"), m[:, 2 * s, :],
                                                m[:, 2 * s + 1, :], ALU.add).then_inc(rope_add, 1)

                    if n is not None:
                        pool.wait_ge(kr_ready, START + n)
                        rotated(1, n)
                        pool.wait_ge(v_ps, START + 2 * n)
                        own_wait(pool, passed)
                        nc.gpsimd.tensor_copy(hs[:, :], xa_pad[:, bass.ds(col(i), WIN + BLK)]).then_inc(hs_ready, 1)
                    if q is not None:
                        pool.wait_ge(sim_ps, START + q)
                        rotated(0, q)

                pipelined(pool, layer, step)

        @block.tensor
        def _(pe):
            pe.wait_ge(consts, START + 48)
            pe.wait_ge(mask_ready, START + 2)
            pe.wait_ge(mem, START + MEMSETS)
            with pe.Fori(0, BATCH) as b:
                for c in range(2):
                    ln.tensor(pe, b * 2 + c, x[:, bass.ds(b * SEQ + c * CH, CH)], pa[:, 0, :], pa[:, 1, 0:4])
            pe.wait_ge(ln.out_ready, START + PRE)
            with pe.Fori(0, DEPTH) as layer:
                pe.wait_ge(aw, START + AW * layer + AW)
                pe.wait_ge(xa_done, START + FL * layer)

                def step(q, n, late, iq, i, li):
                    def project(k, banks, at):
                        src = xaf[:, bass.ds(col(at), BLK)]
                        for p in range(PAIRS):
                            ins = nc.tensor.matmul(pa[:, banks + p // 4, (p % 4) * BLK:(p % 4 + 1) * BLK], wqk[:, k, p * P:(p + 1) * P],
                                                   src, start=True, stop=True)
                        ins.then_inc(qk_ps, 1)

                    def values(first_window):
                        for w in range(first_window, first_window + 2):
                            for hp in range(2):
                                ins = nc.tensor.matmul(pw[hp * DH:(hp + 1) * DH, 2 + w % 2, :], hs[:, WIN * w:WIN * w + 2 * WIN], wv[:, hp, :],
                                                       start=True, stop=True, tile_position=(0, hp * DH))
                        ins.then_inc(v_ps, 1)

                    if n is not None:
                        project(1, 2, i)
                    if late is not None:
                        pe.wait_ge(hs_ready, START + late + 1)
                        pe.wait_ge(xb_done, START + late)
                        values(0)
                    if n is not None:
                        pe.wait_ge(sq_ready, START + 2 * n + 2)
                        pe.wait_ge(rot, START + 4 * n + 2)
                        for s in range(2):
                            for half in range(2):
                                qd = 2 * s + half
                                ins = nc.tensor.matmul(pa[WIN * qd:WIN * qd + WIN, 0, :], head_sum[:, :], sq[:, s, half * 512:(half + 1) * 512],
                                                       start=True, stop=True, tile_position=(0, WIN * qd))
                        ins.then_inc(norm_ps, 1)
                    if late is not None:
                        pe.wait_ge(v_ready, START + 2 * late + 1)
                        values(2)
                    if n is not None:
                        pe.wait_ge(nT_ready, START + n + 1)
                        for k in range(4):
                            ins = nc.tensor.transpose(pa[:, 1, k * P:(k + 1) * P], nT[:, k * P:(k + 1) * P], ident[:, :])
                        ins.then_inc(nT_ps, 1)
                    if late is not None:
                        pe.wait_ge(exp_ready, START + late + 1)
                        for p in range(PAIRS):
                            ins = nc.tensor.transpose(pw[:, p // 4, (p % 4) * BLK:(p % 4 + 1) * BLK],
                                                      probs[:, p, :, :].rearrange("t h j -> t (h j)"), ident[:, :])
                            if p % 4 == 3:
                                ins.then_inc(probsT_ps, 1)
                    if late is not None:
                        pe.wait_ge(v_ready, START + 2 * late + 2)
                        for p in range(PAIRS):
                            if p % 4 == 0:
                                pe.wait_ge(probsT_ready, START + 2 * late + p // 4 + 1)
                                own_wait(pe, passed)
                            for w in range(4):
                                for hp in range(2):
                                    part = slice(hp * DH, (hp + 1) * DH)
                                    ins = nc.tensor.matmul(pw[WIN * w:WIN * w + WIN, 2 + hp, p * DH:(p + 1) * DH],
                                                           probsT[part, p, WIN * w:WIN * w + WIN], v[part, w, p * DH:(p + 1) * DH],
                                                           start=True, stop=True, tile_position=(hp * DH, WIN * w))
                        ins.then_inc(pv_ps, 1)
                    if n is not None:
                        pe.wait_ge(rnorm_ready, START + n + 1)
                        for p in range(PAIRS):
                            ins = nc.tensor.matmul(pa[:, 2 + p // 4, (p % 4) * BLK:(p % 4 + 1) * BLK], rk_wide[:, p * P:(p + 1) * P],
                                                   ident[:, :], start=True, stop=True)
                        ins.then_inc(spread_ps, 1)
                    if late is not None:
                        pe.wait_ge(o_ready, START + 2 * late + 2)
                        for p in range(PAIRS):
                            ins = nc.tensor.transpose(pw[:, 2 + p // 4, (p % 4) * BLK:(p % 4 + 1) * BLK],
                                                      o[:, p, :, :].rearrange("t h e -> t (h e)"), ident[:, :])
                        ins.then_inc(oT_ps, 1)
                    if q is not None:
                        project(0, 0, iq)
                    if n is not None:
                        pe.wait_ge(rope_add, START + 2 * n + 1)
                        pe.wait_ge(kr_ready, START + n + 1)
                        for hp in range(2):
                            nc.tensor.matmul(pw[:, hp, :], ident16[:, :], bcast_mid(mask[:, :, :].rearrange("p c j -> p (c j)")
                                             [:, bass.ds((i % BPS) * 2 * WIN, 2 * WIN)], PAIRS), start=True, stop=False, skip_group_check=True)
                        for w in range(4):
                            for p in range(PAIRS):
                                for hp in range(2):
                                    part = slice(hp * DH, (hp + 1) * DH)
                                    ins = nc.tensor.matmul(pw[WIN * w:WIN * w + WIN, hp, p * 2 * WIN:(p + 1) * 2 * WIN],
                                                           qr[part, p, WIN * w:WIN * w + WIN], kr[part, p, WIN * w:WIN * w + 2 * WIN],
                                                           start=False, stop=True, skip_group_check=True, tile_position=(hp * DH, WIN * w))
                        ins.then_inc(sim_ps, 1)
                    if late is not None:
                        pe.wait_ge(oT_ready, START + late + 1)
                        for p in range(PAIRS):
                            ins = nc.tensor.matmul(pw[:, 2, 0:BLK], wo[:, p, :], oT[:, p, :], start=p == 0, stop=p == PAIRS - 1)
                        ins.then_inc(wo_ps, 1)

                pipelined(pe, layer, step)
                pe.wait_ge(xb_done, START + BL * layer + BL)
                pe.wait_ge(fw, START + FW * layer + FW)
                own_wait(pe, passed)
                with pe.Fori(0, BATCH) as b:
                    for c in range(2):
                        n = layer * FL + b * 2 + c
                        ln.tensor(pe, PRE + n, xbf[:, bass.ds(b * SROW + c * CH, CH)], pa[:, 0, :], pa[:, 1, 0:4])
                        pe.wait_ge(ln.out_ready, START + PRE + n + 1)
                        for j in range(NFB + 1):
                            if j < NFB:
                                if j >= 2:
                                    pe.wait_ge(hidden_ready, START + NFB * n + j - 1)
                                nc.tensor.matmul(pa[0:FB[j], 2 + j % 2, :], w1[:, j * P:j * P + FB[j]], h[:, :], start=True, stop=True)
                                nc.tensor.matmul(pw[0:FB[j], j % 2, :], w1[:, INNER + j * P:INNER + j * P + FB[j]], h[:, :],
                                                 start=True, stop=True).then_inc(ff_ps, 1)
                            if j > 0:
                                pe.wait_ge(hidden_ready, START + NFB * n + j)
                                ins = nc.tensor.matmul(pw[:, 2, :], w2[0:FB[j - 1], j - 1, :], act_out[0:FB[j - 1], j - 1, :],
                                                       start=j == 1, stop=j == NFB)
                        ins.then_inc(y_ps, 1)
                pe.wait_ge(xa_done, START + FL * layer + FL)

        @block.scalar
        def _(act):
            with act.Fori(0, BATCH) as b:
                act.wait_ge(mods_ready, START + b + 1)
                for c in range(2):
                    n = b * 2 + c
                    ln.scalar_squares(act, n)
                    at = b * SROW + c * CH
                    ln.scalar_out(act, n, [(slice(0, DH), xaf[0:DH, bass.ds(at, CH)]), (slice(DH, P), xaf[DH:P, bass.ds(at + 1, CH)])], mods[:, 0:1])
            with act.Fori(0, DEPTH) as layer:
                def step(q, n, late, iq, i, li):
                    def square(s, block):
                        if block is not None:
                            act.wait_ge(qk_ps, START + 2 * block + s + 1)
                            nc.scalar.activation(sq[:, s, :], pa[:, 2 * s:2 * s + 2, :].rearrange("p a t -> p (a t)"), ACT.Square).then_inc(sq_ready, 1)

                    def exponentials(hp, pairs):
                        if late is not None:
                            if pairs[0] == 0:
                                act.wait_ge(ebias_ready, START + 2 * late + hp + 1)
                            for p in pairs:
                                k = PAIRS * hp + p
                                ins = nc.scalar.activation(probs[:, p, hp, :], pw[:, hp, p * 2 * WIN:(p + 1) * 2 * WIN], ACT.Exp, bias=ebias[:, k:k + 1],
                                                           scale=rnorm[:, 2 * p + hp:2 * p + hp + 1], accum_out=total[:, k:k + 1])
                            if hp == 1 and pairs[-1] == PAIRS - 1:
                                ins.then_inc(exp_ready, 1)

                    def values_out(k):
                        if late is not None:
                            act.wait_ge(v_ps, START + 2 * late + k + 1)
                            nc.scalar.activation(v[:, 2 * k:2 * k + 2, :], pw[:, 2:4, :], ACT.Copy).then_inc(v_ready, 1)

                    def norms_out():
                        if n is not None:
                            act.wait_ge(norm_ps, START + n + 1)
                            nc.scalar.activation(nT[:, :], pa[:, 0, :], ACT.Copy).then_inc(nT_ready, 1)

                    exponentials(0, range(0, 5))
                    square(1, n)
                    exponentials(0, range(5, 8))
                    exponentials(1, range(0, 2))
                    values_out(0)
                    norms_out()
                    exponentials(1, range(2, 8))
                    values_out(1)
                    if late is not None:
                        for k in range(2):
                            act.wait_ge(probsT_ps, START + 2 * late + k + 1)
                            nc.scalar.activation(probsT[:, 4 * k:4 * k + 4, :].rearrange("p g t -> p (g t)"), pw[:, k, :], ACT.Copy)\
                                .then_inc(probsT_ready, 1)
                    if late is not None:
                        act.wait_ge(oT_ps, START + late + 1)
                        nc.scalar.activation(oT[:, :, :].rearrange("p g t -> p (g t)"), pw[:, 2:4, :].rearrange("p a t -> p (a t)"), ACT.Copy)\
                            .then_inc(oT_ready, 1)
                    square(0, q)

                pipelined(act, layer, step)
                act.wait_ge(fw, START + FW * layer + FW)
                with act.Fori(0, BATCH) as b:
                    for c in range(2):
                        n = layer * FL + b * 2 + c
                        ln.scalar_squares(act, PRE + n)
                        ln.scalar_out(act, PRE + n, [(slice(0, P), h[:, :])], fpar[:, 1:2])
                        for j in range(NFB):
                            act.wait_ge(ff_ps, START + NFB * n + j + 1)
                            if j >= 2:
                                act.wait_ge(hidden_ready, START + NFB * n + j - 1)
                            nc.scalar.activation(gelu[0:FB[j], j % 2, :], pw[0:FB[j], j % 2, :], ACT.Gelu,
                                                 bias=fpar[0:FB[j], 3 + NFB + j:4 + NFB + j]).then_inc(gelu_ready, 1)

        @block.vector
        def _(dve):
            dve.wait_ge(consts, START + 48)
            nc.vector.tensor_copy(mask[:, :, :].rearrange("p c j -> p (c j)"), mask32).then_inc(mask_ready, 1)
            nc.vector.tensor_copy(ident16[:, :], ident[:, :]).then_inc(mask_ready, 1)
            dve.wait_ge(mask_ready, START + 2)
            link = Links(dve, flinks)
            with dve.Fori(0, BATCH) as b:
                link.start(b)
                dve.wait_ge(ln.normed_ready, START + 2 * b)
                dve.wait_ge(ln.out_ready, START + 2 * b)
                for k in range(3):
                    ins = nc.vector.tensor_copy(mods[:, k:k + 1], const["mod"][:, bass.ds(b + (3 + k) * BATCH, 1)])
                link(ins)
                dve.sem_inc(mods_ready, 1)
                for c in range(2):
                    ln.vector(dve, b * 2 + c, x[:, bass.ds(b * SEQ + c * CH, CH)], pa[:, 0, :], pa[:, 1, 0:4], mods[:, 1:2])
            dve.wait_ge(ln.out_ready, START + PRE)
            with dve.Fori(0, DEPTH) as layer:
                dve.wait_ge(consts, START + 48)
                dve.wait_ge(aw, START + AW * layer + AW)
                for k in range(4):
                    ins = nc.vector.tensor_scalar(tab[:, k, :], base_tab[:, k, :], scales[:, k // 2:k // 2 + 1], None, ALU.mult)
                ins.then_inc(tabs_ready, 1)
                dve.wait_ge(tabs_ready, START + layer + 1)
                link, late_link = Links(dve, links), Links(dve, late_links)

                def step(q, n, late, iq, i, li):
                    if n is not None:
                        link.start(EARLY_LINKS * n)
                    if late is not None:
                        late_link.start(LATE_LINKS * late)

                    def table(k, at_block):
                        return bcast_mid(tab[:, k, bass.ds((at_block % BPS) * BLK, BLK)], PAIRS)

                    flat = lambda ap: ap.rearrange("p (g t) -> p g t", g=PAIRS)
                    projected = lambda s: flat(pa[:, 2 * s:2 * s + 2, :].rearrange("p a t -> p (a t)"))

                    def rotate_cos(s, block, at_block):
                        dve.wait_ge(sq_ready, START + 2 * block + s + 1)
                        nc.vector.tensor_tensor(flat(m[:, 2 * s, :]), projected(s), table(2 * s, at_block), ALU.mult).then_inc(rot, 1)

                    def rotate_sin(s, at_block, quadrants):
                        for a in quadrants:
                            at, to = (slice(HALF * k, HALF * k + HALF) for k in (a, a ^ 1))
                            ins = nc.vector.tensor_tensor(flat(m[to, 2 * s + 1, :]), projected(s)[at], table(2 * s + 1, at_block)[at], ALU.mult)
                        if a == 3:
                            ins.then_inc(rot, 1)

                    if n is not None:
                        rotate_cos(1, n, i)
                        rotate_sin(1, i, (0, 1, 2, 3))
                    if late is not None:
                        dve.wait_ge(exp_ready, START + late + 1)
                        late_link(nc.vector.reciprocal(recip[:, :], total[:, :]))
                    if n is not None:
                        dve.wait_ge(nT_ps, START + n + 1)
                        link(nc.vector.tensor_scalar(norm[:, :].rearrange("t (a k x) -> t k a x", a=4, k=4),
                                                     pa[:, 1, :].rearrange("t (k a y) -> t k a y", k=4, a=4)[:, :, :, 0:2], 1e-24, None, ALU.max))
                        newton_rsqrt(nc, link, rnorm[:, :], norm[:, :], ntmp[:, :])
                        nc.vector.tensor_copy(rk_wide[:, :].rearrange("p (a f) -> p a f", f=DH), bcast_last(rnorm[:, HEADS:], DH))\
                            .then_inc(rnorm_ready, 1)
                    if late is not None:
                        dve.wait_ge(pv_ps, START + late + 1)
                        for hp in range(2):
                            nc.vector.tensor_tensor(o[:, :, hp, :], pw[:, 2 + hp, :].rearrange("t (g e) -> t g e", g=PAIRS),
                                                    bcast_last(recip[:, PAIRS * hp:PAIRS * hp + PAIRS], DH), ALU.mult).then_inc(o_ready, 1)
                        assert late_link.n == LATE_LINKS
                    if n is not None:
                        dve.wait_ge(ktail, START + n)
                        dve.wait_ge(rope_add, START + 2 * n + 2)
                        dve.wait_ge(spread_ps, START + n + 1)
                        nc.vector.tensor_tensor(kr[:, :, WIN:WIN + BLK], ks[:, :, :],
                                                pa[:, 2:4, :].rearrange("p a t -> p (a t)").rearrange("p (g t) -> p g t", g=PAIRS), ALU.mult).then_inc(kr_ready, 1)
                    if q is not None:
                        rotate_cos(0, q, iq)
                        rotate_sin(0, iq, (0, 1))
                    if n is not None:
                        dve.wait_ge(sim_ps, START + n + 1)
                        for hp in range(2):
                            k = slice(PAIRS * hp, PAIRS * hp + PAIRS)
                            link(nc.vector.tensor_reduce(mx[:, k], pw[:, hp, :].rearrange("p (g j) -> p g j", g=PAIRS), AX.X, ALU.max))
                            nc.vector.scalar_tensor_tensor(ebias[:, k], mx[:, k], -1.0, rnorm[:, 0:HEADS].rearrange("p (g x) -> p x g", x=2)[:, hp, :],
                                                           ALU.mult, ALU.mult).then_inc(ebias_ready, 1)
                        assert link.n == EARLY_LINKS
                    if q is not None:
                        rotate_sin(0, iq, (2, 3))
                    if late is not None:
                        dve.wait_ge(wo_ps, START + late + 1)
                        c = col(li)
                        nc.vector.tensor_tensor(xbf[0:DH, bass.ds(c, BLK)], pw[0:DH, 2, 0:BLK], xaf[0:DH, bass.ds(c, BLK)], ALU.add)
                        nc.vector.tensor_tensor(xbf[DH:P, bass.ds(c + 1, BLK)], pw[DH:P, 2, 0:BLK], xaf[DH:P, bass.ds(c + 1, BLK)], ALU.add)\
                            .then_inc(xb_done, 1)

                pipelined(dve, layer, step)
                dve.wait_ge(xb_done, START + BL * layer + BL)
                dve.wait_ge(fw, START + FW * layer + FW)
                own_wait(dve, passed)
                with dve.Fori(0, BATCH) as b:
                    for c in range(2):
                        n = layer * FL + b * 2 + c
                        at = b * SROW + c * CH
                        ln.vector(dve, PRE + n, xbf[:, bass.ds(at, CH)], pa[:, 0, :], pa[:, 1, 0:4], fpar[:, 0:1])
                        dve.wait_ge(y_ps, START + n)
                        for j in range(NFB):
                            dve.wait_ge(gelu_ready, START + NFB * n + j + 1)
                            nc.vector.scalar_tensor_tensor(act_out[0:FB[j], j, :], pa[0:FB[j], 2 + j % 2, :], fpar[0:FB[j], 3 + j:4 + j],
                                                           gelu[0:FB[j], j % 2, :], ALU.add, ALU.mult).then_inc(hidden_ready, 1)
                        dve.wait_ge(y_ps, START + n + 1)
                        nc.vector.scalar_tensor_tensor(xaf[0:DH, bass.ds(at, CH)], pw[0:DH, 2, :], fpar[0:DH, 2:3], xbf[0:DH, bass.ds(at, CH)], ALU.add, ALU.add)
                        nc.vector.scalar_tensor_tensor(xaf[DH:P, bass.ds(at + 1, CH)], pw[DH:P, 2, :], fpar[DH:P, 2:3], xbf[DH:P, bass.ds(at + 1, CH)],
                                                       ALU.add, ALU.add).then_inc(xa_done, 1)
            dve.wait_ge(xa_done, START + FL * DEPTH)
            for b in range(BATCH):
                at = (3 + 2) * BATCH + b
                for lo, hi, shift in ((0, DH, 0), (DH, P, 1)):
                    nc.vector.scalar_tensor_tensor(x[lo:hi, b * SEQ:(b + 1) * SEQ], xa[lo:hi, b, shift:shift + SEQ], const["mod"][lo:hi, at:at + 1],
                                                   x[lo:hi, b * SEQ:(b + 1) * SEQ], ALU.mult, ALU.add)


def rwkv(nc, const, t):
    ctx = ExitStack()
    with ctx:
        sb = lambda s, sh, dt=F32: ctx.enter_context(nc.sbuf_tensor("wkv_" + s, sh, dt))
        sems, sem = semaphores(nc, ctx, "wkv_")
        ln = LayerNorm(nc, ctx, "wkv_ln", const, sem)
        x = const["x"]
        w = sb("w", [P, 4, P])
        decay = sb("decay", [P, 2])
        wdec = sb("wdec", [P, 1])
        ew = sb("ew", [P, 1])
        mods = sb("mods", [P, 3])
        h, k, v, sr = sb("h", [P, SEQ]), sb("k", [P, SEQ]), sb("v", [P, SEQ]), sb("sr", [P, SEQ])
        pp, aa, bb = sb("pp", [P, SEQ + 1]), sb("aa", [P, SEQ + 1]), sb("bb", [P, SEQ + 1])
        e1, e2, f1, f2, pm = (sb(n, [P, SEQ]) for n in ("e1", "e2", "f1", "f2", "pm"))
        e2v, num, den, f2v = (sb(n, [P, SEQ]) for n in ("e2v", "num", "den", "f2v"))
        ps = [ctx.enter_context(nc.psum_tensor(f"wkv_ps{i}", [P, 2 * CH], F32)) for i in range(3)]
        ps_ln = ctx.enter_context(nc.psum_tensor("wkv_ps_ln", [P, CH], F32))
        ps_small = ctx.enter_context(nc.psum_tensor("wkv_ps_small", [P, CH], F32))
        loaded, w_ready, mods_ready, init = sem("loaded"), sem("w_ready"), sem("mods_ready"), sem("init")
        proj_ps, proj_ready, arg_ready, exp_ready = sem("proj_ps"), sem("proj_ready"), sem("arg_ready"), sem("exp_ready")
        den_part, y_ready, out_ps, x_done, links, pool_links = sem("den_part"), sem("y_ready"), sem("out_ps"), sem("x_done"), sem("links"), sem("pool_links")
        block = ctx.enter_context(nc.Block())
        VL = 13

        @block.sync
        def _(sp):
            for s in sems:
                sp.sem_inc(s, START)
            sp.dma_start(w[:, :, :], t["wkv_w"]).then_inc(loaded, 16)
            sp.dma_start(decay[:, :], t["wkv_decay"]).then_inc(loaded, 16)
            sp.wait_ge(loaded, START + 32)

        @block.tensor
        def _(pe):
            pe.wait_ge(loaded, START + 32)
            with pe.Fori(0, BATCH) as b:
                for c in range(2):
                    ln.tensor(pe, b * 2 + c, x[:, bass.ds(b * SEQ + c * CH, CH)], ps_ln[:, :], ps_small[:, 0:4])
                pe.wait_ge(ln.out_ready, START + 2 * b + 2)
                pe.wait_ge(x_done, START + b)
                for i in (2, 1, 0):
                    for c in range(2):
                        ins = nc.tensor.matmul(ps[i][:, c * CH:(c + 1) * CH], w[:, i, :], h[:, c * CH:(c + 1) * CH], start=True, stop=True)
                    ins.then_inc(proj_ps, 1)
                pe.wait_ge(y_ready, START + b + 1)
                for c in range(2):
                    ins = nc.tensor.matmul(ps[0][:, c * CH:(c + 1) * CH], w[:, 3, :], num[:, c * CH:(c + 1) * CH], start=True, stop=True)
                ins.then_inc(out_ps, 1)

        @block.gpsimd
        def _(pool):
            nc.gpsimd.memset(pp[:, 0:1], -1e38)
            nc.gpsimd.memset(aa[:, 0:1], 0.0)
            nc.gpsimd.memset(bb[:, 0:1], 0.0).then_inc(init, 1)
            with pool.Fori(0, BATCH) as b:
                pool.wait_ge(proj_ready, START + 3 * b + 2)
                pool.wait_ge(exp_ready, START + 4 * b + 2)
                nc.gpsimd.tensor_tensor(e2v[:, :], e2[:, :], v[:, :], ALU.mult).then_inc(den_part, 1)
                pool.wait_ge(exp_ready, START + 4 * b + 4)
                nc.gpsimd.tensor_tensor(f2v[:, :], f2[:, :], v[:, :], ALU.mult).then_inc(den_part, 1)

        @block.scalar
        def _(act):
            act.wait_ge(loaded, START + 32)
            nc.scalar.activation(ew[:, :], decay[:, 0:1], ACT.Exp).then_inc(w_ready, 1)
            with act.Fori(0, BATCH) as b:
                act.wait_ge(mods_ready, START + b + 1)
                for c in range(2):
                    n = b * 2 + c
                    ln.scalar_squares(act, n)
                    ln.scalar_out(act, n, [(slice(0, P), h[:, c * CH:(c + 1) * CH])], mods[:, 0:1])
                act.wait_ge(proj_ps, START + 3 * b + 1)
                nc.scalar.activation(k[:, :], ps[2][:, :], ACT.Copy).then_inc(proj_ready, 1)
                act.wait_ge(proj_ps, START + 3 * b + 2)
                nc.scalar.activation(v[:, :], ps[1][:, :], ACT.Copy).then_inc(proj_ready, 1)
                act.wait_ge(proj_ps, START + 3 * b + 3)
                nc.scalar.activation(sr[:, :], ps[0][:, :], ACT.Tanh, scale=0.5).then_inc(proj_ready, 1)
                for i, buf in enumerate((e1, e2, f1, f2)):
                    act.wait_ge(arg_ready, START + 4 * b + i + 1)
                    nc.scalar.activation(buf[:, :], buf[:, :], ACT.Exp).then_inc(exp_ready, 1)

        @block.vector
        def _(dve):
            link = Links(dve, links)
            dve.wait_ge(w_ready, START + 1)
            link(nc.vector.tensor_scalar(wdec[:, :], ew[:, :], -1.0, None, ALU.mult))
            dve.wait_ge(init, START + 1)
            with dve.Fori(0, BATCH) as b:
                link.start(1 + b * VL)
                dve.wait_ge(ln.out_ready, START + 2 * b)
                dve.wait_ge(x_done, START + b)
                for i in range(3):
                    ins = nc.vector.tensor_copy(mods[:, i:i + 1], const["mod"][:, bass.ds(b + (6 + i) * BATCH, 1)])
                link(ins)
                dve.sem_inc(mods_ready, 1)
                for c in range(2):
                    ln.vector(dve, b * 2 + c, x[:, bass.ds(b * SEQ + c * CH, CH)], ps_ln[:, :], ps_small[:, 0:4], mods[:, 1:2])
                dve.wait_ge(proj_ready, START + 3 * b + 1)
                first, now, prev = decay[:, 1:2], slice(1, SEQ + 1), slice(0, SEQ)
                link(nc.vector.tensor_tensor_scan(pp[:, now], wdec[:, 0:1].broadcast_to([P, SEQ]), k[:, :], -1e38, ALU.add, ALU.max))
                nc.vector.scalar_tensor_tensor(e1[:, :], pp[:, prev], wdec[:, :], pp[:, now], ALU.add, ALU.subtract).then_inc(arg_ready, 1)
                nc.vector.tensor_tensor(e2[:, :], k[:, :], pp[:, now], ALU.subtract).then_inc(arg_ready, 1)
                link(nc.vector.scalar_tensor_tensor(pm[:, :], k[:, :], first, pp[:, prev], ALU.add, ALU.max))
                nc.vector.tensor_tensor(f1[:, :], pp[:, prev], pm[:, :], ALU.subtract).then_inc(arg_ready, 1)
                nc.vector.scalar_tensor_tensor(f2[:, :], k[:, :], first, pm[:, :], ALU.add, ALU.subtract).then_inc(arg_ready, 1)
                dve.wait_ge(exp_ready, START + 4 * b + 2)
                link(nc.vector.tensor_tensor_scan(bb[:, now], e1[:, :], e2[:, :], 0.0, ALU.mult, ALU.add))
                dve.wait_ge(den_part, START + 2 * b + 1)
                link(nc.vector.tensor_tensor_scan(aa[:, now], e1[:, :], e2v[:, :], 0.0, ALU.mult, ALU.add))
                dve.wait_ge(exp_ready, START + 4 * b + 4)
                link(nc.vector.tensor_tensor(den[:, :], f1[:, :], bb[:, prev], ALU.mult))
                link(nc.vector.tensor_tensor(den[:, :], den[:, :], f2[:, :], ALU.add))
                link(nc.vector.reciprocal(den[:, :], den[:, :]))
                link(nc.vector.tensor_tensor(num[:, :], f1[:, :], aa[:, prev], ALU.mult))
                dve.wait_ge(den_part, START + 2 * b + 2)
                link(nc.vector.tensor_tensor(num[:, :], num[:, :], f2v[:, :], ALU.add))
                link(nc.vector.tensor_tensor(num[:, :], num[:, :], den[:, :], ALU.mult))
                dve.wait_ge(proj_ready, START + 3 * b + 3)
                nc.vector.scalar_tensor_tensor(num[:, :], sr[:, :], 1.0, num[:, :], ALU.add, ALU.mult).then_inc(y_ready, 1)
                link(nc.vector.tensor_scalar(mods[:, 2:3], mods[:, 2:3], 0.5, None, ALU.mult))
                dve.wait_ge(out_ps, START + b + 1)
                cols = bass.ds(b * SEQ, SEQ)
                nc.vector.scalar_tensor_tensor(x[:, cols], ps[0][:, :], mods[:, 2:3], x[:, cols], ALU.mult, ALU.add).then_inc(x_done, 1)
                link(nc.vector.tensor_copy(pm[:, 0:1], mods[:, 2:3]))
                assert link.n == VL, link.n


def mixture(nc, const, t, out):
    ctx = ExitStack()
    with ctx:
        sb = lambda s, sh, dt=F32: ctx.enter_context(nc.sbuf_tensor("moe_" + s, sh, dt))
        sems, sem = semaphores(nc, ctx, "moe_")
        ln = LayerNorm(nc, ctx, "moe_ln", const, sem)
        x, ident = const["x"], const["ident"]
        gate_w, ew, eb, cw = sb("gate_w", [P, EXPERTS]), sb("expert_w", [P, EXPERTS, P]), sb("expert_b", [P, EXPERTS]), sb("combine_w", [P, P])
        mods = sb("mods", [P, 3])
        h = sb("h", [P, CH])
        logits = sb("logits", [P, 4, EXPERTS])
        one = sb("one", [P, 4])
        probs, top, gates = sb("probs", [P, 4, EXPERTS]), sb("top", [P, 4, 8]), sb("gates", [P, 4, EXPERTS])
        idx, idxf, iota = sb("idx", [P, 4, 8], U32), sb("idxf", [P, 4, 8]), sb("iota", [P, 4, EXPERTS])
        wide = sb("wide", [P, 2, 4, P])
        y, yg = sb("y", [P, 2, CH]), sb("yg", [P, 2, CH])
        pb = lambda n: ctx.enter_context(nc.psum_tensor("moe_ps_" + n, [P, CH], F32))
        ps_ln, ps_small, ps_c = pb("ln"), pb("small"), pb("c")
        ps_e, ps_g = [pb(f"e{i}") for i in range(2)], [pb(f"g{i}") for i in range(2)]
        loaded, mods_ready, logits_ps, centred, exp_ready, gates_ready = (sem(n) for n in ("loaded", "mods_ready", "logits_ps", "centred", "exp_ready", "gates_ready"))
        wide_ready, expert_ps, spread_ps, y_ready, yg_ready, c_ps, x_done, stored, links = (
            sem(n) for n in ("wide_ready", "expert_ps", "spread_ps", "y_ready", "yg_ready", "c_ps", "x_done", "stored", "links"))
        passed = sem("passed")
        block = ctx.enter_context(nc.Block())
        VL = 15

        @block.sync
        def _(sp):
            for s in sems:
                sp.sem_inc(s, START)
            for name, dst in (("gate_w", gate_w), ("expert_w", ew), ("expert_b", eb), ("combine_w", cw), ("iota", iota)):
                sp.dma_start(dst[:], t[name]).then_inc(loaded, 16)
            sp.wait_ge(loaded, START + 80)
            with sp.Fori(0, NCH) as n:
                sp.wait_ge(x_done, START + n + 1)
                sp.dma_start(out[:, bass.ds(n * CH, CH)], x[:, bass.ds(n * CH, CH)]).then_inc(stored, 16)
            sp.wait_ge(stored, START + 16 * NCH)

        @block.tensor
        def _(pe):
            pe.wait_ge(loaded, START + 80)
            with pe.Fori(0, NCH) as n:
                ln.tensor(pe, n, x[:, bass.ds(n * CH, CH)], ps_ln[:, :], ps_small[:, 0:4])
                pe.wait_ge(ln.out_ready, START + n + 1)
                for c in range(4):
                    ins = nc.tensor.matmul(ps_small[:, 64 + c * EXPERTS:64 + (c + 1) * EXPERTS], h[:, c * P:(c + 1) * P], gate_w[:, :], start=True, stop=True)
                ins.then_inc(logits_ps, 1)
                for e in range(EXPERTS + 1):
                    if e < EXPERTS:
                        if e >= 2:
                            pe.wait_ge(yg_ready, START + EXPERTS * n + e - 1)
                        nc.tensor.matmul(ps_e[e % 2][:, :], ew[:, e, :], h[:, :], start=True, stop=True).then_inc(expert_ps, 1)
                        pe.wait_ge(wide_ready, START + EXPERTS * n + e + 1)
                        for c in range(4):
                            ins = nc.tensor.matmul(ps_g[e % 2][:, c * P:(c + 1) * P], wide[:, e % 2, c, :], ident[:, :], start=True, stop=True)
                        ins.then_inc(spread_ps, 1)
                    if e > 0:
                        pe.wait_ge(yg_ready, START + EXPERTS * n + e)
                        ins = nc.tensor.matmul(ps_c[:, :], cw[:, :], yg[:, (e - 1) % 2, :], start=e == 1, stop=e == EXPERTS)
                ins.then_inc(c_ps, 1)

        @block.gpsimd
        def _(pool):
            with pool.Fori(0, NCH) as n:
                pool.wait_ge(gates_ready, START + n + 1)
                for e in range(EXPERTS):
                    if e >= 2:
                        pool.wait_ge(spread_ps, START + EXPERTS * n + e - 1)
                    own_wait(pool, passed)
                    nc.gpsimd.tensor_copy(wide[:, e % 2, :, :], bcast_last(gates[:, :, e], P)).then_inc(wide_ready, 1)

        @block.scalar
        def _(act):
            act.wait_ge(loaded, START + 80)
            with act.Fori(0, NCH) as n:
                ln.scalar_squares(act, n)
                act.wait_ge(mods_ready, START + n + 1)
                ln.scalar_out(act, n, [(slice(0, P), h[:, :])], mods[:, 0:1])
                act.wait_ge(centred, START + n + 1)
                nc.scalar.activation(probs[:, :, :], logits[:, :, :], ACT.Exp).then_inc(exp_ready, 1)
                for e in range(EXPERTS):
                    act.wait_ge(expert_ps, START + EXPERTS * n + e + 1)
                    if e >= 2:
                        act.wait_ge(yg_ready, START + EXPERTS * n + e - 1)
                    nc.scalar.activation(y[:, e % 2, :], ps_e[e % 2][:, :], ACT.Silu, bias=eb[:, e:e + 1]).then_inc(y_ready, 1)

        @block.vector
        def _(dve):
            dve.wait_ge(loaded, START + 80)
            link = Links(dve, links)
            with dve.Fori(0, NCH) as n:
                link.start(n * VL)
                dve.wait_ge(ln.out_ready, START + n)
                dve.wait_ge(x_done, START + n)
                for i in range(3):
                    ins = nc.vector.tensor_copy(mods[:, i:i + 1], const["mod"][:, bass.ds(n // 2 + (9 + i) * BATCH, 1)])
                link(ins)
                dve.sem_inc(mods_ready, 1)
                ln.vector(dve, n, x[:, bass.ds(n * CH, CH)], ps_ln[:, :], ps_small[:, 0:4], mods[:, 1:2])
                dve.wait_ge(logits_ps, START + n + 1)
                raw = ps_small[:, 64:64 + 4 * EXPERTS].rearrange("p (c e) -> p c e", c=4)
                link(nc.vector.tensor_reduce(one[:, :], raw, AX.X, ALU.max))
                nc.vector.tensor_tensor(logits[:, :, :], raw, bcast_last(one[:, :], EXPERTS), ALU.subtract).then_inc(centred, 1)
                dve.wait_ge(exp_ready, START + n + 1)
                link(nc.vector.tensor_reduce(one[:, :], probs[:, :, :], AX.X, ALU.add))
                link(nc.vector.reciprocal(one[:, :], one[:, :]))
                link(nc.vector.tensor_tensor(probs[:, :, :], probs[:, :, :], bcast_last(one[:, :], EXPERTS), ALU.mult))
                own_wait(dve, passed)
                for c in range(4):
                    link(nc.vector.max(top[:, c, :], probs[:, c, :]))
                    own_wait(dve, passed)
                for c in range(4):
                    ins = nc.vector.max_index(idx[:, c, :], top[:, c, :], probs[:, c, :])
                link(ins)
                link(nc.vector.tensor_copy(idxf[:, :, :], idx[:, :, :]))
                link(nc.vector.tensor_tensor(gates[:, :, :], iota[:, :, :], idxf[:, :, 0:1].broadcast_to([P, 4, EXPERTS]), ALU.is_equal))
                link(nc.vector.tensor_tensor(logits[:, :, :], iota[:, :, :], idxf[:, :, 1:2].broadcast_to([P, 4, EXPERTS]), ALU.is_equal))
                link(nc.vector.tensor_tensor(gates[:, :, :], gates[:, :, :], logits[:, :, :], ALU.add))
                link(nc.vector.tensor_tensor(gates[:, :, :], gates[:, :, :], probs[:, :, :], ALU.mult))
                dve.sem_inc(gates_ready, 1)
                for e in range(EXPERTS):
                    dve.wait_ge(y_ready, START + EXPERTS * n + e + 1)
                    dve.wait_ge(spread_ps, START + EXPERTS * n + e + 1)
                    nc.vector.tensor_tensor(yg[:, e % 2, :], y[:, e % 2, :], ps_g[e % 2][:, :], ALU.mult).then_inc(yg_ready, 1)
                dve.wait_ge(c_ps, START + n + 1)
                cols = bass.ds(n * CH, CH)
                nc.vector.scalar_tensor_tensor(x[:, cols], ps_c[:, :], mods[:, 2:3], x[:, cols], ALU.mult, ALU.add).then_inc(x_done, 1)
                assert link.n == VL, link.n


def kernel_program(nc, t, out, phases=5):
    ctx = ExitStack()
    with ctx:
        sb = lambda s, sh, dt=F32: ctx.enter_context(nc.sbuf_tensor(s, sh, dt))
        const = {
            "x": sb("x", [P, TOK]), "ident": sb("ident", [P, P]), "mean_w": sb("mean_w", [P, P]),
            "mod": sb("mod", [P, 2 * 6 * BATCH]),
        }
        prepare(nc, const, t)
        if phases >= 1:
            theta_attention(nc, const, t)
        if phases >= 2:
            local_layers(nc, const, t)
        if phases >= 3:
            rwkv(nc, const, t)
        if phases >= 4:
            mixture(nc, const, t, out)
        else:
            store(nc, const, out)


def store(nc, const, out):
    with ExitStack() as ctx:
        sems, sem = semaphores(nc, ctx, "store_")
        stored = sem("stored")
        block = ctx.enter_context(nc.Block())

        @block.sync
        def _(sp):
            for s in sems:
                sp.sem_inc(s, START)
            sp.dma_start(out, const["x"][:, :]).then_inc(stored, 16)
            sp.wait_ge(stored, START + 16)


def rotary_tables():
    half = np.arange(0, DH, 2, dtype=np.float32)
    inv_freq = (1.0 / np.float32(10000.0) ** (half / np.float32(DH))).astype(np.float32)
    pos = np.arange(SEQ, dtype=np.float32)
    freqs = (inv_freq[:, None] * pos[None, :]).astype(np.float32).astype(np.float64)
    base = ((half + np.float32(0.4 * DH)) / np.float32(1.4 * DH)).astype(np.float32).astype(np.float64)
    scale = base[:, None] ** ((pos[None, :] - SEQ // 2) / (WIN // 2)).astype(np.float64)
    tabs = [8 * np.cos(freqs) * scale, 8 * np.sin(freqs) * scale, np.cos(freqs) / scale, np.sin(freqs) / scale]
    both = [np.concatenate([x, -x if k % 2 else x], 0) for k, x in enumerate(tabs)]
    return np.ascontiguousarray(np.stack([np.tile(x, (2, 1)) for x in both], 1).astype(np.float32))


def band_mask():
    m = np.full((4, WIN, BPS, 2, WIN), MASKED, np.float32)
    i, j = np.arange(WIN)[:, None], np.arange(WIN)[None, :]
    m[:, :, :, 0, :] = np.where(j >= i, 0.0, MASKED)[None, :, None, :]
    m[:, :, :, 1, :] = np.where(j <= i, 0.0, MASKED)[None, :, None, :]
    m[0, :, 0, 0, :] = MASKED
    return m.reshape(P, BPS * 2 * WIN)


def lay_out(i):
    a = {k: np.asarray(v) for k, v in i.items()}
    c = np.ascontiguousarray
    o = {}
    o["xT"] = c(a["L0_attn_x"].reshape(TOK, P).T)
    o["cT"] = c(np.stack([a["L0_c"].T, a["L1_c"].T], 1))
    o["wmod"] = c(np.stack([a["L0_wmod"], a["L1_wmod"]], 1))
    o["ident"] = np.eye(P, dtype=np.float32)
    o["att_w"] = c(np.stack([a["L0_attn_" + n].T for n in ("Wq", "Wk", "Wv", "Wo")], 1))
    o["att_b"] = c(np.stack([a["L0_attn_" + n] for n in ("bq", "bk", "bv", "bo")], 1))
    o["wkv_w"] = c(np.stack([a["L1_attn_W_rvk"][k * P:(k + 1) * P].T for k in range(3)] + [a["L1_attn_W_out"].T], 1))
    o["wkv_decay"] = c(np.stack([a["L1_attn_time_decay"], a["L1_attn_time_first"]], 1))
    o["gate_w"], o["combine_w"] = c(a["L1_ffn_gate_w"].T), c(a["L1_ffn_combine_w"].T)
    o["expert_w"], o["expert_b"] = c(a["L1_ffn_expert_w"].transpose(2, 0, 1)), c(a["L1_ffn_expert_b"].T)
    o["iota"] = np.ascontiguousarray(np.broadcast_to(np.arange(EXPERTS, dtype=np.float32), (P, 4, EXPERTS)))
    o["tables"], o["mask"] = rotary_tables(), band_mask()
    o["head_sum"] = np.repeat(np.eye(2, WIN, dtype=np.float32), DH, 0)
    wqkv = a["L0_ffn_Wqkv"]
    pad = lambda w: c(np.concatenate([w, np.zeros_like(w[:1])], 0))
    o["wqk"] = pad(wqkv[:, :, :2 * HEADS * DH].reshape(DEPTH, P, 2, HEADS * DH))
    o["wv"] = pad(wqkv[:, :, 2 * HEADS * DH:].reshape(DEPTH, P, PAIRS, 2, DH).transpose(0, 1, 3, 2, 4).reshape(DEPTH, P, 2, PAIRS * DH))
    o["wo"] = pad(a["L0_ffn_Wo"].reshape(DEPTH, PAIRS, P, P).transpose(0, 2, 1, 3))
    o["scales"] = pad(np.tile(np.stack([a["L0_ffn_q_scale"], a["L0_ffn_k_scale"]], 2), (1, 2, 1)))
    o["w1"] = c(a["L0_ffn_W1"])
    pad_rows = lambda w: np.concatenate([w, np.zeros((DEPTH, NFB * P - INNER) + w.shape[2:], np.float32)], 1)
    o["w2"] = c(pad_rows(a["L0_ffn_W2"]).reshape(DEPTH, NFB, P, P).transpose(0, 2, 1, 3))
    b1 = [pad_rows(a["L0_ffn_b1"][:, k * INNER:(k + 1) * INNER]).reshape(DEPTH, NFB, P).transpose(0, 2, 1) for k in range(2)]
    o["fpar"] = c(np.concatenate([a["L0_ffn_ln_g"][:, :, None], a["L0_ffn_ln_b"][:, :, None], a["L0_ffn_b2"][:, :, None]] + b1, 2))
    return o


def kernel(**inputs):
    import concourse.bacc as _bacc
    from concourse.bass_utils import run_bass_kernel_spmd as _run

    nc = _bacc.Bacc("TRN2", target_bir_lowering=False, num_devices=1)
    arrays, t = {}, {}
    for name, a in lay_out(inputs).items():
        arrays[name + "_dram"] = a
        t[name] = nc.dram_tensor(name + "_dram", a.shape, mybir.dt.from_np(a.dtype), kind="ExternalInput").ap()
    out = nc.dram_tensor("out_dram", (P, TOK), F32, kind="ExternalOutput").ap()
    kernel_program(nc, t, out)
    r = _run(nc, [arrays], core_ids=[0])
    return np.ascontiguousarray(r.results[0]["out_dram"].T.reshape(BATCH, SEQ, P))
```

```python
from contextlib import ExitStack

import numpy as np

import concourse.bass as bass
from concourse import mybir

ALU = mybir.AluOpType
ACT = mybir.ActivationFunctionType
AX = mybir.AxisListType
F32 = mybir.dt.float32
BF16 = mybir.dt.bfloat16
I32 = mybir.dt.int32
U32 = mybir.dt.uint32

P = 128
BATCH = 4
SEQ = 1024
TOK = BATCH * SEQ
CH = 512
NCH = TOK // CH
DEPTH = 6
HEADS = 16
DH = 64
HALF = DH // 2
WIN = 32
PAIRS = HEADS // 2
BLK = 128
NBLK = TOK // BLK
BPS = SEQ // BLK
SROW = SEQ + 2
INNER = 341
NFB = -(-INNER // P)
FB = [min(P, INNER - P * j) for j in range(NFB)]
EXPERTS = 8
MASKED = -1.0e30
RSQRT_MAGIC = float(0x5F3759DF)
EPS = 1e-5
START = 1


def semaphores(nc, ctx, prefix):
    made = []

    def sem(name):
        made.append(ctx.enter_context(nc.semaphore(prefix + name)))
        return made[-1]

    return made, sem


class Links:

    def __init__(self, eng, sem):
        self.eng, self.sem, self.base, self.n = eng, sem, 0, 0

    def start(self, base):
        self.base, self.n = base, 0

    def __call__(self, ins):
        ins.then_inc(self.sem, 1)
        self.n += 1
        self.eng.wait_ge(self.sem, START + self.base + self.n)


def bcast_mid(ap, n):
    return ap.unsqueeze(1).broadcast_to([ap.shape[0], n, ap.shape[1]])


def bcast_last(ap, n):
    return ap.unsqueeze(len(ap.shape)).broadcast_to(list(ap.shape) + [n])


def newton_rsqrt(nc, link, y, v, a, last=None):
    link(nc.vector.tensor_scalar(y.bitcast(I32), v.bitcast(I32), -0.5, RSQRT_MAGIC, ALU.mult, ALU.add))
    for i in range(3):
        link(nc.vector.scalar_tensor_tensor(a, y, -0.5, v, ALU.mult, ALU.mult))
        link(nc.vector.tensor_tensor(a, a, y, ALU.mult))
        ins = nc.vector.scalar_tensor_tensor(y, a, 1.5, y, ALU.add, ALU.mult)
        if i < 2 or last is None:
            link(ins)
        else:
            ins.then_inc(last, 1)


def own_wait(eng, passed):
    eng.sem_inc(passed, 1)


LN_LINKS = 1 + 10


class LayerNorm:

    def __init__(self, nc, ctx, name, const, phase_sem):
        self.nc, self.const = nc, const
        sb = lambda s, sh: ctx.enter_context(nc.sbuf_tensor(f"{name}_{s}", sh, F32))
        sem = lambda s: phase_sem("ln_" + s)
        self.xc = sb("centred", [P, CH])
        self.sq = sb("squares", [P, CH])
        self.xn = sb("normed", [P, CH])
        self.var = sb("var", [P, 4])
        self.rstd = sb("rstd", [P, 4])
        self.tmp = sb("tmp", [P, 4])
        self.mean_ready, self.centred_ready, self.squares_ready = sem("mean_ready"), sem("centred_ready"), sem("squares_ready")
        self.var_ready, self.rstd_ready, self.spread_ready = sem("var_ready"), sem("rstd_ready"), sem("spread_ready")
        self.normed_ready, self.out_ready, self.links = sem("normed_ready"), sem("out_ready"), sem("links")

    def tensor(self, pe, n, src, wide, small):
        self.tensor_mean(pe, n, src, wide)
        self.tensor_var(pe, n, small)
        self.tensor_spread(pe, n, wide)

    def tensor_mean(self, pe, n, src, wide):
        nc, c = self.nc, self.const
        pe.wait_ge(self.normed_ready, START + n)
        nc.tensor.matmul(wide, c["mean_w"][:, :], src, start=True, stop=True).then_inc(self.mean_ready, 1)

    def tensor_var(self, pe, n, small):
        nc, c = self.nc, self.const
        pe.wait_ge(self.squares_ready, START + n + 1)
        for k in range(4):
            ins = nc.tensor.matmul(small[:, k:k + 1], self.sq[:, k * P:(k + 1) * P], c["mean_w"][:, 0:1], start=True, stop=True)
        ins.then_inc(self.var_ready, 1)

    def tensor_spread(self, pe, n, wide):
        nc, c = self.nc, self.const
        pe.wait_ge(self.rstd_ready, START + n + 1)
        for k in range(4):
            ins = nc.tensor.matmul(wide[:, k * P:(k + 1) * P], self.rstd[:, k:k + 1].broadcast_to([P, P]),
                                   c["ident"][:, :], start=True, stop=True)
        ins.then_inc(self.spread_ready, 1)

    def vector(self, dve, n, src, wide, small, gain):
        self.vector_centre(dve, n, src, wide)
        self.vector_rstd(dve, n, small)
        self.vector_normed(dve, n, wide, gain)

    def vector_centre(self, dve, n, src, wide):
        nc = self.nc
        dve.wait_ge(self.mean_ready, START + n + 1)
        nc.vector.tensor_tensor(self.xc[:, :], src, wide, ALU.subtract).then_inc(self.centred_ready, 1)

    def vector_rstd(self, dve, n, small):
        nc = self.nc
        link = Links(dve, self.links)
        link.start(n * LN_LINKS)
        dve.wait_ge(self.var_ready, START + n + 1)
        link(nc.vector.tensor_scalar(self.var[:, :], small, EPS, None, ALU.add))
        newton_rsqrt(nc, link, self.rstd[:, :], self.var[:, :], self.tmp[:, :])
        dve.sem_inc(self.rstd_ready, 1)

    def vector_normed(self, dve, n, wide, gain):
        nc = self.nc
        dve.wait_ge(self.spread_ready, START + n + 1)
        dve.wait_ge(self.out_ready, START + n)
        nc.vector.scalar_tensor_tensor(self.xn[:, :], self.xc[:, :], gain, wide, ALU.mult, ALU.mult).then_inc(self.normed_ready, 1)

    def scalar_squares(self, act, n):
        act.wait_ge(self.centred_ready, START + n + 1)
        self.nc.scalar.activation(self.sq[:, :], self.xc[:, :], ACT.Square).then_inc(self.squares_ready, 1)

    def vector_squares(self, dve, n):
        dve.wait_ge(self.centred_ready, START + n + 1)
        self.nc.vector.tensor_tensor(self.sq[:, :], self.xc[:, :], self.xc[:, :], ALU.mult).then_inc(self.squares_ready, 1)

    def pool_squares(self, pool, n):
        pool.wait_ge(self.centred_ready, START + n + 1)
        self.nc.gpsimd.tensor_tensor(self.sq[:, :], self.xc[:, :], self.xc[:, :], ALU.mult).then_inc(self.squares_ready, 1)

    def scalar_out(self, act, n, dsts, bias):
        act.wait_ge(self.normed_ready, START + n + 1)
        for ps, dst in dsts:
            ins = self.nc.scalar.activation(dst, self.xn[ps, :], ACT.Identity, bias=bias[ps, :])
        ins.then_inc(self.out_ready, 1)


def prepare(nc, const, t):
    ctx = ExitStack()
    with ctx:
        sb = lambda s, sh, dt=F32: ctx.enter_context(nc.sbuf_tensor("prep_" + s, sh, dt))
        sems, sem = semaphores(nc, ctx, "prep_")
        cT = sb("cT", [P, 2, BATCH])
        silu = sb("silu", [P, 2, BATCH])
        wmod = sb("wmod", [P, 2, 6 * P])
        neg = sb("neg", [P, 2, 2, BATCH])
        sign = sb("sign", [P, 2, 2, BATCH])
        ps = ctx.enter_context(nc.psum_tensor("prep_ps", [P, 512], F32))
        loaded, silu_ready, mod_ready, links, ones = sem("loaded"), sem("silu_ready"), sem("mod_ready"), sem("links"), sem("ones")
        block = ctx.enter_context(nc.Block())
        mod = const["mod"]

        @block.sync
        def _(sp):
            for s in sems:
                sp.sem_inc(s, START)
            sp.dma_start(const["x"][:, :], t["xT"]).then_inc(loaded, 16)
            sp.dma_start(cT[:, :, :], t["cT"]).then_inc(loaded, 16)
            sp.dma_start(wmod[:, :, :], t["wmod"]).then_inc(loaded, 16)
            sp.dma_start(const["ident"][:, :], t["ident"]).then_inc(loaded, 16)
            sp.wait_ge(loaded, START + 64)

        @block.gpsimd
        def _(pool):
            nc.gpsimd.memset(const["mean_w"][:, :], 1.0 / P).then_inc(ones, 1)

        @block.scalar
        def _(act):
            act.wait_ge(loaded, START + 64)
            nc.scalar.activation(silu[:, :, :], cT[:, :, :], ACT.Silu).then_inc(silu_ready, 1)

        @block.tensor
        def _(pe):
            pe.wait_ge(silu_ready, START + 1)
            for b in range(2):
                for j in range(6):
                    ins = nc.tensor.matmul(ps[:, (b * 6 + j) * BATCH:(b * 6 + j + 1) * BATCH], wmod[:, b, j * P:(j + 1) * P],
                                           silu[:, b, :], start=True, stop=True)
            ins.then_inc(mod_ready, 1)

        @block.vector
        def _(dve):
            link = Links(dve, links)
            dve.wait_ge(mod_ready, START + 1)
            psm = ps[:, 0:48].rearrange("p (b j n) -> p b j n", b=2, j=6)
            link(nc.vector.tensor_copy(mod[:, :], ps[:, 0:48]))
            m = mod[:, :].rearrange("p (b k j n) -> p b k j n", b=2, k=2, j=3)
            for b in range(2):
                link(nc.vector.tensor_scalar(m[:, b, :, 1, :], m[:, b, :, 1, :], 1.0, None, ALU.add))
                gate = m[:, b, :, 2, :]
                link(nc.vector.tensor_scalar(neg[:, b, :, :], gate, -1.0, None, ALU.mult))
                link(nc.vector.tensor_scalar(sign[:, b, :, :], gate, 0.0, 2.0, ALU.is_ge, ALU.mult))
                link(nc.vector.tensor_tensor(gate, gate, neg[:, b, :, :], ALU.max))
                link(nc.vector.tensor_scalar(gate, gate, 0.25, None, ALU.max))
                link(nc.vector.scalar_tensor_tensor(gate, sign[:, b, :, :], -1.0, gate, ALU.add, ALU.mult))


def modcol(const, block, which, b):
    at = (block * 6 + which) * BATCH + b
    return const["mod"][:, at:at + 1]


def theta_attention(nc, const, t):
    ctx = ExitStack()
    with ctx:
        sb = lambda s, sh, dt=F32: ctx.enter_context(nc.sbuf_tensor("att_" + s, sh, dt))
        pb = lambda s, sh: ctx.enter_context(nc.psum_tensor("att_ps_" + s, sh, F32))
        sems, sem = semaphores(nc, ctx, "att_")
        ln = LayerNorm(nc, ctx, "att_ln", const, sem)
        x = const["x"]
        w = sb("w", [P, 4, P])
        bias = sb("bias", [P, 4])
        out_bias = sb("out_bias", [P, 1])
        mods = sb("mods", [P, 3])
        gated_bias = sb("gated_bias", [P, 1])
        h = sb("h", [P, SEQ])
        q, k, v = sb("q", [P, SEQ]), sb("k", [P, SEQ]), sb("v", [P, SEQ])
        t1, t2, theta = sb("t1", [P, SEQ]), sb("t2", [P, SEQ]), sb("theta", [P, SEQ])
        probs, probsT = sb("probs", [P, SEQ]), sb("probsT", [P, SEQ])
        mx, shift, total, recip = sb("mx", [P, 1]), sb("shift", [P, 1]), sb("total", [P, 1]), sb("recip", [P, 1])
        spread, oT, upd = sb("spread", [P, P]), sb("oT", [P, P]), sb("upd", [P, P])
        ps_s = pb("scores", [P, SEQ])
        ps_t = pb("probsT", [P, SEQ])
        ps_ln, ps_small, ps_o, ps_y = pb("ln", [P, CH]), pb("small", [P, CH]), pb("o", [P, CH]), pb("y", [P, CH])
        loaded, bias_ps, bias_ready, mods_ready = sem("loaded"), sem("bias_ps"), sem("bias_ready"), sem("mods_ready")
        proj_ps, proj_ready, scores_ps, tanh_ready = sem("proj_ps"), sem("proj_ready"), sem("scores_ps"), sem("tanh_ready")
        theta_ready, probs_ready, probsT_ps = sem("theta_ready"), sem("probs_ready"), sem("probsT_ps")
        probsT_a, probsT_d = sem("probsT_act"), sem("probsT_dve")
        recip_ready, pv_ps, o_ready, y_ps, x_done = sem("recip_ready"), sem("pv_ps"), sem("o_ready"), sem("y_ps"), sem("x_done")
        links, setup_links, scores_used = sem("links"), sem("setup_links"), sem("scores_used")
        block = ctx.enter_context(nc.Block())
        NS = SEQ // P
        VL = 1 + 5 * NS

        @block.sync
        def _(sp):
            for s in sems:
                sp.sem_inc(s, START)
            sp.dma_start(w[:, :, :], t["att_w"]).then_inc(loaded, 16)
            sp.dma_start(bias[:, :], t["att_b"]).then_inc(loaded, 16)
            sp.wait_ge(loaded, START + 32)

        @block.tensor
        def _(pe):
            pe.wait_ge(loaded, START + 32)
            nc.tensor.matmul(ps_y[:, 0:1], w[:, 3, :], bias[:, 2:3], start=True, stop=True).then_inc(bias_ps, 1)
            pe.wait_ge(bias_ready, START + 1)
            with pe.Fori(0, BATCH) as b:
                for c in range(2):
                    ln.tensor(pe, b * 2 + c, x[:, bass.ds(b * SEQ + c * CH, CH)], ps_ln[:, :], ps_small[:, 0:4])
                pe.wait_ge(ln.out_ready, START + 2 * b + 2)
                for i, dst in ((0, ps_s), (1, ps_t)):
                    for c in range(2):
                        ins = nc.tensor.matmul(dst[:, c * CH:(c + 1) * CH], w[:, i, :], h[:, c * CH:(c + 1) * CH], start=True, stop=True)
                    ins.then_inc(proj_ps, 1)
                pe.wait_ge(proj_ready, START + 3 * b + 1)
                for j in range(NS):
                    ins = nc.tensor.matmul(ps_s[:, j * P:(j + 1) * P], h[:, j * P:(j + 1) * P], w[:, 2, :], start=True, stop=True)
                ins.then_inc(proj_ps, 1)
                pe.wait_ge(proj_ready, START + 3 * b + 3)
                for j in range(NS + 2):
                    n = b * NS + j
                    if j < NS:
                        pe.wait_ge(scores_used, START + n)
                        for c in range(2):
                            ins = nc.tensor.matmul(ps_s[:, c * CH:(c + 1) * CH], q[:, j * P:(j + 1) * P], k[:, c * CH:(c + 1) * CH], start=True, stop=True)
                        ins.then_inc(scores_ps, 1)
                    if j >= 2:
                        pe.wait_ge(o_ready, START + n - 1)
                        nc.tensor.matmul(ps_y[:, 0:P], w[:, 3, :], oT[:, :], start=True, stop=True).then_inc(y_ps, 1)
                    if 1 <= j <= NS:
                        pe.wait_ge(probs_ready, START + n)
                        for c in range(8):
                            ins = nc.tensor.transpose(ps_t[:, c * P:(c + 1) * P], probs[:, c * P:(c + 1) * P], const["ident"][:, :])
                        ins.then_inc(probsT_ps, 1)
                        pe.wait_ge(recip_ready, START + n)
                        nc.tensor.matmul(ps_o[:, P:2 * P], recip[:, 0:1].broadcast_to([P, P]), const["ident"][:, :], start=True, stop=True)
                        pe.wait_ge(probsT_a, START + n)
                        pe.wait_ge(probsT_d, START + n)
                        for c in range(8):
                            ins = nc.tensor.matmul(ps_o[:, 0:P], v[:, c * P:(c + 1) * P], probsT[:, c * P:(c + 1) * P], start=c == 0, stop=c == 7)
                        ins.then_inc(pv_ps, 1)
                pe.wait_ge(x_done, START + NS * b + NS)

        @block.scalar
        def _(act):
            act.wait_ge(loaded, START + 32)
            with act.Fori(0, BATCH) as b:
                act.wait_ge(mods_ready, START + b + 1)
                for c in range(2):
                    n = b * 2 + c
                    ln.scalar_squares(act, n)
                    ln.scalar_out(act, n, [(slice(0, P), h[:, c * CH:(c + 1) * CH])], mods[:, 0:1])
                act.wait_ge(proj_ps, START + 3 * b + 1)
                nc.scalar.activation(q[:, :], ps_s[:, :], ACT.Identity, bias=bias[:, 0:1]).then_inc(proj_ready, 1)
                act.wait_ge(proj_ps, START + 3 * b + 2)
                nc.scalar.activation(k[:, :], ps_t[:, :], ACT.Identity, bias=bias[:, 1:2]).then_inc(proj_ready, 1)
                act.wait_ge(proj_ps, START + 3 * b + 3)
                nc.scalar.activation(v[:, :], ps_s[:, :], ACT.Copy).then_inc(proj_ready, 1)
                for j in range(NS + 1):
                    n = b * NS + j
                    if j < NS:
                        act.wait_ge(scores_ps, START + n + 1)
                        for c in range(2):
                            cols = slice(c * CH, (c + 1) * CH)
                            nc.scalar.activation(t1[:, cols], ps_s[:, cols], ACT.Tanh, scale=0.5)
                            nc.scalar.activation(t2[:, cols], ps_s[:, cols], ACT.Tanh).then_inc(tanh_ready, 1)
                    if j >= 1:
                        act.wait_ge(probsT_ps, START + n)
                        nc.scalar.activation(probsT[:, 0:CH], ps_t[:, 0:CH], ACT.Copy).then_inc(probsT_a, 1)
                    if j < NS:
                        act.wait_ge(theta_ready, START + n + 1)
                        nc.scalar.activation(probs[:, :], theta[:, :], ACT.Exp, bias=shift[:, :], scale=0.15, accum_out=total[:, :]).then_inc(probs_ready, 1)

        @block.vector
        def _(dve):
            link = Links(dve, setup_links)
            dve.wait_ge(loaded, START + 32)
            dve.wait_ge(bias_ps, START + 1)
            link(nc.vector.tensor_tensor(out_bias[:, :], ps_y[:, 0:1], bias[:, 3:4], ALU.add))
            dve.sem_inc(bias_ready, 1)
            link = Links(dve, links)
            with dve.Fori(0, BATCH) as b:
                link.start(b * VL)
                for i in range(3):
                    ins = nc.vector.tensor_copy(mods[:, i:i + 1], const["mod"][:, bass.ds(b + i * BATCH, 1)])
                link(ins)
                dve.sem_inc(mods_ready, 1)
                nc.vector.tensor_tensor(gated_bias[:, :], mods[:, 2:3], out_bias[:, :], ALU.mult)
                for c in range(2):
                    ln.vector(dve, b * 2 + c, x[:, bass.ds(b * SEQ + c * CH, CH)], ps_ln[:, :], ps_small[:, 0:4], mods[:, 1:2])
                for j in range(NS + 2):
                    n = b * NS + j
                    if j < NS:
                        for c in range(2):
                            cols = slice(c * CH, (c + 1) * CH)
                            dve.wait_ge(tanh_ready, START + 2 * n + c + 1)
                            ins = nc.vector.scalar_tensor_tensor(theta[:, cols], ps_s[:, cols], 0.0, t1[:, cols], ALU.max, ALU.add)
                        link(ins)
                        dve.sem_inc(scores_used, 1)
                    if 1 <= j <= NS:
                        dve.wait_ge(probsT_ps, START + n)
                        nc.vector.tensor_copy(probsT[:, CH:], ps_t[:, CH:]).then_inc(probsT_d, 1)
                    if j < NS:
                        link(nc.vector.scalar_tensor_tensor(theta[:, :], theta[:, :], 2.0 / 3.0, t2[:, :], ALU.mult, ALU.add))
                        link(nc.vector.tensor_reduce(mx[:, :], theta[:, :], AX.X, ALU.max))
                        nc.vector.tensor_scalar(shift[:, :], mx[:, :], -0.15, None, ALU.mult).then_inc(theta_ready, 1)
                    if j >= 2:
                        dve.wait_ge(y_ps, START + n - 1)
                        link(nc.vector.tensor_scalar(upd[:, :], ps_y[:, 0:P], mods[:, 2:3], gated_bias[:, 0:1], ALU.mult, ALU.add))
                        cols = bass.ds(b * SEQ + (j - 2) * P, P)
                        nc.vector.tensor_tensor(x[:, cols], x[:, cols], upd[:, :], ALU.add).then_inc(x_done, 1)
                    if 1 <= j <= NS:
                        dve.wait_ge(pv_ps, START + n)
                        link(nc.vector.tensor_copy(spread[:, :], ps_o[:, P:2 * P]))
                        nc.vector.tensor_tensor(oT[:, :], ps_o[:, 0:P], spread[:, :], ALU.mult).then_inc(o_ready, 1)
                    if j < NS:
                        dve.wait_ge(probs_ready, START + n + 1)
                        nc.vector.reciprocal(recip[:, :], total[:, :]).then_inc(recip_ready, 1)
                assert link.n == VL, link.n

def local_layers(nc, const, t):
    ctx = ExitStack()
    with ctx:
        sb = lambda s, sh, dt=F32: ctx.enter_context(nc.sbuf_tensor("loc_" + s, sh, dt))
        sems, sem = semaphores(nc, ctx, "loc_")
        ln = LayerNorm(nc, ctx, "loc_ln", const, sem)
        x, ident = const["x"], const["ident"]
        xa_pad, xb = sb("xa", [P, WIN + BATCH * SROW]), sb("xb", [P, BATCH, SROW])
        xaf, xbf = xa_pad[:, WIN:], xb[:, :, :].rearrange("p b s -> p (b s)")
        xa = xaf.rearrange("p (b s) -> p b s", b=BATCH)
        base_tab, tab = sb("base_tab", [P, 4, SEQ]), sb("tab", [P, 4, SEQ])
        ident16, mask = sb("ident16", [P, P], BF16), sb("mask", [P, BPS, 2 * WIN], BF16)
        head_sum = sb("head_sum", [P, WIN])
        wqk, wv, wo = sb("wqk", [P, 2, PAIRS * P]), sb("wv", [P, 2, PAIRS * DH]), sb("wo", [P, PAIRS, P])
        scales = sb("scales", [P, 2])
        kept = sb("kept", [P, BPS])
        w1, w2, fpar = sb("w1", [P, 2 * INNER]), sb("w2", [P, NFB, P]), sb("fpar", [P, 3 + 2 * NFB])
        mods = sb("mods", [P, 3])
        hs = sb("hs", [P, WIN + BLK])
        sq = sb("sq", [P, 2, PAIRS * BLK])
        m = sb("m", [P, 4, PAIRS * BLK])
        mask32 = m[:, 0, 0:BPS * 2 * WIN]
        act_out = m[:, :, :].rearrange("p a t -> p (a t)").rearrange("p (j t) -> p j t", t=CH)
        qr, ks = sb("qr", [P, PAIRS, BLK]), sb("ks", [P, PAIRS, BLK])
        kr = sb("kr", [P, PAIRS, WIN + BLK])
        nT = sb("nT", [P, 4 * BLK])
        norm, rnorm, ntmp = sb("norm", [P, 2 * HEADS]), sb("rnorm", [P, 2 * HEADS]), sb("ntmp", [P, 2 * HEADS])
        rk_wide = sb("rk_wide", [P, HEADS * DH])
        mx, ebias, total, recip = sb("mx", [P, HEADS]), sb("ebias", [P, HEADS]), sb("total", [P, HEADS]), sb("recip", [P, HEADS])
        probs = sb("probs", [P, PAIRS, 2, 2 * WIN])
        probsT = sb("probsT", [P, PAIRS, BLK])
        v = sb("v", [P, 4, PAIRS * DH])
        o, oT = sb("o", [P, PAIRS, 2, DH]), sb("oT", [P, PAIRS, BLK])
        h, gelu = sb("h", [P, CH]), sb("gelu", [P, 2, CH])
        pa = ctx.enter_context(nc.psum_tensor("loc_pa", [P, 4, 512], F32))
        pw = ctx.enter_context(nc.psum_tensor("loc_pw", [P, 4, 512], F32))

        mask_ready = sem("mask_ready")
        consts, mem, tabs_ready = sem("consts"), sem("mem"), sem("tabs_ready")
        mods_ready, ln_in_done = sem("mods_ready"), sem("ln_in_done")
        aw, fw = sem("attn_weights"), sem("ffn_weights")
        hs_ready, qk_ps, sq_ready, rot, rope_add = sem("hs_ready"), sem("qk_ps"), sem("sq_ready"), sem("rot"), sem("rope_add")
        v_ps, v_ready, norm_ps, nT_ready, nT_ps = sem("v_ps"), sem("v_ready"), sem("norm_ps"), sem("nT_ready"), sem("nT_ps")
        rnorm_ready, spread_ps, kr_ready, ktail = sem("rnorm_ready"), sem("spread_ps"), sem("kr_ready"), sem("ktail")
        sim_ps, ebias_ready, exp_ready, probsT_ps = sem("sim_ps"), sem("ebias_ready"), sem("exp_ready"), sem("probsT_ps")
        probsT_ready, pv_ps, o_ready = sem("probsT_ready"), sem("pv_ps"), sem("o_ready")
        oT_ps, oT_ready, wo_ps, xb_done = sem("oT_ps"), sem("oT_ready"), sem("wo_ps"), sem("xb_done")
        ff_ps, gelu_ready, hidden_ready, y_ps, xa_done = sem("ff_ps"), sem("gelu_ready"), sem("hidden_ready"), sem("y_ps"), sem("xa_done")
        links, late_links, flinks, passed = sem("links"), sem("late_links"), sem("flinks"), sem("passed")
        block = ctx.enter_context(nc.Block())

        BL = NBLK
        FL = NCH
        PRE = NCH
        EARLY_LINKS, LATE_LINKS = 1 + 10 + 2, 1
        AW, FW = 16 * 4, 16 * 3
        MEMSETS = 8

        def pipelined(eng, layer, step):
            first = layer * BL
            step(first, None, None, 0, None, None)
            step(first + 1, first, None, 1, 0, None)
            with eng.Fori(1, BL - 1) as i:
                step(first + i + 1, first + i, first + i - 1, i + 1, i, i - 1)
            step(None, first + BL - 1, first + BL - 2, None, BL - 1, BL - 2)
            step(None, None, first + BL - 1, None, None, BL - 1)

        def chunks(eng, layer, step):
            first = layer * FL
            step(first, None, 0, None)
            with eng.Fori(1, FL) as i:
                step(first + i, first + i - 1, i, i - 1)
            step(None, first + FL - 1, None, FL - 1)

        def chunk_col(i):
            return i * CH + (i // (SEQ // CH)) * (SROW - SEQ)

        def col(i):
            return i * BLK + (i // BPS) * (SROW - SEQ)

        @block.sync
        def _(sp):
            for s in sems:
                sp.sem_inc(s, START)
            for name, dst in (("tables", base_tab), ("mask", mask32), ("head_sum", head_sum)):
                sp.dma_start(dst if name == "mask" else dst[:], t[name]).then_inc(consts, 16)

            def attn_weights(layer):
                sp.dma_start(wqk[:, :, :], t["wqk"][bass.ds(layer, 1)].rearrange("l p a n -> (l p) a n")).then_inc(aw, 16)
                sp.dma_start(wv[:, :, :], t["wv"][bass.ds(layer, 1)].rearrange("l p a n -> (l p) a n")).then_inc(aw, 16)
                sp.dma_start(wo[:, :, :], t["wo"][bass.ds(layer, 1)].rearrange("l p a n -> (l p) a n")).then_inc(aw, 16)
                sp.dma_start(scales[:, :], t["scales"][bass.ds(layer, 1)].rearrange("l p n -> (l p) n")).then_inc(aw, 16)

            attn_weights(0)
            sp.wait_ge(mem, START + MEMSETS)
            with sp.Fori(0, DEPTH) as layer:
                sp.wait_ge(xa_done, START + FL * layer)
                sp.dma_start(w1[:, :], t["w1"][bass.ds(layer, 1)].rearrange("l p n -> (l p) n")).then_inc(fw, 16)
                sp.dma_start(w2[:, :, :], t["w2"][bass.ds(layer, 1)].rearrange("l p j n -> (l p) j n")).then_inc(fw, 16)
                sp.dma_start(fpar[:, :], t["fpar"][bass.ds(layer, 1)].rearrange("l p n -> (l p) n")).then_inc(fw, 16)

                sp.wait_ge(wo_ps, START + BL * layer + BL)
                attn_weights(layer + 1)
            sp.wait_ge(aw, START + AW * (DEPTH + 1))
            sp.wait_ge(fw, START + FW * DEPTH)

        @block.gpsimd
        def _(pool):
            memsets = ((kept[:, :], 1.0), (kept[:, BPS - 1:BPS], 0.0), (kr[:, :, 0:WIN], 0.0), (xa_pad[:, 0:WIN], 0.0),
                       (xa[0:DH, :, SEQ:SROW], 0.0), (xa[DH:P, :, SEQ + 1:SROW], 0.0), (xa[DH:P, :, 0:1], 0.0), (xb[DH:P, :, 0:1], 0.0))
            assert len(memsets) == MEMSETS
            for k, (view, value) in enumerate(memsets):
                nc.gpsimd.memset(view, value).then_inc(mem, 1)
                pool.wait_ge(mem, START + k + 1)
            pool.wait_ge(ln.out_ready, START + PRE)
            with pool.Fori(0, DEPTH) as layer:
                pool.wait_ge(xa_done, START + FL * layer)

                def step(q, n, late, iq, i, li):
                    if late is not None:
                        pool.wait_ge(sim_ps, START + late + 1)
                        keep = kept[:, bass.ds(li % BPS, 1)].broadcast_to([P, PAIRS * WIN]).rearrange("p (g j) -> p g j", g=PAIRS)
                        nc.gpsimd.tensor_tensor(kr[:, :, 0:WIN], kr[:, :, BLK:BLK + WIN], keep, ALU.mult).then_inc(ktail, 1)
                    def rotated(s, block):
                        pool.wait_ge(rot, START + 4 * block + 2 * s + 2)
                        nc.gpsimd.tensor_tensor((qr, ks)[s][:, :, :].rearrange("p g t -> p (g t)"), m[:, 2 * s, :],
                                                m[:, 2 * s + 1, :], ALU.add).then_inc(rope_add, 1)

                    if n is not None:
                        pool.wait_ge(kr_ready, START + n)
                        rotated(1, n)
                        pool.wait_ge(v_ps, START + 2 * n)
                        own_wait(pool, passed)
                        nc.gpsimd.tensor_copy(hs[:, :], xa_pad[:, bass.ds(col(i), WIN + BLK)]).then_inc(hs_ready, 1)
                    if q is not None:
                        pool.wait_ge(sim_ps, START + q)
                        rotated(0, q)

                pipelined(pool, layer, step)
                with pool.Fori(0, FL) as i:
                    ln.pool_squares(pool, PRE + layer * FL + i)

        @block.tensor
        def _(pe):
            pe.wait_ge(consts, START + 48)
            pe.wait_ge(mask_ready, START + 2)
            pe.wait_ge(mem, START + MEMSETS)
            with pe.Fori(0, BATCH) as b:
                for c in range(2):
                    ln.tensor(pe, b * 2 + c, x[:, bass.ds(b * SEQ + c * CH, CH)], pa[:, 0, :], pa[:, 1, 0:4])
            pe.wait_ge(ln.out_ready, START + PRE)
            with pe.Fori(0, DEPTH) as layer:
                pe.wait_ge(aw, START + AW * layer + AW)
                pe.wait_ge(xa_done, START + FL * layer)

                def step(q, n, late, iq, i, li):
                    def project(k, banks, at):
                        src = xaf[:, bass.ds(col(at), BLK)]
                        for p in range(PAIRS):
                            ins = nc.tensor.matmul(pa[:, banks + p // 4, (p % 4) * BLK:(p % 4 + 1) * BLK], wqk[:, k, p * P:(p + 1) * P],
                                                   src, start=True, stop=True)
                        ins.then_inc(qk_ps, 1)

                    def values(first_window):
                        for w in range(first_window, first_window + 2):
                            for hp in range(2):
                                ins = nc.tensor.matmul(pw[hp * DH:(hp + 1) * DH, 2 + w % 2, :], hs[:, WIN * w:WIN * w + 2 * WIN], wv[:, hp, :],
                                                       start=True, stop=True, tile_position=(0, hp * DH))
                        ins.then_inc(v_ps, 1)

                    if n is not None:
                        pe.wait_ge(sq_ready, START + 2 * n + 2)
                        pe.wait_ge(rot, START + 4 * n + 2)
                        for s in range(2):
                            for half in range(2):
                                qd = 2 * s + half
                                ins = nc.tensor.matmul(pa[WIN * qd:WIN * qd + WIN, 0, :], head_sum[:, :], sq[:, s, half * 512:(half + 1) * 512],
                                                       start=True, stop=True, tile_position=(0, WIN * qd))
                        ins.then_inc(norm_ps, 1)
                    if late is not None:
                        pe.wait_ge(hs_ready, START + late + 1)
                        pe.wait_ge(xb_done, START + late)
                        values(0)
                    if n is not None:
                        pe.wait_ge(nT_ready, START + n + 1)
                        for k in range(4):
                            ins = nc.tensor.transpose(pa[:, 1, k * P:(k + 1) * P], nT[:, k * P:(k + 1) * P], ident[:, :])
                        ins.then_inc(nT_ps, 1)
                    if late is not None:
                        pe.wait_ge(v_ready, START + 2 * late + 1)
                        values(2)
                    if late is not None:
                        pe.wait_ge(exp_ready, START + late + 1)
                        for p in range(PAIRS):
                            ins = nc.tensor.transpose(pw[:, p // 4, (p % 4) * BLK:(p % 4 + 1) * BLK],
                                                      probs[:, p, :, :].rearrange("t h j -> t (h j)"), ident[:, :])
                            if p % 4 == 3:
                                ins.then_inc(probsT_ps, 1)
                    if late is not None:
                        pe.wait_ge(v_ready, START + 2 * late + 2)
                        for p in range(PAIRS):
                            if p % 4 == 0:
                                pe.wait_ge(probsT_ready, START + 2 * late + p // 4 + 1)
                                own_wait(pe, passed)
                            for w in range(4):
                                for hp in range(2):
                                    part = slice(hp * DH, (hp + 1) * DH)
                                    ins = nc.tensor.matmul(pw[WIN * w:WIN * w + WIN, 2 + hp, p * DH:(p + 1) * DH],
                                                           probsT[part, p, WIN * w:WIN * w + WIN], v[part, w, p * DH:(p + 1) * DH],
                                                           start=True, stop=True, tile_position=(hp * DH, WIN * w))
                        ins.then_inc(pv_ps, 1)
                    if n is not None:
                        pe.wait_ge(rnorm_ready, START + n + 1)
                        for p in range(PAIRS):
                            ins = nc.tensor.matmul(pa[:, 2 + p // 4, (p % 4) * BLK:(p % 4 + 1) * BLK], rk_wide[:, p * P:(p + 1) * P],
                                                   ident[:, :], start=True, stop=True)
                        ins.then_inc(spread_ps, 1)
                    if q is not None:
                        project(0, 0, iq)
                    if late is not None:
                        pe.wait_ge(o_ready, START + 2 * late + 2)
                        for p in range(PAIRS):
                            ins = nc.tensor.transpose(pw[:, 2 + p // 4, (p % 4) * BLK:(p % 4 + 1) * BLK],
                                                      o[:, p, :, :].rearrange("t h e -> t (h e)"), ident[:, :])
                        ins.then_inc(oT_ps, 1)
                    if n is not None:
                        pe.wait_ge(rope_add, START + 2 * n + 1)
                        pe.wait_ge(kr_ready, START + n + 1)
                        for hp in range(2):
                            nc.tensor.matmul(pw[:, hp, :], ident16[:, :], bcast_mid(mask[:, :, :].rearrange("p c j -> p (c j)")
                                             [:, bass.ds((i % BPS) * 2 * WIN, 2 * WIN)], PAIRS), start=True, stop=False, skip_group_check=True)
                        for w in range(4):
                            for p in range(PAIRS):
                                for hp in range(2):
                                    part = slice(hp * DH, (hp + 1) * DH)
                                    ins = nc.tensor.matmul(pw[WIN * w:WIN * w + WIN, hp, p * 2 * WIN:(p + 1) * 2 * WIN],
                                                           qr[part, p, WIN * w:WIN * w + WIN], kr[part, p, WIN * w:WIN * w + 2 * WIN],
                                                           start=False, stop=True, skip_group_check=True, tile_position=(hp * DH, WIN * w))
                        ins.then_inc(sim_ps, 1)
                    if q is not None:
                        project(1, 2, iq)
                    if late is not None:
                        pe.wait_ge(oT_ready, START + late + 1)
                        for p in range(PAIRS):
                            ins = nc.tensor.matmul(pw[:, 2, 0:BLK], wo[:, p, :], oT[:, p, :], start=p == 0, stop=p == PAIRS - 1)
                        ins.then_inc(wo_ps, 1)

                pipelined(pe, layer, step)
                pe.wait_ge(xb_done, START + BL * layer + BL)
                pe.wait_ge(fw, START + FW * layer + FW)
                own_wait(pe, passed)

                def step(n, late, i, li):
                    def hidden(j):
                        if late is not None:
                            if j >= 2:
                                pe.wait_ge(hidden_ready, START + NFB * late + j - 1)
                            nc.tensor.matmul(pa[0:FB[j], 2 + j % 2, :], w1[:, j * P:j * P + FB[j]], h[:, :], start=True, stop=True)
                            nc.tensor.matmul(pw[0:FB[j], j % 2, :], w1[:, INNER + j * P:INNER + j * P + FB[j]], h[:, :],
                                             start=True, stop=True).then_inc(ff_ps, 1)

                    def output(j):
                        if late is not None:
                            pe.wait_ge(hidden_ready, START + NFB * late + j + 1)
                            ins = nc.tensor.matmul(pw[:, 2, :], w2[0:FB[j], j, :], act_out[0:FB[j], j, :], start=j == 0, stop=j == NFB - 1)
                            if j == NFB - 1:
                                ins.then_inc(y_ps, 1)

                    if n is not None:
                        ln.tensor_mean(pe, PRE + n, xbf[:, bass.ds(chunk_col(i), CH)], pa[:, 0, :])
                    if late is not None:
                        pe.wait_ge(ln.out_ready, START + PRE + late + 1)
                    hidden(0)
                    hidden(1)
                    if n is not None:
                        ln.tensor_var(pe, PRE + n, pa[:, 1, 0:4])
                    output(0)
                    hidden(2)
                    if n is not None:
                        ln.tensor_spread(pe, PRE + n, pa[:, 0, :])
                    output(1)
                    output(2)

                chunks(pe, layer, step)
                pe.wait_ge(xa_done, START + FL * layer + FL)

        @block.scalar
        def _(act):
            with act.Fori(0, BATCH) as b:
                act.wait_ge(mods_ready, START + b + 1)
                for c in range(2):
                    n = b * 2 + c
                    ln.scalar_squares(act, n)
                    at = b * SROW + c * CH
                    ln.scalar_out(act, n, [(slice(0, DH), xaf[0:DH, bass.ds(at, CH)]), (slice(DH, P), xaf[DH:P, bass.ds(at + 1, CH)])], mods[:, 0:1])
            with act.Fori(0, DEPTH) as layer:
                def step(q, n, late, iq, i, li):
                    def square(s, block):
                        if block is not None:
                            act.wait_ge(qk_ps, START + 2 * block + s + 1)
                            nc.scalar.activation(sq[:, s, :], pa[:, 2 * s:2 * s + 2, :].rearrange("p a t -> p (a t)"), ACT.Square).then_inc(sq_ready, 1)

                    def exponentials(hp, pairs):
                        if late is not None:
                            if pairs[0] == 0:
                                act.wait_ge(ebias_ready, START + 2 * late + hp + 1)
                            for p in pairs:
                                k = PAIRS * hp + p
                                ins = nc.scalar.activation(probs[:, p, hp, :], pw[:, hp, p * 2 * WIN:(p + 1) * 2 * WIN], ACT.Exp, bias=ebias[:, k:k + 1],
                                                           scale=rnorm[:, 2 * p + hp:2 * p + hp + 1], accum_out=total[:, k:k + 1])
                            if hp == 1 and pairs[-1] == PAIRS - 1:
                                ins.then_inc(exp_ready, 1)

                    def values_out(k):
                        if late is not None:
                            act.wait_ge(v_ps, START + 2 * late + k + 1)
                            nc.scalar.activation(v[:, 2 * k:2 * k + 2, :], pw[:, 2:4, :], ACT.Copy).then_inc(v_ready, 1)

                    def norms_out():
                        if n is not None:
                            act.wait_ge(norm_ps, START + n + 1)
                            nc.scalar.activation(nT[:, :], pa[:, 0, :], ACT.Copy).then_inc(nT_ready, 1)

                    exponentials(0, range(0, 4))
                    square(1, n)
                    exponentials(0, range(4, 8))
                    exponentials(1, range(0, 1))
                    norms_out()
                    exponentials(1, range(1, 3))
                    values_out(0)
                    exponentials(1, range(3, 8))
                    values_out(1)
                    if late is not None:
                        for k in range(2):
                            act.wait_ge(probsT_ps, START + 2 * late + k + 1)
                            nc.scalar.activation(probsT[:, 4 * k:4 * k + 4, :].rearrange("p g t -> p (g t)"), pw[:, k, :], ACT.Copy)\
                                .then_inc(probsT_ready, 1)
                    square(0, q)
                    if late is not None:
                        act.wait_ge(oT_ps, START + late + 1)
                        nc.scalar.activation(oT[:, :, :].rearrange("p g t -> p (g t)"), pw[:, 2:4, :].rearrange("p a t -> p (a t)"), ACT.Copy)\
                            .then_inc(oT_ready, 1)

                pipelined(act, layer, step)
                act.wait_ge(fw, START + FW * layer + FW)

                def step(n, late, i, li):
                    if late is not None:
                        for j in range(NFB):
                            act.wait_ge(ff_ps, START + NFB * late + j + 1)
                            if j >= 2:
                                act.wait_ge(hidden_ready, START + NFB * late + j - 1)
                            nc.scalar.activation(gelu[0:FB[j], j % 2, :], pw[0:FB[j], j % 2, :], ACT.Gelu,
                                                 bias=fpar[0:FB[j], 3 + NFB + j:4 + NFB + j]).then_inc(gelu_ready, 1)
                    if n is not None:
                        ln.scalar_out(act, PRE + n, [(slice(0, P), h[:, :])], fpar[:, 1:2])

                chunks(act, layer, step)

        @block.vector
        def _(dve):
            dve.wait_ge(consts, START + 48)
            nc.vector.tensor_copy(mask[:, :, :].rearrange("p c j -> p (c j)"), mask32).then_inc(mask_ready, 1)
            nc.vector.tensor_copy(ident16[:, :], ident[:, :]).then_inc(mask_ready, 1)
            dve.wait_ge(mask_ready, START + 2)
            link = Links(dve, flinks)
            with dve.Fori(0, BATCH) as b:
                link.start(b)
                dve.wait_ge(ln.normed_ready, START + 2 * b)
                dve.wait_ge(ln.out_ready, START + 2 * b)
                for k in range(3):
                    ins = nc.vector.tensor_copy(mods[:, k:k + 1], const["mod"][:, bass.ds(b + (3 + k) * BATCH, 1)])
                link(ins)
                dve.sem_inc(mods_ready, 1)
                for c in range(2):
                    ln.vector(dve, b * 2 + c, x[:, bass.ds(b * SEQ + c * CH, CH)], pa[:, 0, :], pa[:, 1, 0:4], mods[:, 1:2])
            dve.wait_ge(ln.out_ready, START + PRE)
            with dve.Fori(0, DEPTH) as layer:
                dve.wait_ge(consts, START + 48)
                dve.wait_ge(aw, START + AW * layer + AW)
                for k in range(4):
                    ins = nc.vector.tensor_scalar(tab[:, k, :], base_tab[:, k, :], scales[:, k // 2:k // 2 + 1], None, ALU.mult)
                ins.then_inc(tabs_ready, 1)
                dve.wait_ge(tabs_ready, START + layer + 1)
                link, late_link = Links(dve, links), Links(dve, late_links)

                def step(q, n, late, iq, i, li):
                    if n is not None:
                        link.start(EARLY_LINKS * n)
                    if late is not None:
                        late_link.start(LATE_LINKS * late)

                    def table(k, at_block):
                        return bcast_mid(tab[:, k, bass.ds((at_block % BPS) * BLK, BLK)], PAIRS)

                    flat = lambda ap: ap.rearrange("p (g t) -> p g t", g=PAIRS)
                    projected = lambda s: flat(pa[:, 2 * s:2 * s + 2, :].rearrange("p a t -> p (a t)"))

                    def rotate_cos(s, block, at_block):
                        dve.wait_ge(sq_ready, START + 2 * block + s + 1)
                        nc.vector.tensor_tensor(flat(m[:, 2 * s, :]), projected(s), table(2 * s, at_block), ALU.mult).then_inc(rot, 1)

                    def rotate_sin(s, at_block, quadrants):
                        for a in quadrants:
                            at, to = (slice(HALF * k, HALF * k + HALF) for k in (a, a ^ 1))
                            ins = nc.vector.tensor_tensor(flat(m[to, 2 * s + 1, :]), projected(s)[at], table(2 * s + 1, at_block)[at], ALU.mult)
                        if a == 3:
                            ins.then_inc(rot, 1)

                    if n is not None:
                        rotate_cos(1, n, i)
                        rotate_sin(1, i, (0, 1, 2, 3))
                    if late is not None:
                        dve.wait_ge(exp_ready, START + late + 1)
                        late_link(nc.vector.reciprocal(recip[:, :], total[:, :]))
                    if n is not None:
                        dve.wait_ge(nT_ps, START + n + 1)
                        link(nc.vector.tensor_scalar(norm[:, :].rearrange("t (a k x) -> t k a x", a=4, k=4),
                                                     pa[:, 1, :].rearrange("t (k a y) -> t k a y", k=4, a=4)[:, :, :, 0:2], 1e-24, None, ALU.max))
                        newton_rsqrt(nc, link, rnorm[:, :], norm[:, :], ntmp[:, :])
                        nc.vector.tensor_copy(rk_wide[:, :].rearrange("p (a f) -> p a f", f=DH), bcast_last(rnorm[:, HEADS:], DH))\
                            .then_inc(rnorm_ready, 1)
                    if late is not None:
                        dve.wait_ge(pv_ps, START + late + 1)
                        for hp in range(2):
                            nc.vector.tensor_tensor(o[:, :, hp, :], pw[:, 2 + hp, :].rearrange("t (g e) -> t g e", g=PAIRS),
                                                    bcast_last(recip[:, PAIRS * hp:PAIRS * hp + PAIRS], DH), ALU.mult).then_inc(o_ready, 1)
                        assert late_link.n == LATE_LINKS
                    if n is not None:
                        dve.wait_ge(ktail, START + n)
                        dve.wait_ge(rope_add, START + 2 * n + 2)
                        dve.wait_ge(spread_ps, START + n + 1)
                        nc.vector.tensor_tensor(kr[:, :, WIN:WIN + BLK], ks[:, :, :],
                                                pa[:, 2:4, :].rearrange("p a t -> p (a t)").rearrange("p (g t) -> p g t", g=PAIRS), ALU.mult).then_inc(kr_ready, 1)
                    if q is not None:
                        rotate_cos(0, q, iq)
                        rotate_sin(0, iq, (0, 1))
                    if n is not None:
                        dve.wait_ge(sim_ps, START + n + 1)
                        for hp in range(2):
                            k = slice(PAIRS * hp, PAIRS * hp + PAIRS)
                            link(nc.vector.tensor_reduce(mx[:, k], pw[:, hp, :].rearrange("p (g j) -> p g j", g=PAIRS), AX.X, ALU.max))
                            nc.vector.scalar_tensor_tensor(ebias[:, k], mx[:, k], -1.0, rnorm[:, 0:HEADS].rearrange("p (g x) -> p x g", x=2)[:, hp, :],
                                                           ALU.mult, ALU.mult).then_inc(ebias_ready, 1)
                        assert link.n == EARLY_LINKS
                    if q is not None:
                        rotate_sin(0, iq, (2, 3))
                    if late is not None:
                        dve.wait_ge(wo_ps, START + late + 1)
                        c = col(li)
                        nc.vector.tensor_tensor(xbf[0:DH, bass.ds(c, BLK)], pw[0:DH, 2, 0:BLK], xaf[0:DH, bass.ds(c, BLK)], ALU.add)
                        nc.vector.tensor_tensor(xbf[DH:P, bass.ds(c + 1, BLK)], pw[DH:P, 2, 0:BLK], xaf[DH:P, bass.ds(c + 1, BLK)], ALU.add)\
                            .then_inc(xb_done, 1)

                pipelined(dve, layer, step)
                dve.wait_ge(xb_done, START + BL * layer + BL)
                dve.wait_ge(fw, START + FW * layer + FW)
                own_wait(dve, passed)

                def step(n, late, i, li):
                    def hidden(j):
                        if late is not None:
                            dve.wait_ge(gelu_ready, START + NFB * late + j + 1)
                            nc.vector.scalar_tensor_tensor(act_out[0:FB[j], j, :], pa[0:FB[j], 2 + j % 2, :], fpar[0:FB[j], 3 + j:4 + j],
                                                           gelu[0:FB[j], j % 2, :], ALU.add, ALU.mult).then_inc(hidden_ready, 1)

                    if n is not None:
                        ln.vector_centre(dve, PRE + n, xbf[:, bass.ds(chunk_col(i), CH)], pa[:, 0, :])
                    hidden(0)
                    if n is not None:
                        ln.vector_rstd(dve, PRE + n, pa[:, 1, 0:4])
                    hidden(1)
                    hidden(2)
                    if n is not None:
                        ln.vector_normed(dve, PRE + n, pa[:, 0, :], fpar[:, 0:1])
                    if late is not None:
                        dve.wait_ge(y_ps, START + late + 1)
                        for part, c in ((slice(0, DH), chunk_col(li)), (slice(DH, P), chunk_col(li) + 1)):
                            ins = nc.vector.scalar_tensor_tensor(xaf[part, bass.ds(c, CH)], pw[part, 2, :], fpar[part, 2:3],
                                                                 xbf[part, bass.ds(c, CH)], ALU.add, ALU.add)
                        ins.then_inc(xa_done, 1)

                chunks(dve, layer, step)
            dve.wait_ge(xa_done, START + FL * DEPTH)
            for b in range(BATCH):
                at = (3 + 2) * BATCH + b
                for lo, hi, shift in ((0, DH, 0), (DH, P, 1)):
                    nc.vector.scalar_tensor_tensor(x[lo:hi, b * SEQ:(b + 1) * SEQ], xa[lo:hi, b, shift:shift + SEQ], const["mod"][lo:hi, at:at + 1],
                                                   x[lo:hi, b * SEQ:(b + 1) * SEQ], ALU.mult, ALU.add)


def rwkv(nc, const, t):
    ctx = ExitStack()
    with ctx:
        sb = lambda s, sh, dt=F32: ctx.enter_context(nc.sbuf_tensor("wkv_" + s, sh, dt))
        sems, sem = semaphores(nc, ctx, "wkv_")
        ln = LayerNorm(nc, ctx, "wkv_ln", const, sem)
        x = const["x"]
        w = sb("w", [P, 4, P])
        decay = sb("decay", [P, 2])
        wdec = sb("wdec", [P, 1])
        ew = sb("ew", [P, 1])
        mods, gate = sb("mods", [P, 2]), sb("gate", [P, 1])
        h, k, v, sr = sb("h", [P, SEQ]), sb("k", [P, SEQ]), sb("v", [P, SEQ]), sb("sr", [P, SEQ])
        pp, aa, bb = sb("pp", [P, SEQ + 1]), sb("aa", [P, SEQ + 1]), sb("bb", [P, SEQ + 1])
        e1, e2, f1, f2, pm = (sb(n, [P, SEQ]) for n in ("e1", "e2", "f1", "f2", "pm"))
        e2v, num, den, f2v = (sb(n, [P, SEQ]) for n in ("e2v", "num", "den", "f2v"))
        ps = [ctx.enter_context(nc.psum_tensor(f"wkv_ps{i}", [P, 2 * CH], F32)) for i in range(3)]
        ps_ln = ctx.enter_context(nc.psum_tensor("wkv_ps_ln", [P, CH], F32))
        ps_small = ctx.enter_context(nc.psum_tensor("wkv_ps_small", [P, CH], F32))
        loaded, w_ready, mods_ready, init = sem("loaded"), sem("w_ready"), sem("mods_ready"), sem("init")
        proj_ps, proj_ready, arg_ready, exp_ready = sem("proj_ps"), sem("proj_ready"), sem("arg_ready"), sem("exp_ready")
        den_part, y_ready, out_ps, x_done, links, ln_links = sem("den_part"), sem("y_ready"), sem("out_ps"), sem("x_done"), sem("links"), sem("mod_links")
        block = ctx.enter_context(nc.Block())
        VL = 11

        def sequences(eng, step):
            step(0, None)
            with eng.Fori(1, BATCH) as b:
                step(b, b - 1)
            step(None, BATCH - 1)

        @block.sync
        def _(sp):
            for s in sems:
                sp.sem_inc(s, START)
            sp.dma_start(w[:, :, :], t["wkv_w"]).then_inc(loaded, 16)
            sp.dma_start(decay[:, :], t["wkv_decay"]).then_inc(loaded, 16)
            sp.wait_ge(loaded, START + 32)

        @block.tensor
        def _(pe):
            pe.wait_ge(loaded, START + 32)

            def step(n, late):
                if late is not None:
                    pe.wait_ge(ln.out_ready, START + 2 * late + 2)
                    pe.wait_ge(x_done, START + late)
                    for i in (2, 1, 0):
                        for c in range(2):
                            ins = nc.tensor.matmul(ps[i][:, c * CH:(c + 1) * CH], w[:, i, :], h[:, c * CH:(c + 1) * CH], start=True, stop=True)
                        ins.then_inc(proj_ps, 1)
                if n is not None:
                    for c in range(2):
                        ln.tensor(pe, n * 2 + c, x[:, bass.ds(n * SEQ + c * CH, CH)], ps_ln[:, :], ps_small[:, 0:4])
                if late is not None:
                    pe.wait_ge(y_ready, START + late + 1)
                    for c in range(2):
                        ins = nc.tensor.matmul(ps[0][:, c * CH:(c + 1) * CH], w[:, 3, :], num[:, c * CH:(c + 1) * CH], start=True, stop=True)
                    ins.then_inc(out_ps, 1)

            sequences(pe, step)

        @block.gpsimd
        def _(pool):
            nc.gpsimd.memset(pp[:, 0:1], -1e38)
            nc.gpsimd.memset(aa[:, 0:1], 0.0)
            nc.gpsimd.memset(bb[:, 0:1], 0.0).then_inc(init, 1)
            with pool.Fori(0, BATCH) as b:
                pool.wait_ge(proj_ready, START + 3 * b + 2)
                pool.wait_ge(exp_ready, START + 4 * b + 2)
                nc.gpsimd.tensor_tensor(e2v[:, :], e2[:, :], v[:, :], ALU.mult).then_inc(den_part, 1)
                pool.wait_ge(exp_ready, START + 4 * b + 4)
                nc.gpsimd.tensor_tensor(f2v[:, :], f2[:, :], v[:, :], ALU.mult).then_inc(den_part, 1)

        @block.scalar
        def _(act):
            act.wait_ge(loaded, START + 32)
            nc.scalar.activation(ew[:, :], decay[:, 0:1], ACT.Exp).then_inc(w_ready, 1)

            def step(n, late):
                if late is not None:
                    act.wait_ge(proj_ps, START + 3 * late + 1)
                    nc.scalar.activation(k[:, :], ps[2][:, :], ACT.Copy).then_inc(proj_ready, 1)
                    act.wait_ge(proj_ps, START + 3 * late + 2)
                    nc.scalar.activation(v[:, :], ps[1][:, :], ACT.Copy).then_inc(proj_ready, 1)
                    act.wait_ge(proj_ps, START + 3 * late + 3)
                    nc.scalar.activation(sr[:, :], ps[0][:, :], ACT.Tanh, scale=0.5).then_inc(proj_ready, 1)
                    for i, buf in enumerate((e1, e2, f1, f2)):
                        act.wait_ge(arg_ready, START + 4 * late + i + 1)
                        nc.scalar.activation(buf[:, :], buf[:, :], ACT.Exp).then_inc(exp_ready, 1)
                if n is not None:
                    act.wait_ge(mods_ready, START + n + 1)
                    for c in range(2):
                        ln.scalar_squares(act, n * 2 + c)
                        ln.scalar_out(act, n * 2 + c, [(slice(0, P), h[:, c * CH:(c + 1) * CH])], mods[:, 0:1])

            sequences(act, step)

        @block.vector
        def _(dve):
            link = Links(dve, links)
            dve.wait_ge(w_ready, START + 1)
            link(nc.vector.tensor_scalar(wdec[:, :], ew[:, :], -1.0, None, ALU.mult))
            dve.wait_ge(init, START + 1)
            ln_link = Links(dve, ln_links)

            def step(n, late):
                if late is not None:
                    link.start(1 + late * VL)
                    dve.wait_ge(x_done, START + late)
                    link(nc.vector.tensor_scalar(gate[:, :], const["mod"][:, bass.ds(late + 8 * BATCH, 1)], 0.5, None, ALU.mult))
                    dve.wait_ge(proj_ready, START + 3 * late + 1)
                    first, now, prev = decay[:, 1:2], slice(1, SEQ + 1), slice(0, SEQ)
                    link(nc.vector.tensor_tensor_scan(pp[:, now], wdec[:, 0:1].broadcast_to([P, SEQ]), k[:, :], -1e38, ALU.add, ALU.max))
                    nc.vector.scalar_tensor_tensor(e1[:, :], pp[:, prev], wdec[:, :], pp[:, now], ALU.add, ALU.subtract).then_inc(arg_ready, 1)
                    nc.vector.tensor_tensor(e2[:, :], k[:, :], pp[:, now], ALU.subtract).then_inc(arg_ready, 1)
                    link(nc.vector.scalar_tensor_tensor(pm[:, :], k[:, :], first, pp[:, prev], ALU.add, ALU.max))
                    nc.vector.tensor_tensor(f1[:, :], pp[:, prev], pm[:, :], ALU.subtract).then_inc(arg_ready, 1)
                    nc.vector.scalar_tensor_tensor(f2[:, :], k[:, :], first, pm[:, :], ALU.add, ALU.subtract).then_inc(arg_ready, 1)
                if n is not None:
                    ln_link.start(n)
                    dve.wait_ge(ln.out_ready, START + 2 * n)
                    for i in range(2):
                        ins = nc.vector.tensor_copy(mods[:, i:i + 1], const["mod"][:, bass.ds(n + (6 + i) * BATCH, 1)])
                    ln_link(ins)
                    dve.sem_inc(mods_ready, 1)
                    for c in range(2):
                        ln.vector(dve, n * 2 + c, x[:, bass.ds(n * SEQ + c * CH, CH)], ps_ln[:, :], ps_small[:, 0:4], mods[:, 1:2])
                if late is not None:
                    dve.wait_ge(exp_ready, START + 4 * late + 2)
                    link(nc.vector.tensor_tensor_scan(bb[:, now], e1[:, :], e2[:, :], 0.0, ALU.mult, ALU.add))
                    dve.wait_ge(den_part, START + 2 * late + 1)
                    link(nc.vector.tensor_tensor_scan(aa[:, now], e1[:, :], e2v[:, :], 0.0, ALU.mult, ALU.add))
                    dve.wait_ge(exp_ready, START + 4 * late + 4)
                    link(nc.vector.tensor_tensor(den[:, :], f1[:, :], bb[:, prev], ALU.mult))
                    link(nc.vector.tensor_tensor(den[:, :], den[:, :], f2[:, :], ALU.add))
                    link(nc.vector.reciprocal(den[:, :], den[:, :]))
                    link(nc.vector.tensor_tensor(num[:, :], f1[:, :], aa[:, prev], ALU.mult))
                    dve.wait_ge(den_part, START + 2 * late + 2)
                    link(nc.vector.tensor_tensor(num[:, :], num[:, :], f2v[:, :], ALU.add))
                    link(nc.vector.tensor_tensor(num[:, :], num[:, :], den[:, :], ALU.mult))
                    dve.wait_ge(proj_ready, START + 3 * late + 3)
                    nc.vector.scalar_tensor_tensor(num[:, :], sr[:, :], 1.0, num[:, :], ALU.add, ALU.mult).then_inc(y_ready, 1)
                    dve.wait_ge(out_ps, START + late + 1)
                    cols = bass.ds(late * SEQ, SEQ)
                    nc.vector.scalar_tensor_tensor(x[:, cols], ps[0][:, :], gate[:, :], x[:, cols], ALU.mult, ALU.add).then_inc(x_done, 1)
                    assert link.n == VL, link.n

            sequences(dve, step)


def mixture(nc, const, t, out):
    ctx = ExitStack()
    with ctx:
        sb = lambda s, sh, dt=F32: ctx.enter_context(nc.sbuf_tensor("moe_" + s, sh, dt))
        sems, sem = semaphores(nc, ctx, "moe_")
        ln = LayerNorm(nc, ctx, "moe_ln", const, sem)
        x, ident = const["x"], const["ident"]
        gate_w, ew, eb, cw = sb("gate_w", [P, EXPERTS]), sb("expert_w", [P, EXPERTS, P]), sb("expert_b", [P, EXPERTS]), sb("combine_w", [P, P])
        mods = sb("mods", [P, 2, 3])
        h = sb("h", [P, 2, CH])
        logits = sb("logits", [P, 4, EXPERTS])
        one = sb("one", [P, 4])
        probs, top, gates = sb("probs", [P, 4, EXPERTS]), sb("top", [P, 4, 8]), sb("gates", [P, 2, 4, EXPERTS])
        idx, idxf, iota = sb("idx", [P, 4, 8], U32), sb("idxf", [P, 4, 8]), sb("iota", [P, 4, EXPERTS])
        wide = sb("wide", [P, 2, 4, P])
        y, yg = sb("y", [P, 2, CH]), sb("yg", [P, 2, CH])
        pb = lambda n: ctx.enter_context(nc.psum_tensor("moe_ps_" + n, [P, CH], F32))
        ps_ln, ps_small, ps_c = pb("ln"), pb("small"), pb("c")
        ps_e, ps_g = [pb(f"e{i}") for i in range(2)], [pb(f"g{i}") for i in range(2)]
        loaded, mods_ready, logits_ps, centred, exp_ready, gates_ready = (sem(n) for n in ("loaded", "mods_ready", "logits_ps", "centred", "exp_ready", "gates_ready"))
        wide_ready, expert_ps, spread_ps, y_ready, yg_ready, c_ps, x_done, stored, links = (
            sem(n) for n in ("wide_ready", "expert_ps", "spread_ps", "y_ready", "yg_ready", "c_ps", "x_done", "stored", "links"))
        passed = sem("passed")
        block = ctx.enter_context(nc.Block())
        VL = 15

        def chunks(eng, step):
            step(0, None, 0, None)
            with eng.Fori(0, NCH // 2 - 1) as i:
                step(2 * i + 1, 2 * i, 1, 0)
                step(2 * i + 2, 2 * i + 1, 0, 1)
            step(NCH - 1, NCH - 2, 1, 0)
            step(None, NCH - 1, None, 1)

        @block.sync
        def _(sp):
            for s in sems:
                sp.sem_inc(s, START)
            for name, dst in (("gate_w", gate_w), ("expert_w", ew), ("expert_b", eb), ("combine_w", cw), ("iota", iota)):
                sp.dma_start(dst[:], t[name]).then_inc(loaded, 16)
            sp.wait_ge(loaded, START + 80)
            with sp.Fori(0, NCH) as n:
                sp.wait_ge(x_done, START + n + 1)
                sp.dma_start(out[:, bass.ds(n * CH, CH)], x[:, bass.ds(n * CH, CH)]).then_inc(stored, 16)
            sp.wait_ge(stored, START + 16 * NCH)

        @block.tensor
        def _(pe):
            pe.wait_ge(loaded, START + 80)

            def step(n, late, buf, late_buf):
                if n is not None:
                    ln.tensor_mean(pe, n, x[:, bass.ds(n * CH, CH)], ps_ln[:, :])
                for e in range(EXPERTS + 1):
                    if late is not None and e < EXPERTS:
                        if e >= 2:
                            pe.wait_ge(yg_ready, START + EXPERTS * late + e - 1)
                        nc.tensor.matmul(ps_e[e % 2][:, :], ew[:, e, :], h[:, late_buf, :], start=True, stop=True).then_inc(expert_ps, 1)
                        pe.wait_ge(wide_ready, START + EXPERTS * late + e + 1)
                        for c in range(4):
                            ins = nc.tensor.matmul(ps_g[e % 2][:, c * P:(c + 1) * P], wide[:, e % 2, c, :], ident[:, :], start=True, stop=True)
                        ins.then_inc(spread_ps, 1)
                    if late is not None and e > 0:
                        pe.wait_ge(yg_ready, START + EXPERTS * late + e)
                        ins = nc.tensor.matmul(ps_c[:, :], cw[:, :], yg[:, (e - 1) % 2, :], start=e == 1, stop=e == EXPERTS)
                        if e == EXPERTS:
                            ins.then_inc(c_ps, 1)
                    if n is not None and e == 0:
                        ln.tensor_var(pe, n, ps_small[:, 0:4])
                    if n is not None and e == 1:
                        ln.tensor_spread(pe, n, ps_ln[:, :])
                    if n is not None and e == 2:
                        pe.wait_ge(ln.out_ready, START + n + 1)
                        for c in range(4):
                            ins = nc.tensor.matmul(ps_small[:, 64 + c * EXPERTS:64 + (c + 1) * EXPERTS], h[:, buf, c * P:(c + 1) * P], gate_w[:, :],
                                                   start=True, stop=True)
                        ins.then_inc(logits_ps, 1)

            chunks(pe, step)

        @block.gpsimd
        def _(pool):
            def step(n, late, buf, late_buf):
                if late is None:
                    return
                pool.wait_ge(gates_ready, START + late + 1)
                for e in range(EXPERTS):
                    pool.wait_ge(spread_ps, START + EXPERTS * late + max(e - 1, 0))
                    own_wait(pool, passed)
                    nc.gpsimd.tensor_copy(wide[:, e % 2, :, :], bcast_last(gates[:, late_buf, :, e], P)).then_inc(wide_ready, 1)

            chunks(pool, step)

        @block.scalar
        def _(act):
            act.wait_ge(loaded, START + 80)

            def step(n, late, buf, late_buf):
                for e in range(EXPERTS):
                    if late is not None:
                        act.wait_ge(expert_ps, START + EXPERTS * late + e + 1)
                        if e >= 2:
                            act.wait_ge(yg_ready, START + EXPERTS * late + e - 1)
                        nc.scalar.activation(y[:, e % 2, :], ps_e[e % 2][:, :], ACT.Silu, bias=eb[:, e:e + 1]).then_inc(y_ready, 1)
                    if n is not None and e == 1:
                        act.wait_ge(mods_ready, START + n + 1)
                        ln.scalar_out(act, n, [(slice(0, P), h[:, buf, :])], mods[:, buf, 0:1])
                    if n is not None and e == 3:
                        act.wait_ge(centred, START + n + 1)
                        nc.scalar.activation(probs[:, :, :], logits[:, :, :], ACT.Exp).then_inc(exp_ready, 1)

            chunks(act, step)

        @block.vector
        def _(dve):
            dve.wait_ge(loaded, START + 80)
            link = Links(dve, links)

            def step(n, late, buf, late_buf):
                def gated(e):
                    if late is not None:
                        dve.wait_ge(y_ready, START + EXPERTS * late + e + 1)
                        dve.wait_ge(spread_ps, START + EXPERTS * late + e + 1)
                        nc.vector.tensor_tensor(yg[:, e % 2, :], y[:, e % 2, :], ps_g[e % 2][:, :], ALU.mult).then_inc(yg_ready, 1)

                if n is not None:
                    link.start(n * VL)
                    if late is not None:
                        dve.wait_ge(x_done, START + late)
                    for i in range(3):
                        ins = nc.vector.tensor_copy(mods[:, buf, i:i + 1], const["mod"][:, bass.ds(n // 2 + (9 + i) * BATCH, 1)])
                    link(ins)
                    dve.sem_inc(mods_ready, 1)
                    ln.vector_centre(dve, n, x[:, bass.ds(n * CH, CH)], ps_ln[:, :])
                    ln.vector_squares(dve, n)
                gated(0)
                if n is not None:
                    ln.vector_rstd(dve, n, ps_small[:, 0:4])
                gated(1)
                if n is not None:
                    ln.vector_normed(dve, n, ps_ln[:, :], mods[:, buf, 1:2])
                gated(2)
                if n is not None:
                    dve.wait_ge(logits_ps, START + n + 1)
                    raw = ps_small[:, 64:64 + 4 * EXPERTS].rearrange("p (c e) -> p c e", c=4)
                    link(nc.vector.tensor_reduce(one[:, :], raw, AX.X, ALU.max))
                    nc.vector.tensor_tensor(logits[:, :, :], raw, bcast_last(one[:, :], EXPERTS), ALU.subtract).then_inc(centred, 1)
                gated(3)
                gated(4)
                if n is not None:
                    dve.wait_ge(exp_ready, START + n + 1)
                    link(nc.vector.tensor_reduce(one[:, :], probs[:, :, :], AX.X, ALU.add))
                    link(nc.vector.reciprocal(one[:, :], one[:, :]))
                    link(nc.vector.tensor_tensor(probs[:, :, :], probs[:, :, :], bcast_last(one[:, :], EXPERTS), ALU.mult))
                    own_wait(dve, passed)
                    for c in range(4):
                        link(nc.vector.max(top[:, c, :], probs[:, c, :]))
                        own_wait(dve, passed)
                gated(5)
                if n is not None:
                    for c in range(4):
                        ins = nc.vector.max_index(idx[:, c, :], top[:, c, :], probs[:, c, :])
                    link(ins)
                    link(nc.vector.tensor_copy(idxf[:, :, :], idx[:, :, :]))
                    g = gates[:, buf, :, :]
                    link(nc.vector.tensor_tensor(g, iota[:, :, :], idxf[:, :, 0:1].broadcast_to([P, 4, EXPERTS]), ALU.is_equal))
                    link(nc.vector.tensor_tensor(logits[:, :, :], iota[:, :, :], idxf[:, :, 1:2].broadcast_to([P, 4, EXPERTS]), ALU.is_equal))
                    link(nc.vector.tensor_tensor(g, g, logits[:, :, :], ALU.add))
                    link(nc.vector.tensor_tensor(g, g, probs[:, :, :], ALU.mult))
                    dve.sem_inc(gates_ready, 1)
                    assert link.n == VL, link.n
                gated(6)
                gated(7)
                if late is not None:
                    dve.wait_ge(c_ps, START + late + 1)
                    cols = bass.ds(late * CH, CH)
                    nc.vector.scalar_tensor_tensor(x[:, cols], ps_c[:, :], mods[:, late_buf, 2:3], x[:, cols], ALU.mult, ALU.add).then_inc(x_done, 1)

            chunks(dve, step)


def kernel_program(nc, t, out, phases=5):
    ctx = ExitStack()
    with ctx:
        sb = lambda s, sh, dt=F32: ctx.enter_context(nc.sbuf_tensor(s, sh, dt))
        const = {
            "x": sb("x", [P, TOK]), "ident": sb("ident", [P, P]), "mean_w": sb("mean_w", [P, P]),
            "mod": sb("mod", [P, 2 * 6 * BATCH]),
        }
        prepare(nc, const, t)
        if phases >= 1:
            theta_attention(nc, const, t)
        if phases >= 2:
            local_layers(nc, const, t)
        if phases >= 3:
            rwkv(nc, const, t)
        if phases >= 4:
            mixture(nc, const, t, out)
        else:
            store(nc, const, out)


def store(nc, const, out):
    with ExitStack() as ctx:
        sems, sem = semaphores(nc, ctx, "store_")
        stored = sem("stored")
        block = ctx.enter_context(nc.Block())

        @block.sync
        def _(sp):
            for s in sems:
                sp.sem_inc(s, START)
            sp.dma_start(out, const["x"][:, :]).then_inc(stored, 16)
            sp.wait_ge(stored, START + 16)


def rotary_tables():
    half = np.arange(0, DH, 2, dtype=np.float32)
    inv_freq = (1.0 / np.float32(10000.0) ** (half / np.float32(DH))).astype(np.float32)
    pos = np.arange(SEQ, dtype=np.float32)
    freqs = (inv_freq[:, None] * pos[None, :]).astype(np.float32).astype(np.float64)
    base = ((half + np.float32(0.4 * DH)) / np.float32(1.4 * DH)).astype(np.float32).astype(np.float64)
    scale = base[:, None] ** ((pos[None, :] - SEQ // 2) / (WIN // 2)).astype(np.float64)
    tabs = [8 * np.cos(freqs) * scale, 8 * np.sin(freqs) * scale, np.cos(freqs) / scale, np.sin(freqs) / scale]
    both = [np.concatenate([x, -x if k % 2 else x], 0) for k, x in enumerate(tabs)]
    return np.ascontiguousarray(np.stack([np.tile(x, (2, 1)) for x in both], 1).astype(np.float32))


def band_mask():
    m = np.full((4, WIN, BPS, 2, WIN), MASKED, np.float32)
    i, j = np.arange(WIN)[:, None], np.arange(WIN)[None, :]
    m[:, :, :, 0, :] = np.where(j >= i, 0.0, MASKED)[None, :, None, :]
    m[:, :, :, 1, :] = np.where(j <= i, 0.0, MASKED)[None, :, None, :]
    m[0, :, 0, 0, :] = MASKED
    return m.reshape(P, BPS * 2 * WIN)


def lay_out(i):
    a = {k: np.asarray(v) for k, v in i.items()}
    c = np.ascontiguousarray
    o = {}
    o["xT"] = c(a["L0_attn_x"].reshape(TOK, P).T)
    o["cT"] = c(np.stack([a["L0_c"].T, a["L1_c"].T], 1))
    o["wmod"] = c(np.stack([a["L0_wmod"], a["L1_wmod"]], 1))
    o["ident"] = np.eye(P, dtype=np.float32)
    o["att_w"] = c(np.stack([a["L0_attn_" + n].T for n in ("Wq", "Wk", "Wv", "Wo")], 1))
    o["att_b"] = c(np.stack([a["L0_attn_" + n] for n in ("bq", "bk", "bv", "bo")], 1))
    o["wkv_w"] = c(np.stack([a["L1_attn_W_rvk"][k * P:(k + 1) * P].T for k in range(3)] + [a["L1_attn_W_out"].T], 1))
    o["wkv_decay"] = c(np.stack([a["L1_attn_time_decay"], a["L1_attn_time_first"]], 1))
    o["gate_w"], o["combine_w"] = c(a["L1_ffn_gate_w"].T), c(a["L1_ffn_combine_w"].T)
    o["expert_w"], o["expert_b"] = c(a["L1_ffn_expert_w"].transpose(2, 0, 1)), c(a["L1_ffn_expert_b"].T)
    o["iota"] = np.ascontiguousarray(np.broadcast_to(np.arange(EXPERTS, dtype=np.float32), (P, 4, EXPERTS)))
    o["tables"], o["mask"] = rotary_tables(), band_mask()
    o["head_sum"] = np.repeat(np.eye(2, WIN, dtype=np.float32), DH, 0)
    wqkv = a["L0_ffn_Wqkv"]
    pad = lambda w: c(np.concatenate([w, np.zeros_like(w[:1])], 0))
    o["wqk"] = pad(wqkv[:, :, :2 * HEADS * DH].reshape(DEPTH, P, 2, HEADS * DH))
    o["wv"] = pad(wqkv[:, :, 2 * HEADS * DH:].reshape(DEPTH, P, PAIRS, 2, DH).transpose(0, 1, 3, 2, 4).reshape(DEPTH, P, 2, PAIRS * DH))
    o["wo"] = pad(a["L0_ffn_Wo"].reshape(DEPTH, PAIRS, P, P).transpose(0, 2, 1, 3))
    o["scales"] = pad(np.tile(np.stack([a["L0_ffn_q_scale"], a["L0_ffn_k_scale"]], 2), (1, 2, 1)))
    o["w1"] = c(a["L0_ffn_W1"])
    pad_rows = lambda w: np.concatenate([w, np.zeros((DEPTH, NFB * P - INNER) + w.shape[2:], np.float32)], 1)
    o["w2"] = c(pad_rows(a["L0_ffn_W2"]).reshape(DEPTH, NFB, P, P).transpose(0, 2, 1, 3))
    b1 = [pad_rows(a["L0_ffn_b1"][:, k * INNER:(k + 1) * INNER]).reshape(DEPTH, NFB, P).transpose(0, 2, 1) for k in range(2)]
    o["fpar"] = c(np.concatenate([a["L0_ffn_ln_g"][:, :, None], a["L0_ffn_ln_b"][:, :, None], a["L0_ffn_b2"][:, :, None]] + b1, 2))
    return o


def kernel(**inputs):
    import concourse.bacc as _bacc
    from concourse.bass_utils import run_bass_kernel_spmd as _run

    nc = _bacc.Bacc("TRN2", target_bir_lowering=False, num_devices=1)
    arrays, t = {}, {}
    for name, a in lay_out(inputs).items():
        arrays[name + "_dram"] = a
        t[name] = nc.dram_tensor(name + "_dram", a.shape, mybir.dt.from_np(a.dtype), kind="ExternalInput").ap()
    out = nc.dram_tensor("out_dram", (P, TOK), F32, kind="ExternalOutput").ap()
    kernel_program(nc, t, out)
    r = _run(nc, [arrays], core_ids=[0])
    return np.ascontiguousarray(r.results[0]["out_dram"].T.reshape(BATCH, SEQ, P))
```
